# Optimizing a Trainium2 kernel written in Bass

```python
import numpy as np
import jax
import jax.numpy as jnp

def _softmax(x, axis=-1):
    return jax.nn.softmax(x, axis=axis)

def _gelu(x):
    return jax.nn.gelu(x, approximate=True)

def _silu(x):
    return jax.nn.silu(x)

def _sigmoid(x):
    return jax.nn.sigmoid(x)

def _layernorm(x, axis=-1, eps=1e-05):
    m = jnp.mean(x, axis=axis, keepdims=True)
    v = jnp.var(x, axis=axis, keepdims=True)
    return (x - m) / jnp.sqrt(v + eps)

def _scatter_add(tgt, idx, src, axis=0):
    return tgt.at[idx].add(src)

def _segment_sum(src, seg, n):
    return jax.ops.segment_sum(src, seg, n)
kernel_name = 'mk_hybrid_d1_jaxref_r8_341682'

def setup_inputs(seed: int=0):
    np.random.seed(seed)
    _w = jnp.asarray

    def _L0_attn_a_setup():
        import jax, jax.numpy as jnp
        import numpy as np
        D_MODEL = 128
        D_STATE = 128
        D_CONV = 4
        EXPAND = 2
        HEADDIM = 128
        NGROUPS = 1
        CHUNK = 32
        D_INNER = EXPAND * D_MODEL
        NHEADS = D_INNER // HEADDIM
        D_IN_PROJ = 2 * D_INNER + 2 * NGROUPS * D_STATE + NHEADS
        CONV_DIM = D_INNER + 2 * NGROUPS * D_STATE
        DT_MIN, DT_MAX = (0.001, 0.02)
        EPS = 1e-05

        def _segsum(x):
            T = x.shape[-1]
            xc = jnp.cumsum(x, axis=-1)
            s = xc[..., :, None] - xc[..., None, :]
            mask = jnp.tril(jnp.ones((T, T), dtype=bool))
            return jnp.where(mask, s, -jnp.inf)

        def _mamba2_forward(u, W_in, conv_w, conv_b, dt_bias, A_log, D, norm_w, W_out):
            b, l, _ = u.shape
            h, p, n, cs, K = (NHEADS, HEADDIM, D_STATE, CHUNK, D_CONV)
            d_ssm = D_INNER
            zxbcdt = jnp.einsum('bld,ed->ble', u, W_in)
            z = zxbcdt[..., :d_ssm]
            xBC = zxbcdt[..., d_ssm:d_ssm + CONV_DIM]
            dt_raw = zxbcdt[..., d_ssm + CONV_DIM:]
            xp = jnp.pad(xBC, ((0, 0), (K - 1, 0), (0, 0)))
            xc = conv_b
            for k in range(K):
                xc = xc + xp[:, k:k + l, :] * conv_w[:, k]
            xc = jax.nn.silu(xc)
            x = xc[..., :d_ssm].reshape(b, l, h, p)
            Bmat = xc[..., d_ssm:d_ssm + n]
            Cmat = xc[..., d_ssm + n:]
            dt = jax.nn.softplus(dt_raw + dt_bias)
            A = -jnp.exp(A_log)
            dA = dt * A
            nc = l // cs
            xd = (x * dt[..., None]).reshape(b, nc, cs, h, p)
            Bn = Bmat.reshape(b, nc, cs, n)
            Cn = Cmat.reshape(b, nc, cs, n)
            Ac = jnp.moveaxis(dA.reshape(b, nc, cs, h), -1, 1)
            A_cs = jnp.cumsum(Ac, axis=-1)
            L = jnp.exp(_segsum(Ac))
            Y_diag = jnp.einsum('bcln,bcsn,bhcls,bcshp->bclhp', Cn, Bn, L, xd)
            decay_states = jnp.exp(A_cs[..., -1:] - A_cs)
            states = jnp.einsum('bcsn,bhcs,bcshp->bchpn', Bn, decay_states, xd)
            chunk_decay = jnp.exp(A_cs[..., -1])
            states_t = jnp.moveaxis(states, 1, 0)
            decay_t = jnp.moveaxis(chunk_decay, -1, 0)

            def step(carry, inp):
                s, d = inp
                new = carry * d[..., None, None] + s
                return (new, carry)
            _, prev_states = jax.lax.scan(step, jnp.zeros_like(states_t[0]), (states_t, decay_t))
            prev_states = jnp.moveaxis(prev_states, 0, 1)
            state_decay = jnp.exp(A_cs)
            Y_off = jnp.einsum('bcln,bchpn,bhcl->bclhp', Cn, prev_states, state_decay)
            Y = (Y_diag + Y_off).reshape(b, l, h, p) + x * D[None, None, :, None]
            y = Y.reshape(b, l, d_ssm)
            yg = y * jax.nn.silu(z)
            yg = yg * jax.lax.rsqrt(jnp.mean(yg * yg, axis=-1, keepdims=True) + EPS) * norm_w
            return jnp.einsum('bld,od->blo', yg, W_out)
        key = jax.random.key(seed)
        ks = jax.random.split(key, 8)
        u = jax.random.normal(ks[0], (4, 256, D_MODEL), dtype=jnp.float32)
        W_in = jax.random.normal(ks[1], (D_IN_PROJ, D_MODEL), dtype=jnp.float32) * D_MODEL ** (-0.5)
        conv_w = jax.random.normal(ks[2], (CONV_DIM, D_CONV), dtype=jnp.float32) * D_CONV ** (-0.5)
        conv_b = jnp.zeros((CONV_DIM,), dtype=jnp.float32)
        dt = jnp.exp(jax.random.uniform(ks[3], (NHEADS,)) * (np.log(DT_MAX) - np.log(DT_MIN)) + np.log(DT_MIN))
        dt_bias = dt + jnp.log(-jnp.expm1(-dt))
        A_log = jnp.log(jax.random.uniform(ks[4], (NHEADS,), minval=1.0, maxval=16.0))
        D = jnp.ones((NHEADS,), dtype=jnp.float32)
        norm_w = jnp.ones((D_INNER,), dtype=jnp.float32)
        W_out = jax.random.normal(ks[5], (D_MODEL, D_INNER), dtype=jnp.float32) * D_INNER ** (-0.5)
        return {'u': u, 'W_in': W_in, 'conv_w': conv_w, 'conv_b': conv_b, 'dt_bias': dt_bias, 'A_log': A_log, 'D': D, 'norm_w': norm_w, 'W_out': W_out}
    _L0_attn_a_in = _L0_attn_a_setup()

    def _L0_attn_b_setup():
        import jax, jax.numpy as jnp
        import numpy as np
        NUM_HEADS = 16
        D_MODEL = 128
        D_HEAD = D_MODEL // NUM_HEADS
        TOP_K = 64
        key = jax.random.key(seed)
        k0, k1, k2 = jax.random.split(key, 3)
        B, S = (2, 256)
        x = jax.random.normal(k0, (B, S, D_MODEL), dtype=jnp.float32)
        w_qkv_w = jax.random.normal(k1, (3 * D_MODEL, D_MODEL), dtype=jnp.float32) * (1.0 / np.sqrt(D_MODEL))
        w_qkv_b = jnp.zeros((3 * D_MODEL,), dtype=jnp.float32)
        w_out_w = jax.random.normal(k2, (D_MODEL, D_MODEL), dtype=jnp.float32) * (1.0 / np.sqrt(D_MODEL))
        w_out_b = jnp.zeros((D_MODEL,), dtype=jnp.float32)
        return {'x': x, 'w_qkv_w': w_qkv_w, 'w_qkv_b': w_qkv_b, 'w_out_w': w_out_w, 'w_out_b': w_out_b}
    _L0_attn_b_in = _L0_attn_b_setup()

    def _L0_ffn_setup():
        import jax, jax.numpy as jnp
        import numpy as np
        B, T, D = (2, 256, 128)
        E, K, FF = (8, 2, 512)

        def _reference_tuple_inner(x, gate_w, gate_b, w1, b1, w2, b2):
            n_experts = w1.shape[0]
            gate_logits = x @ gate_w + gate_b
            topk_vals, topk_idx = jax.lax.top_k(gate_logits, K)
            topk_w = jax.nn.softmax(topk_vals, axis=-1)
            onehot = jax.nn.one_hot(topk_idx, n_experts, dtype=x.dtype)
            comb = jnp.sum(onehot * topk_w[..., None], axis=2)
            h = jax.nn.gelu(jnp.einsum('btd,edf->ebtf', x, w1) + b1[:, None, None, :], approximate=False)
            y = jnp.einsum('ebtf,efd->ebtd', h, w2) + b2[:, None, None, :]
            output = jnp.einsum('ebtd,bte->btd', y, comb)
            expert_counts = jnp.sum(onehot, axis=(0, 1, 2)).astype(jnp.float32)
            return (output, gate_logits, topk_idx, expert_counts)
        key = jax.random.key(seed)
        ks = jax.random.split(key, 4)
        scale = 0.02
        return {'x': jax.random.normal(ks[0], (B, T, D), jnp.float32), 'gate_w': jax.random.normal(ks[1], (D, E), jnp.float32) * scale, 'gate_b': jnp.zeros((E,), jnp.float32), 'w1': jax.random.normal(ks[2], (E, D, FF), jnp.float32) * scale, 'b1': jnp.zeros((E, FF), jnp.float32), 'w2': jax.random.normal(ks[3], (E, FF, D), jnp.float32) * scale, 'b2': jnp.zeros((E, D), jnp.float32)}
    _L0_ffn_in = _L0_ffn_setup()
    _d = {'L0_attn_a_u': _L0_attn_a_in['u'], 'L0_attn_a_W_in': _L0_attn_a_in['W_in'], 'L0_attn_a_conv_w': _L0_attn_a_in['conv_w'], 'L0_attn_a_conv_b': _L0_attn_a_in['conv_b'], 'L0_attn_a_dt_bias': _L0_attn_a_in['dt_bias'], 'L0_attn_a_A_log': _L0_attn_a_in['A_log'], 'L0_attn_a_D': _L0_attn_a_in['D'], 'L0_attn_a_norm_w': _L0_attn_a_in['norm_w'], 'L0_attn_a_W_out': _L0_attn_a_in['W_out'], 'L0_attn_b_w_qkv_w': _L0_attn_b_in['w_qkv_w'], 'L0_attn_b_w_qkv_b': _L0_attn_b_in['w_qkv_b'], 'L0_attn_b_w_out_w': _L0_attn_b_in['w_out_w'], 'L0_attn_b_w_out_b': _L0_attn_b_in['w_out_b'], 'L0_ffn_gate_w': _L0_ffn_in['gate_w'], 'L0_ffn_gate_b': _L0_ffn_in['gate_b'], 'L0_ffn_w1': _L0_ffn_in['w1'], 'L0_ffn_b1': _L0_ffn_in['b1'], 'L0_ffn_w2': _L0_ffn_in['w2'], 'L0_ffn_b2': _L0_ffn_in['b2']}
    _x0 = _d['L0_attn_a_u']
    _d['L0_attn_a_u'] = jax.random.normal(jax.random.fold_in(jax.random.key(seed), 1), (1, 2048, 128), dtype=_x0.dtype)
    del _x0
    return _d

def reference(L0_attn_a_u, L0_attn_a_W_in, L0_attn_a_conv_w, L0_attn_a_conv_b, L0_attn_a_dt_bias, L0_attn_a_A_log, L0_attn_a_D, L0_attn_a_norm_w, L0_attn_a_W_out, L0_attn_b_w_qkv_w, L0_attn_b_w_qkv_b, L0_attn_b_w_out_w, L0_attn_b_w_out_b, L0_ffn_gate_w, L0_ffn_gate_b, L0_ffn_w1, L0_ffn_b1, L0_ffn_w2, L0_ffn_b2):

    def _L0_attn_a_ref(u, W_in, conv_w, conv_b, dt_bias, A_log, D, norm_w, W_out):
        import jax, jax.numpy as jnp
        import numpy as np
        D_MODEL = 128
        D_STATE = 128
        D_CONV = 4
        EXPAND = 2
        HEADDIM = 128
        NGROUPS = 1
        CHUNK = 32
        D_INNER = EXPAND * D_MODEL
        NHEADS = D_INNER // HEADDIM
        D_IN_PROJ = 2 * D_INNER + 2 * NGROUPS * D_STATE + NHEADS
        CONV_DIM = D_INNER + 2 * NGROUPS * D_STATE
        DT_MIN, DT_MAX = (0.001, 0.02)
        EPS = 1e-05

        def _segsum(x):
            T = x.shape[-1]
            xc = jnp.cumsum(x, axis=-1)
            s = xc[..., :, None] - xc[..., None, :]
            mask = jnp.tril(jnp.ones((T, T), dtype=bool))
            return jnp.where(mask, s, -jnp.inf)

        def _mamba2_forward(u, W_in, conv_w, conv_b, dt_bias, A_log, D, norm_w, W_out):
            b, l, _ = u.shape
            h, p, n, cs, K = (NHEADS, HEADDIM, D_STATE, CHUNK, D_CONV)
            d_ssm = D_INNER
            zxbcdt = jnp.einsum('bld,ed->ble', u, W_in)
            z = zxbcdt[..., :d_ssm]
            xBC = zxbcdt[..., d_ssm:d_ssm + CONV_DIM]
            dt_raw = zxbcdt[..., d_ssm + CONV_DIM:]
            xp = jnp.pad(xBC, ((0, 0), (K - 1, 0), (0, 0)))
            xc = conv_b
            for k in range(K):
                xc = xc + xp[:, k:k + l, :] * conv_w[:, k]
            xc = jax.nn.silu(xc)
            x = xc[..., :d_ssm].reshape(b, l, h, p)
            Bmat = xc[..., d_ssm:d_ssm + n]
            Cmat = xc[..., d_ssm + n:]
            dt = jax.nn.softplus(dt_raw + dt_bias)
            A = -jnp.exp(A_log)
            dA = dt * A
            nc = l // cs
            xd = (x * dt[..., None]).reshape(b, nc, cs, h, p)
            Bn = Bmat.reshape(b, nc, cs, n)
            Cn = Cmat.reshape(b, nc, cs, n)
            Ac = jnp.moveaxis(dA.reshape(b, nc, cs, h), -1, 1)
            A_cs = jnp.cumsum(Ac, axis=-1)
            L = jnp.exp(_segsum(Ac))
            Y_diag = jnp.einsum('bcln,bcsn,bhcls,bcshp->bclhp', Cn, Bn, L, xd)
            decay_states = jnp.exp(A_cs[..., -1:] - A_cs)
            states = jnp.einsum('bcsn,bhcs,bcshp->bchpn', Bn, decay_states, xd)
            chunk_decay = jnp.exp(A_cs[..., -1])
            states_t = jnp.moveaxis(states, 1, 0)
            decay_t = jnp.moveaxis(chunk_decay, -1, 0)

            def step(carry, inp):
                s, d = inp
                new = carry * d[..., None, None] + s
                return (new, carry)
            _, prev_states = jax.lax.scan(step, jnp.zeros_like(states_t[0]), (states_t, decay_t))
            prev_states = jnp.moveaxis(prev_states, 0, 1)
            state_decay = jnp.exp(A_cs)
            Y_off = jnp.einsum('bcln,bchpn,bhcl->bclhp', Cn, prev_states, state_decay)
            Y = (Y_diag + Y_off).reshape(b, l, h, p) + x * D[None, None, :, None]
            y = Y.reshape(b, l, d_ssm)
            yg = y * jax.nn.silu(z)
            yg = yg * jax.lax.rsqrt(jnp.mean(yg * yg, axis=-1, keepdims=True) + EPS) * norm_w
            return jnp.einsum('bld,od->blo', yg, W_out)
        return _mamba2_forward(u, W_in, conv_w, conv_b, dt_bias, A_log, D, norm_w, W_out)

    def _L0_attn_b_ref(x, w_qkv_w, w_qkv_b, w_out_w, w_out_b):
        import jax, jax.numpy as jnp
        import numpy as np
        NUM_HEADS = 16
        D_MODEL = 128
        D_HEAD = D_MODEL // NUM_HEADS
        TOP_K = 64
        B, S, _ = x.shape
        qkv = x @ w_qkv_w.T + w_qkv_b
        qkv = qkv.reshape(B, S, NUM_HEADS, 3, D_HEAD)
        qkv = qkv.transpose(0, 2, 1, 3, 4)
        q, k, v = (qkv[..., 0, :], qkv[..., 1, :], qkv[..., 2, :])
        scores = jnp.einsum('bhqd,bhkd->bhqk', q, k) / np.sqrt(D_HEAD)
        _, idx = jax.lax.top_k(scores, TOP_K)
        knn_mask = jnp.zeros(scores.shape, dtype=bool).at[jnp.arange(B)[:, None, None, None], jnp.arange(NUM_HEADS)[None, :, None, None], jnp.arange(S)[None, None, :, None], idx].set(True)
        logits = jnp.where(knn_mask, scores, -jnp.inf)
        attn_w = jax.nn.softmax(logits, axis=-1)
        attn = jnp.einsum('bhqk,bhkd->bhqd', attn_w, v)
        attn = attn.transpose(0, 2, 1, 3).reshape(B, S, D_MODEL)
        return x + attn @ w_out_w.T + w_out_b

    def _L0_ffn_ref(x, gate_w, gate_b, w1, b1, w2, b2):
        import jax, jax.numpy as jnp
        import numpy as np
        B, T, D = (2, 256, 128)
        E, K, FF = (8, 2, 512)

        def _reference_tuple_inner(x, gate_w, gate_b, w1, b1, w2, b2):
            n_experts = w1.shape[0]
            gate_logits = x @ gate_w + gate_b
            topk_vals, topk_idx = jax.lax.top_k(gate_logits, K)
            topk_w = jax.nn.softmax(topk_vals, axis=-1)
            onehot = jax.nn.one_hot(topk_idx, n_experts, dtype=x.dtype)
            comb = jnp.sum(onehot * topk_w[..., None], axis=2)
            h = jax.nn.gelu(jnp.einsum('btd,edf->ebtf', x, w1) + b1[:, None, None, :], approximate=False)
            y = jnp.einsum('ebtf,efd->ebtd', h, w2) + b2[:, None, None, :]
            output = jnp.einsum('ebtd,bte->btd', y, comb)
            expert_counts = jnp.sum(onehot, axis=(0, 1, 2)).astype(jnp.float32)
            return (output, gate_logits, topk_idx, expert_counts)
        return _reference_tuple_inner(x, gate_w, gate_b, w1, b1, w2, b2)[0]
    x = L0_attn_a_u
    x = x + _L0_attn_a_ref(_layernorm(x, axis=-1), L0_attn_a_W_in, L0_attn_a_conv_w, L0_attn_a_conv_b, L0_attn_a_dt_bias, L0_attn_a_A_log, L0_attn_a_D, L0_attn_a_norm_w, L0_attn_a_W_out)
    x = x + _L0_ffn_ref(_layernorm(x, axis=-1), L0_ffn_gate_w, L0_ffn_gate_b, L0_ffn_w1, L0_ffn_b1, L0_ffn_w2, L0_ffn_b2)
    x = x + _L0_attn_b_ref(_layernorm(x, axis=-1), L0_attn_b_w_qkv_w, L0_attn_b_w_qkv_b, L0_attn_b_w_out_w, L0_attn_b_w_out_b)
    x = x + _L0_ffn_ref(_layernorm(x, axis=-1), L0_ffn_gate_w, L0_ffn_gate_b, L0_ffn_w1, L0_ffn_b1, L0_ffn_w2, L0_ffn_b2)
    return x

_drawn_inputs = setup_inputs


def setup_inputs(seed=0):
    import zlib

    import numpy as np

    out = dict(_drawn_inputs(seed))
    spreads = {'L0_attn_a_conv_b': (0.0, 0.1),
     'L0_attn_a_D': (1.0, 0.2),
     'L0_attn_a_norm_w': (1.0, 0.2),
     'L0_attn_b_w_qkv_b': (0.0, 0.1),
     'L0_attn_b_w_out_b': (0.0, 0.1),
     'L0_ffn_gate_b': (0.0, 0.1),
     'L0_ffn_b1': (0.0, 0.416),
     'L0_ffn_b2': (0.0, 0.1)}
    factors = {}
    for name, (base, spread) in spreads.items():
        noise = np.random.default_rng([zlib.crc32(name.encode()), seed]).standard_normal(out[name].shape)
        drawn = base * np.exp(spread * noise) if base else spread * noise
        out[name] = jnp.asarray(drawn.astype(out[name].dtype))
    for name, factor in factors.items():
        out[name] = (out[name] * factor).astype(out[name].dtype)
    return out
```

```python
from contextlib import ExitStack

import numpy as np

import concourse.bass as bass
from concourse import mybir

ALU = mybir.AluOpType
ACT = mybir.ActivationFunctionType
AX = mybir.AxisListType
F32 = mybir.dt.float32

P = 128
D = 128
BANK = 512
EPS = 1e-5
BIG = 1e30


HEADS, DH = 16, 8


class Chain:

    def __init__(self, eng, sem):
        self.eng, self.sem, self.n = eng, sem, 0

    def __call__(self, ins):
        self.n += 1
        ins.then_inc(self.sem, 1)
        self.eng.wait_ge(self.sem, self.n)


def constants(nc, ctx, S):
    sb = lambda name, shape: ctx.enter_context(nc.sbuf_tensor(name, shape, F32))
    S.ident = sb("ident", [P, P])
    S.upper = sb("upper", [P, P])
    S.cap = sb("cap", [P, P])
    S.ones = sb("ones", [P, P])
    S.headmask = sb("headmask", [P, HEADS])
    filled = ctx.enter_context(nc.semaphore("const_filled"))
    built = ctx.enter_context(nc.semaphore("const_built"))
    with nc.Block() as block:

        @block.gpsimd
        def _(pool):
            nc.gpsimd.memset(S.ident[:], 0.0)
            nc.gpsimd.memset(S.upper[:], 1.0)
            nc.gpsimd.memset(S.cap[:], 0.0)
            nc.gpsimd.memset(S.ones[:], 1.0).then_inc(filled, 1)
            pool.wait_ge(filled, 1)
            nc.gpsimd.affine_select(out=S.ident[:], in_=S.ident[:], compare_op=ALU.not_equal, fill=1.0,
                                    base=0, pattern=[[-1, P]], channel_multiplier=1)
            nc.gpsimd.affine_select(out=S.upper[:], in_=S.upper[:], compare_op=ALU.is_ge, fill=0.0,
                                    base=0, pattern=[[1, P]], channel_multiplier=-1)
            nc.gpsimd.affine_select(out=S.cap[:], in_=S.cap[:], compare_op=ALU.is_ge, fill=-BIG,
                                    base=0, pattern=[[1, P]], channel_multiplier=-1).then_inc(built, 1)
            pool.wait_ge(built, 1)
            nc.gpsimd.memset(S.headmask[:], 1.0).then_inc(built, 1)
            pool.wait_ge(built, 2)
            nc.gpsimd.affine_select(out=S.headmask[:], in_=S.headmask[:], compare_op=ALU.is_ge, fill=0.0, base=0,
                                    pattern=[[-DH, HEADS]], channel_multiplier=1).then_inc(built, 1)
            pool.wait_ge(built, 3)
            nc.gpsimd.affine_select(out=S.headmask[:], in_=S.headmask[:], compare_op=ALU.is_ge, fill=0.0, base=DH - 1,
                                    pattern=[[DH, HEADS]], channel_multiplier=-1).then_inc(built, 1)
            pool.wait_ge(built, 4)


class Norm:

    def __init__(self, nc, ctx, tag, S):
        sem = lambda n: ctx.enter_context(nc.semaphore(f"{tag}_{n}"))
        self.S = S
        self.stats_done, self.chain, self.var_ready = sem("stats_done"), sem("stat_chain"), sem("var_ready")
        self.sqrt_done, self.normed = sem("sqrt_done"), sem("normed")
        self.turned, self.stored = sem("turned"), sem("hT_stored")

    def all(self):
        return [self.stats_done, self.chain, self.var_ready, self.sqrt_done, self.normed, self.turned, self.stored]

    def vector(self, v, NT):
        S = self.S
        with v.Fori(0, NT) as t:
            v.bn_stats(S.st[:, t, :], S.x[:, t, :]).then_inc(self.stats_done, 1)
        v.wait_ge(self.stats_done, NT)
        me, mo = S.st[:, :, 1], S.st[:, :, 4]
        qe, qo = S.st[:, :, 2], S.st[:, :, 5]
        a = lambda k: S.sm[:, k, 0:NT]
        step = Chain(v, self.chain)
        v.tensor_tensor(a(0), me, mo, ALU.add)
        v.tensor_tensor(a(1), me, mo, ALU.subtract)
        step(v.tensor_tensor(a(2), qe, qo, ALU.add))
        v.tensor_scalar(a(3), a(0), 0.5, None, ALU.mult)
        v.tensor_tensor(a(4), a(1), a(1), ALU.mult)
        step(v.tensor_scalar(a(5), a(2), 1.0 / D, EPS, ALU.mult, ALU.add))
        v.scalar_tensor_tensor(a(6), a(4), 0.25, a(5), ALU.mult, ALU.add).then_inc(self.var_ready, 1)
        v.wait_ge(self.sqrt_done, 1)
        step(v.reciprocal(a(0), a(7)))
        with v.Fori(0, NT) as t:
            v.tensor_scalar(S.hn[:, t, :], S.x[:, t, :], S.sm[:, 3, bass.ds(t, 1)], S.sm[:, 0, bass.ds(t, 1)],
                            ALU.subtract, ALU.mult).then_inc(self.normed, 1)
        for b in (1, 3):
            v.wait_ge(self.turned, 4 * (b + 1))
            v.tensor_copy(S.hT[:, b * BANK:(b + 1) * BANK], S.ps[:, b * BANK:(b + 1) * BANK]).then_inc(self.stored, 1)

    def scalar(self, act, NT):
        S = self.S
        act.wait_ge(self.var_ready, 1)
        act.activation(S.sm[:, 7, 0:NT], S.sm[:, 6, 0:NT], ACT.Sqrt).then_inc(self.sqrt_done, 1)
        for b in (0, 2):
            act.wait_ge(self.turned, 4 * (b + 1))
            act.copy(S.hT[:, b * BANK:(b + 1) * BANK], S.ps[:, b * BANK:(b + 1) * BANK]).then_inc(self.stored, 1)

    def tensor(self, pe, NT):
        S = self.S
        for t in range(NT):
            pe.wait_ge(self.normed, t + 1)
            pe.transpose(S.ps[:, bass.ds(t * P, P)], S.hn[:, t, :], S.ident[:]).then_inc(self.turned, 1)
        pe.wait_ge(self.stored, NT * P // BANK)


def mamba(nc, ctx, S, A):
    with ExitStack() as own:
        sb = lambda name, shape: own.enter_context(nc.sbuf_tensor(name, shape, F32))
        sem = lambda name: ctx.enter_context(nc.semaphore("m_" + name))
        NT, T, H, G = S.NT, S.T, 2, 4
        w_in = sb("w_in", [P, A["w_in"].shape[1]])
        w_mo = sb("w_mo", [P, H, D])
        convw = sb("convw", [P, G, 4])
        vecs = sb("vecs", [P, G + H])
        rows = sb("rows", [P, 3, H])
        xp = sb("xp", [P, G, 3 + T])
        xc = sb("xc", [P, G, T])
        z = sb("z", [P, NT, H * P])
        y = sb("y", [P, NT, H * P])
        dtr = sb("dtr", [P, 6, NT * H])
        negA = sb("negA", [P, H])
        diagD = sb("diagD", [P, H, P])
        state = sb("state", [P, 2, H, P])
        xt = sb("xt", [P, 2, 3 * P])
        uda = sb("uda", [P, 2, H, P])
        arg = sb("arg", [P, 2, H, P])
        el = sb("el", [P, 2, H, P])
        ec = sb("ec", [P, 2, H, P])
        cd = sb("cd", [P, 2, H, P])
        mt = sb("mt", [P, 2, H, P])
        bw = sb("bw", [P, 2, H, P])
        sq = sb("sq", [P, H * P])
        ygT = sb("ygT", [P, 2, H, P])
        norm = Norm(nc, ctx, "ln0", S)
        loaded = S.m_loaded
        names = ("xin_ready xin_stored z_ready z_stored dt_ready dt_stored dt_chain pad_zero conv_step act_chain silu_done "
                 "cs_ready cs_stored dec_done wdt_done uda_done csb_ready ec_done arg_done exp_done turned xt_stored g_ready "
                 "mix_done y_ready y_done ds_ready state_done yn_chain ssq_done rms_sqrt yn_done ygt_ready ygt_stored "
                 "o_ready res_done diag_done sumsq const_done").split()
        s = {n: sem(n) for n in names}
        ps = S.ps
        block = own.enter_context(nc.Block())

        @block.sync
        def _(sp):
            sp.dma_start(S.x[:], A["u"].rearrange("(t p) d -> p t d", p=P)).then_inc(S.x_loaded, 16)
            sp.dma_start(w_in[:], A["w_in"]).then_inc(loaded, 16)
            sp.dma_start(convw[:], A["conv_w"].rearrange("(g p) k -> p g k", p=P)).then_inc(loaded, 16)
            sp.dma_start(vecs[:, 0:G], A["conv_b"]).then_inc(loaded, 16)
            sp.dma_start(vecs[:, G:G + H], A["norm_w"]).then_inc(loaded, 16)
            sp.dma_start(w_mo[:], A["w_mo"].rearrange("(h p) o -> p h o", p=P)).then_inc(loaded, 16)
            for k, vec in enumerate((A["dt_bias"], A["a_log"], A["dskip"])):
                sp.dma_start(rows[:, k, :], vec.partition_broadcast(P)).then_inc(loaded, 16)

        @block.tensor
        def _(pe):
            norm.tensor(pe, NT)
            pe.wait_ge(loaded, 16 * 8)
            for n in range(G * 4):
                g, c = n // 4, n % 4
                if n >= 4:
                    pe.wait_ge(s["xin_stored"], n - 3)
                pe.matmul(ps[:, (4 + n % 4) * BANK:(5 + n % 4) * BANK], w_in[:, H * P + g * P:H * P + (g + 1) * P],
                          S.hT[:, c * BANK:(c + 1) * BANK], start=True, stop=True).then_inc(s["xin_ready"], 1)
            for t in range(NT):
                pe.matmul(ps[:, bass.ds(t * H, H)], S.hT[:, bass.ds(t * P, P)], w_in[:, 6 * P:6 * P + H],
                          start=True, stop=True).then_inc(s["dt_ready"], 1)
            for i in range(NT // 2):
                for u in range(2):
                    if i >= 1:
                        pe.wait_ge(s["z_stored"], i * 2 - 1 + u)
                    pe.matmul(ps[:, (2 + u) * BANK:(2 + u) * BANK + H * P], S.hT[:, bass.ds(i * 2 * P + u * P, P)],
                              w_in[:, 0:H * P], start=True, stop=True).then_inc(s["z_ready"], 1)
            pe.wait_ge(s["dt_stored"], 1)
            pe.matmul(ps[:, BANK:BANK + NT * H], S.upper[:], dtr[:, 1, :], start=True, stop=True)
            pe.matmul(ps[:, BANK + 64:BANK + 64 + NT * H], S.ones[:], dtr[:, 1, :], start=True,
                      stop=True).then_inc(s["cs_ready"], 1)
            pe.wait_ge(s["silu_done"], G + 1)
            pe.wait_ge(s["const_done"], 2)
            pe.wait_ge(s["cs_stored"], 1)

            def chunk(c, u):
                tk = bass.ds(c * P, P)
                for k in range(3):
                    ins = pe.transpose(ps[:, u * BANK + k * P:u * BANK + (k + 1) * P], xc[:, k, tk], S.ident[:])
                ins.then_inc(s["turned"], 1)
                pe.matmul(ps[:, (2 + u) * BANK:(2 + u) * BANK + P], xc[:, 2, tk], xc[:, 3, tk], start=True,
                          stop=True).then_inc(s["g_ready"], 1)
                pe.wait_ge(s["uda_done"], c + 1)
                pe.matmul(ps[:, (4 + u) * BANK:(4 + u) * BANK + H * P], S.ones[:],
                          uda[:, u, :, :].rearrange("p h l -> p (h l)"), start=True,
                          stop=True).then_inc(s["csb_ready"], 1)
                pe.wait_ge(s["xt_stored"], c + 1)
                pe.wait_ge(s["mix_done"], c + 1)
                for h in range(H):
                    Y = ps[:, 6 * BANK + h * P:6 * BANK + (h + 1) * P]
                    xh = xt[:, u, h * P:(h + 1) * P]
                    pe.matmul(Y, mt[:, u, h, :], xh, start=True, stop=False)
                    pe.matmul(Y, diagD[:, h, :], xh, start=False, stop=False)
                    ins = pe.matmul(Y, cd[:, u, h, :], state[:, u, h, :], start=False, stop=True)
                ins.then_inc(s["y_ready"], 1)
                for h in range(H):
                    ins = pe.matmul(ps[:, 7 * BANK + h * P:7 * BANK + (h + 1) * P], bw[:, u, h, :],
                                    xt[:, u, h * P:(h + 1) * P], start=True, stop=True)
                ins.then_inc(s["ds_ready"], 1)
                pe.wait_ge(s["y_done"], c + 1)
                pe.wait_ge(s["state_done"], c + 1)

            for i in range(NT // 2):
                for u in range(2):
                    chunk(i * 2 + u, u)

            for i in range(NT // 2):
                for u in range(2):
                    t = i * 2 + u
                    pe.wait_ge(s["yn_done"], t + 1)
                    for h in range(H):
                        ins = pe.transpose(ps[:, u * BANK + h * P:u * BANK + (h + 1) * P],
                                           y[:, t, h * P:(h + 1) * P], S.ident[:])
                    ins.then_inc(s["ygt_ready"], 1)
                    pe.wait_ge(s["ygt_stored"], t + 1)
                    for h in range(H):
                        ins = pe.matmul(ps[:, (2 + u) * BANK:(2 + u) * BANK + D], ygT[:, u, h, :], w_mo[:, h, :],
                                        start=(h == 0), stop=(h == H - 1))
                    ins.then_inc(s["o_ready"], 1)
                    pe.wait_ge(s["res_done"], t + 1)

        @block.scalar
        def _(act):
            norm.scalar(act, NT)
            for n in range(G * 4):
                g, c = n // 4, n % 4
                act.wait_ge(s["xin_ready"], n + 1)
                act.copy(xp[:, g, 3 + c * BANK:3 + (c + 1) * BANK],
                         ps[:, (4 + n % 4) * BANK:(5 + n % 4) * BANK]).then_inc(s["xin_stored"], 1)
            link = Chain(act, s["act_chain"])
            act.wait_ge(s["dt_chain"], 3)
            link(act.activation(dtr[:, 3, :], dtr[:, 2, :], ACT.Exp))
            act.activation(negA[:], rows[:, 1, :], ACT.Exp)
            act.activation(dtr[:, 4, :], dtr[:, 3, :], ACT.Ln, bias=1.0).then_inc(s["act_chain"], 1)
            with act.Fori(0, NT // 2) as i:
                for u in range(2):
                    act.wait_ge(s["z_ready"], i * 2 + u + 1)
                    act.activation(z[:, i * 2 + u, :], ps[:, (2 + u) * BANK:(2 + u) * BANK + H * P],
                                   ACT.Silu).then_inc(s["z_stored"], 1)
            for g in range(G):
                act.wait_ge(s["conv_step"], 4 * (g + 1))
                act.activation(xc[:, g, :], xp[:, g, 3:3 + T], ACT.Silu).then_inc(s["silu_done"], 1)
            act.wait_ge(s["cs_stored"], 1)
            act.activation(dtr[:, 4, :], dtr[:, 3, :], ACT.Exp)
            act.activation(dtr[:, 5, :], dtr[:, 5, :], ACT.Exp).then_inc(s["silu_done"], 1)

            def chunk(c, u):
                act.wait_ge(s["turned"], c + 1)
                act.copy(xt[:, u, :], ps[:, u * BANK:u * BANK + 3 * P]).then_inc(s["xt_stored"], 1)
                act.wait_ge(s["csb_ready"], c + 1)
                act.activation(ec[:, u, :, :].rearrange("p h l -> p (h l)"),
                               ps[:, (4 + u) * BANK:(4 + u) * BANK + H * P], ACT.Exp).then_inc(s["ec_done"], 1)
                act.wait_ge(s["arg_done"], c + 1)
                act.activation(el[:, u, :, :].rearrange("p h l -> p (h l)"),
                               arg[:, u, :, :].rearrange("p h l -> p (h l)"), ACT.Exp).then_inc(s["exp_done"], 1)

            with act.Fori(0, NT // 2) as i:
                for u in range(2):
                    chunk(i * 2 + u, u)
            act.wait_ge(s["ssq_done"], 1)
            act.activation(S.sm[:, 1, 0:NT], S.sm[:, 0, 0:NT], ACT.Sqrt).then_inc(s["rms_sqrt"], 1)
            with act.Fori(0, NT // 2) as i:
                for u in range(2):
                    act.wait_ge(s["ygt_ready"], i * 2 + u + 1)
                    for h in range(H):
                        ins = act.activation(ygT[:, u, h, :], ps[:, u * BANK + h * P:u * BANK + (h + 1) * P],
                                             ACT.Copy, scale=vecs[:, G + h:G + h + 1])
                    ins.then_inc(s["ygt_stored"], 1)

        @block.gpsimd
        def _(pool):
            nc.gpsimd.memset(xp[:, :, 0:3], 0.0).then_inc(s["pad_zero"], 1)
            nc.gpsimd.memset(state[:, 0, :, :], 0.0).then_inc(s["const_done"], 1)
            pool.wait_ge(loaded, 16 * 8)
            for h in range(H):
                ins = nc.gpsimd.tensor_scalar(diagD[:, h, :], S.ident[:], rows[:, 2, h:h + 1], None, ALU.mult)
            ins.then_inc(s["const_done"], 1)

        @block.vector
        def _(v):
            v.wait_ge(S.x_loaded, 16)
            norm.vector(v, NT)
            v.wait_ge(loaded, 16 * 8)
            v.wait_ge(s["pad_zero"], 1)
            step = Chain(v, s["dt_chain"])
            d = lambda k: dtr[:, k, :]
            dth = lambda k, h: dtr[:, k, :].rearrange("p (t h) -> p t h", h=H)[:, :, h]
            v.wait_ge(s["dt_ready"], NT)
            psd = ps[:, 0:NT * H].rearrange("p (t h) -> p t h", h=H)
            for h in range(H):
                ins = v.tensor_scalar(dth(0, h), psd[:, :, h], rows[:, 0, h:h + 1], None, ALU.add)
            step(ins)
            step(v.tensor_scalar(d(5), d(0), -1.0, None, ALU.mult))
            step(v.tensor_tensor(d(2), d(0), d(5), ALU.min))
            v.wait_ge(s["act_chain"], 2)
            step(v.tensor_scalar(d(1), d(0), 0.0, None, ALU.max))
            step(v.tensor_tensor(d(0), d(1), d(4), ALU.add))
            for h in range(H):
                ins = v.tensor_scalar(dth(1, h), dth(0, h), negA[:, h:h + 1], -1.0, ALU.mult, ALU.mult)
            ins.then_inc(s["dt_stored"], 1)
            for g in range(G):
                v.wait_ge(s["xin_stored"], 4 * (g + 1))
                link = g * 4
                v.tensor_scalar(xc[:, g, :], xp[:, g, 0:T], convw[:, g, 0:1], vecs[:, g:g + 1], ALU.mult,
                                ALU.add).then_inc(s["conv_step"], 1)
                v.wait_ge(s["conv_step"], link + 1)
                for k in (1, 2):
                    v.scalar_tensor_tensor(xc[:, g, :], xp[:, g, k:k + T], convw[:, g, k:k + 1], xc[:, g, :],
                                           ALU.mult, ALU.add).then_inc(s["conv_step"], 1)
                    v.wait_ge(s["conv_step"], link + 1 + k)
                v.scalar_tensor_tensor(xp[:, g, 3:3 + T], xp[:, g, 3:3 + T], convw[:, g, 3:4], xc[:, g, :],
                                       ALU.mult, ALU.add).then_inc(s["conv_step"], 1)
            v.wait_ge(s["cs_ready"], 1)
            v.tensor_copy(d(2), ps[:, BANK:BANK + NT * H])
            step(v.tensor_copy(d(5), ps[:, BANK + 64:BANK + 64 + NT * H]))
            v.tensor_tensor(d(3), d(5), d(2), ALU.subtract).then_inc(s["cs_stored"], 1)
            v.wait_ge(s["silu_done"], G + 1)
            step(v.tensor_tensor(d(4), d(4), d(0), ALU.mult))

            def chunk(c, u):
                col = lambda k, h: dtr[:, k, bass.ds(c * H + h, 1)]
                for h in range(H):
                    ins = v.tensor_scalar(uda[:, u, h, :], S.upper[:], col(1, h), None, ALU.mult)
                ins.then_inc(s["uda_done"], 1)
                v.wait_ge(s["ec_done"], c + 1)
                for h in range(H):
                    ins = v.scalar_tensor_tensor(arg[:, u, h, :], ps[:, (4 + u) * BANK + h * P:(4 + u) * BANK + (h + 1) * P],
                                                 col(2, h), S.cap[:], ALU.subtract, ALU.min)
                ins.then_inc(s["arg_done"], 1)
                v.wait_ge(s["xt_stored"], c + 1)
                for h in range(H):
                    v.tensor_scalar(bw[:, u, h, :], xt[:, u, 2 * P:3 * P], col(4, h), None, ALU.mult)
                v.wait_ge(s["exp_done"], c + 1)
                v.wait_ge(s["g_ready"], c + 1)
                for h in range(H):
                    v.tensor_tensor(cd[:, u, h, :], xc[:, 3, bass.ds(c * P, P)], ec[:, u, h, :], ALU.mult)
                    ins = v.scalar_tensor_tensor(mt[:, u, h, :], el[:, u, h, :], col(0, h),
                                                 ps[:, (2 + u) * BANK:(2 + u) * BANK + P], ALU.mult, ALU.mult)
                ins.then_inc(s["mix_done"], 1)
                v.wait_ge(s["y_ready"], c + 1)
                v.tensor_tensor(y[:, c, :], ps[:, 6 * BANK:6 * BANK + H * P], z[:, c, :],
                                ALU.mult).then_inc(s["y_done"], 1)
                v.wait_ge(s["ds_ready"], c + 1)
                for h in range(H):
                    ins = v.scalar_tensor_tensor(state[:, 1 - u, h, :], state[:, u, h, :], col(5, h),
                                                 ps[:, 7 * BANK + h * P:7 * BANK + (h + 1) * P], ALU.mult, ALU.add)
                ins.then_inc(s["state_done"], 1)
                v.wait_ge(s["state_done"], c + 1)

            v.wait_ge(s["const_done"], 2)
            with v.Fori(0, NT // 2) as i:
                for u in range(2):
                    chunk(i * 2 + u, u)
            v.wait_ge(s["y_done"], NT)
            with v.Fori(0, NT) as t:
                v.tensor_tensor(z[:, t, :], y[:, t, :], y[:, t, :], ALU.mult).then_inc(s["sumsq"], 1)
            v.wait_ge(s["sumsq"], NT)
            link = Chain(v, s["yn_chain"])
            link(v.tensor_reduce(S.sm[:, 2, 0:NT], z[:], AX.X, ALU.add))
            v.tensor_scalar(S.sm[:, 0, 0:NT], S.sm[:, 2, 0:NT], 1.0 / (H * P), EPS, ALU.mult,
                            ALU.add).then_inc(s["ssq_done"], 1)
            v.wait_ge(s["rms_sqrt"], 1)
            link(v.reciprocal(S.sm[:, 3, 0:NT], S.sm[:, 1, 0:NT]))
            with v.Fori(0, NT) as t:
                v.tensor_scalar(y[:, t, :], y[:, t, :], S.sm[:, 3, bass.ds(t, 1)], None,
                                ALU.mult).then_inc(s["yn_done"], 1)
            with v.Fori(0, NT // 2) as i:
                for u in range(2):
                    t = i * 2 + u
                    v.wait_ge(s["o_ready"], t + 1)
                    v.tensor_tensor(S.x[:, t, :], S.x[:, t, :], ps[:, (2 + u) * BANK:(2 + u) * BANK + D],
                                    ALU.add).then_inc(s["res_done"], 1)
            v.wait_ge(s["res_done"], NT)


def moe_semaphores(nc, ctx):
    sem = lambda n: ctx.enter_context(nc.semaphore("moe_" + n))
    names = ("loaded gate_ready gate_chain top_done top_diff exp_done comb_done combt_ready combt_stored "
             "bias_ready acc_init iota_done h_ready hid_ready y_ready y_added stored w_loaded "
             "w1_loaded_0 w1_loaded_1 w2_loaded_0 w2_loaded_1 gate").split()
    return {n: sem(n) for n in names}


def moe(nc, S, A, tag, s, norm, out=None):
    with ExitStack() as own:
        sb = lambda name, shape, dt=F32: own.enter_context(nc.sbuf_tensor(f"{tag}_{name}", shape, dt))
        NT, T, E, FB = S.NT, S.T, 8, 4
        NC = T // BANK
        w1 = sb("w1", [P, 2, FB * P])
        w2 = sb("w2", [P, 2, FB, D])
        b1 = sb("b1", [P, E * FB])
        b2 = sb("b2", [E, D])
        gw = sb("gw", [P, E])
        gb = sb("gb", [P, E])
        lg = sb("lg", [P, NT, E])
        m8 = sb("m8", [P, NT, E])
        i8 = sb("i8", [P, NT, E], mybir.dt.uint32)
        i8f = sb("i8f", [P, NT, E])
        iot = sb("iot", [P, NT, E])
        c1 = sb("c1", [P, NT, E])
        c2 = sb("c2", [P, NT, E])
        comb = sb("comb", [P, NT, E])
        combT = sb("combT", [E, T])
        hid = sb("hid", [P, 2, FB, BANK])
        ps = S.ps
        acc = S.x
        block = own.enter_context(nc.Block())

        @block.sync
        def _(sp):
            sp.dma_start(gw[:], A["gate_w"]).then_inc(s["loaded"], 16)
            sp.dma_start(gb[:], A["gate_b"].partition_broadcast(P)).then_inc(s["loaded"], 16)
            sp.dma_start(b2[:], A["b2"]).then_inc(s["loaded"], 16)
            sp.dma_start(b1[:], A["b1T"]).then_inc(s["w_loaded"], 16)


            def load_expert(e, u):
                sp.dma_start(w1[:, u, :], A["w1"][e, :, :]).then_inc(s[f"w1_loaded_{u}"], 16)
                sp.dma_start(w2[:, u, :, :], A["w2"][e, :, :].rearrange("(k f) d -> f k d", f=P)).then_inc(
                    s[f"w2_loaded_{u}"], 16)

            load_expert(0, 0)
            load_expert(1, 1)
            with sp.Fori(1, E // 2) as i:
                for u in range(2):
                    sp.wait_ge(s["y_ready"], (i * 2 + u - 1) * NC)
                    load_expert(i * 2 + u, u)
            if out is not None:
                sp.wait_ge(s["y_added"], 4 * NC * E + 1)
                sp.dma_start(out.rearrange("(t p) d -> p t d", p=P), S.x[:]).then_inc(s["stored"], 16)
                sp.wait_ge(s["stored"], 16)

        @block.gpsimd
        def _(pool):
            nc.gpsimd.iota(iot[:], pattern=[[0, NT], [1, E]], base=0, channel_multiplier=0,
                           allow_small_or_imprecise_dtypes=True).then_inc(s["iota_done"], 1)

        @block.tensor
        def _(pe):
            norm.tensor(pe, NT)
            pe.wait_ge(s["loaded"], 48)
            for t in range(NT):
                pe.matmul(ps[:, bass.ds(t * E, E)], S.hT[:, bass.ds(t * P, P)], gw[:], start=True,
                          stop=True).then_inc(s["gate_ready"], 1)


            def hidden(u, c, n):
                if n is not None:
                    pe.wait_ge(s["hid_ready"], n)
                for f in range(FB):
                    ins = pe.matmul(ps[:, f * BANK:(f + 1) * BANK], w1[:, u, f * P:(f + 1) * P],
                                    S.hT[:, c * BANK:(c + 1) * BANK], start=True, stop=True)
                ins.then_inc(s["h_ready"], 1)

            def down(u, c, n):
                pe.wait_ge(s["hid_ready"], n + 1)
                for k in range(4):
                    Y = ps[:, (6 + c % 2) * BANK + k * P:(6 + c % 2) * BANK + (k + 1) * P]
                    for f in range(FB):
                        ins = pe.matmul(Y, hid[:, c % 2, f, k * P:(k + 1) * P], w2[:, u, f, :],
                                        start=(f == 0), stop=(f == FB - 1))
                ins.then_inc(s["y_ready"], 1)

            pe.wait_ge(s["comb_done"], 1)
            for t in range(NT):
                pe.transpose(ps[0:E, bass.ds(t * P, P)], comb[:, t, :], S.ident[:]).then_inc(s["combt_ready"], 1)
            pe.wait_ge(s["combt_stored"], NC)
            for t in range(NT):
                pe.matmul(ps[:, bass.ds(t * P, P)], combT[:, bass.ds(t * P, P)], b2[:], start=True,
                          stop=True).then_inc(s["bias_ready"], 1)
            pe.wait_ge(s["acc_init"], NC)

            pe.wait_ge(s["w1_loaded_0"], 16)
            hidden(0, 0, None)

            def expert(i, u, last=False):
                e = i * 2 + u
                pe.wait_ge(s[f"w2_loaded_{u}"], i * 16 + 16)
                for c in range(NC):
                    n = e * NC + c
                    if c < NC - 1:
                        hidden(u, c + 1, n + 1)
                    elif not last:
                        pe.wait_ge(s[f"w1_loaded_{1 - u}"], (i + u) * 16 + 16)
                        hidden(1 - u, 0, n + 1)
                    pe.wait_ge(s["y_added"], (n * 4 - 3) if c >= 1 else e * 16 + 1)
                    down(u, c, n)

            with pe.Fori(0, E // 2 - 1) as i:
                expert(i, 0)
                expert(i, 1)
            expert(E // 2 - 1, 0)
            expert(E // 2 - 1, 1, last=True)

        @block.scalar
        def _(act):
            norm.scalar(act, NT)
            act.wait_ge(s["top_diff"], 1)
            act.activation(S.sm[:, 1, 0:NT], S.sm[:, 0, 0:NT], ACT.Exp).then_inc(s["exp_done"], 1)
            for c in range(NC):
                act.wait_ge(s["combt_ready"], 4 * (c + 1))
                act.copy(combT[:, c * BANK:(c + 1) * BANK], ps[0:E, c * BANK:(c + 1) * BANK]).then_inc(
                    s["combt_stored"], 1)
            act.wait_ge(s["w_loaded"], 16)

            def gelus(e, c, first=False):
                n = e * NC + c
                act.wait_ge(s["h_ready"], n + 1)
                if not (first and c < 2):
                    act.wait_ge(s["y_ready"], n - 1)
                act.sem_inc(s["gate"], 1)
                for f in range(FB):
                    ins = act.activation(hid[:, c % 2, f, :], ps[:, f * BANK:(f + 1) * BANK], ACT.Gelu,
                                         bias=b1[:, bass.ds(e * FB + f, 1)])
                ins.then_inc(s["hid_ready"], 1)

            for c in range(NC):
                gelus(0, c, first=True)
            with act.Fori(1, E) as e:
                for c in range(NC):
                    gelus(e, c)

        @block.vector
        def _(v):
            norm.vector(v, NT)
            step = Chain(v, s["gate_chain"])
            bc = lambda ap: ap.unsqueeze(2).to_broadcast([P, NT, E])
            v.wait_ge(s["loaded"], 48)
            v.wait_ge(s["gate_ready"], NT)
            step(v.tensor_tensor(lg[:], ps[:, 0:NT * E].rearrange("p (t e) -> p t e", e=E),
                                 gb[:].unsqueeze(1).to_broadcast([P, NT, E]), ALU.add))
            for t in range(NT):
                ins = v.max(m8[:, t, :], lg[:, t, :])
            ins.then_inc(s["top_done"], 1)
            v.wait_ge(s["top_done"], 1)
            v.tensor_tensor(S.sm[:, 0, 0:NT], m8[:, :, 1], m8[:, :, 0], ALU.subtract).then_inc(s["top_diff"], 1)
            for t in range(NT):
                ins = v.max_index(i8[:, t, :], m8[:, t, :], lg[:, t, :])
            step(ins)
            step(v.tensor_copy(i8f[:], i8[:]))
            v.wait_ge(s["iota_done"], 1)
            v.tensor_tensor(c1[:], iot[:], bc(i8f[:, :, 0]), ALU.is_equal)
            v.tensor_tensor(c2[:], iot[:], bc(i8f[:, :, 1]), ALU.is_equal)
            v.wait_ge(s["exp_done"], 1)
            step(v.tensor_scalar(S.sm[:, 2, 0:NT], S.sm[:, 1, 0:NT], 1.0, None, ALU.add))
            step(v.reciprocal(S.sm[:, 3, 0:NT], S.sm[:, 2, 0:NT]))
            step(v.tensor_tensor(S.sm[:, 4, 0:NT], S.sm[:, 3, 0:NT], S.sm[:, 1, 0:NT], ALU.mult))
            v.tensor_tensor(c1[:], c1[:], bc(S.sm[:, 3, 0:NT]), ALU.mult)
            step(v.tensor_tensor(c2[:], c2[:], bc(S.sm[:, 4, 0:NT]), ALU.mult))
            v.tensor_tensor(comb[:], c1[:], c2[:], ALU.add).then_inc(s["comb_done"], 1)
            for c in range(NC):
                v.wait_ge(s["bias_ready"], 4 * (c + 1))
                v.tensor_tensor(acc[:, 4 * c:4 * c + 4, :], acc[:, 4 * c:4 * c + 4, :],
                                ps[:, c * BANK:(c + 1) * BANK].rearrange("p (t d) -> p t d", d=D),
                                ALU.add).then_inc(s["acc_init"], 1)
            v.wait_ge(s["acc_init"], NC)
            v.sem_inc(s["y_added"], 1)
            v.wait_ge(s["comb_done"], 1)
            v.wait_ge(s["acc_init"], NC)
            with v.Fori(0, E) as e:
                for c in range(NC):
                    n = e * NC + c
                    v.wait_ge(s["y_ready"], n + 1)
                    v.wait_ge(s["y_added"], e * 16 + 1)
                    for k in range(4):
                        t = 4 * c + k
                        Y = ps[:, (6 + c % 2) * BANK + k * P:(6 + c % 2) * BANK + (k + 1) * P]
                        v.scalar_tensor_tensor(acc[:, t, :], Y, comb[:, t, bass.ds(e, 1)], acc[:, t, :],
                                               ALU.mult, ALU.add).then_inc(s["y_added"], 1)
            v.wait_ge(s["y_added"], 4 * NC * E + 1)


TOPK = 64
SEGS = 16
ROUNDS = 7
LOWEST = -3.0e38


def attention(nc, ctx, S, A):
    with ExitStack() as own:
        NT, T = S.NT, S.T
        NCH = T // BANK
        sb = lambda name, shape, dt=F32: own.enter_context(nc.sbuf_tensor("at_" + name, shape, dt))
        sem = lambda name: ctx.enter_context(nc.semaphore("at_" + name))
        qT = sb("qT", [P, T])
        kT = sb("kT", [P, T])
        V = sb("V", [P, NT, HEADS * DH])
        wo = sb("wo", [P, D])
        count = sb("count", [P, NT * HEADS])
        project_qkv(nc, ctx, S, A, qT, kT, V, wo)
        select_and_mix(nc, ctx, S, qT, kT, V, count)
        redo(nc, ctx, S, qT, kT, V, count)
        project_out(nc, ctx, S, A, wo)


def project_qkv(nc, ctx, S, A, qT, kT, V, wo):
    with ExitStack() as own:
        NT, T = S.NT, S.T
        NCH = T // BANK
        sb = lambda name, shape, dt=F32: own.enter_context(nc.sbuf_tensor("qk_" + name, shape, dt))
        wqk = sb("wqk", [P, 2, P])
        bqk = sb("bqk", [P, 2])
        wv = sb("wv", [P, D])
        bv = sb("bv", [P, D])
        bo = sb("bo", [P, D])
        norm = Norm(nc, ctx, "atln", S)
        s = {n: ctx.enter_context(nc.semaphore("qk_" + n)) for n in
             "loaded ready_a ready_v stored_a stored_v v_ready v_stored res".split()}
        ps = S.ps
        block = own.enter_context(nc.Block())

        @block.sync
        def _(sp):
            sp.dma_start(wqk[:], A["wqk"]).then_inc(s["loaded"], 16)
            sp.dma_start(bqk[:], A["bqk"]).then_inc(s["loaded"], 16)
            sp.dma_start(wv[:], A["wv"]).then_inc(s["loaded"], 16)
            sp.dma_start(bv[:], A["bv"].partition_broadcast(P)).then_inc(s["loaded"], 16)
            sp.dma_start(wo[:], A["w_o"]).then_inc(s["loaded"], 16)
            sp.dma_start(bo[:], A["b_o"].partition_broadcast(P)).then_inc(s["loaded"], 16)

        items = [(side, c) for side in range(2) for c in range(NCH)]

        @block.tensor
        def _(pe):
            norm.tensor(pe, NT)
            pe.wait_ge(s["loaded"], 96)
            for n, (side, c) in enumerate(items):
                who = "a" if c % 2 == 0 else "v"
                if n >= NCH:
                    pe.wait_ge(s["stored_" + who], n // NCH * 2 - 1 + c // 2)
                pe.matmul(ps[:, c * BANK:(c + 1) * BANK], wqk[:, side, :], S.hT[:, c * BANK:(c + 1) * BANK],
                          start=True, stop=True).then_inc(s["ready_" + who], 1)
            for t in range(NT):
                pe.matmul(ps[:, 4 * BANK + t * D:4 * BANK + (t + 1) * D], S.hT[:, t * P:(t + 1) * P], wv[:],
                          start=True, stop=True).then_inc(s["v_ready"], 1)

        @block.scalar
        def _(act):
            norm.scalar(act, NT)
            act.wait_ge(s["loaded"], 96)
            for n, (side, c) in enumerate(items):
                if c % 2 == 0:
                    act.wait_ge(s["ready_a"], n // NCH * 2 + c // 2 + 1)
                    act.activation((qT, kT)[side][:, c * BANK:(c + 1) * BANK], ps[:, c * BANK:(c + 1) * BANK],
                                   ACT.Identity,
                                   bias=bqk[:, side:side + 1]).then_inc(s["stored_a"], 1)

        @block.vector
        def _(v):
            norm.vector(v, NT)
            v.wait_ge(s["loaded"], 96)
            v.tensor_tensor(S.x[:], S.x[:], S.hn[:], ALU.add).then_inc(s["res"], 1)
            v.wait_ge(s["res"], 1)
            v.tensor_tensor(S.x[:], S.x[:], bo[:].unsqueeze(1).to_broadcast([P, NT, D]), ALU.add).then_inc(s["res"], 1)
            for n, (side, c) in enumerate(items):
                if c % 2 == 1:
                    v.wait_ge(s["ready_v"], n // NCH * 2 + c // 2 + 1)
                    v.tensor_scalar((qT, kT)[side][:, c * BANK:(c + 1) * BANK], ps[:, c * BANK:(c + 1) * BANK],
                                    bqk[:, side:side + 1], None,
                                    ALU.add).then_inc(s["stored_v"], 1)
            for c in range(NCH):
                v.wait_ge(s["v_ready"], 4 * (c + 1))
                v.tensor_tensor(V[:, 4 * c:4 * c + 4, :],
                                ps[:, (4 + c) * BANK:(5 + c) * BANK].rearrange("p (t d) -> p t d", d=D),
                                bv[:].unsqueeze(1).to_broadcast([P, 4, D]), ALU.add).then_inc(s["v_stored"], 1)


def ge(eng, sem, value):
    if not (isinstance(value, int) and value <= 0):
        eng.wait_ge(sem, value)


def select_and_mix(nc, ctx, S, qT, kT, V, count):
    with ExitStack() as own:
        NT, T = S.NT, S.T
        NCH, NB = T // BANK, T // P
        SCALE = 1.0 / float(np.sqrt(DH))
        BODY = HEADS // 2
        N = NT * HEADS
        SEG = T // SEGS
        sb = lambda name, shape, dt=F32: own.enter_context(nc.sbuf_tensor("sm_" + name, shape, dt))
        qs = sb("qs", [P, 2, P])
        mask = S.headmask
        sc = sb("sc", [P, 4, T])
        ex = sb("ex", [P, 2, T])
        side = sb("side", [P, 2, T], mybir.dt.bfloat16)
        low = sb("low", [P, 2, T])
        pr = sb("pr", [P, 2, T])
        pT = sb("pT", [P, T])
        cand = sb("cand", [P, 2, SEGS * 8])
        tops = sb("tops", [P, 2, ROUNDS, 8])
        nmax = sb("nmax", [P, 4, 1])
        rank = sb("rank", [P, 2, 1])
        nextT = sb("nextT", [P, 2, 8])
        pick = sb("pick", [P, 2, 8])
        kth = sb("kth", [P, 2, 1])
        den = sb("den", [P, 4, 1])
        rden = sb("rden", [P, 2, 1])
        above = sb("above", [P, 4, 1])
        junk = sb("junk", [P, T], mybir.dt.bfloat16)
        iota8 = sb("iota8", [P, 8])
        attn = S.hT
        names = ("qs_ready s_ready sc_stored seg_done max_ready exp_done pivot_ready side_done low_done chain "
                 "rank_done next_done kth_done kept count_done turned pt_stored mixed rden_done attn_done gate iota").split()
        s = {n: ctx.enter_context(nc.semaphore("sm_" + n)) for n in names}
        ps = S.ps
        block = own.enter_context(nc.Block())

        def tile(it, j):
            return it * BODY + j, it // 2, (it % 2) * BODY + j

        def at(start, size):
            return slice(start, start + size) if isinstance(start, int) else bass.ds(start, size)

        def run(eng, step, first=0, last=0):
            for j in range(BODY):
                step(0, j)
            with eng.Fori(1, N // BODY - 1) as it:
                for j in range(BODY):
                    step(it, j)
            for j in range(BODY):
                step(N // BODY - 1, j)

        def before(it, j, k):
            if j >= k:
                return it, j - k
            if isinstance(it, int) and it == 0:
                return None
            return it - 1, j - k + BODY

        def after(it, j, k):
            if j + k < BODY:
                return it, j + k
            if isinstance(it, int) and it == N // BODY - 1:
                return None
            return it + 1, j + k - BODY

        @block.gpsimd
        def _(pool):
            nc.gpsimd.iota(iota8[:], pattern=[[1, 8]], base=0, channel_multiplier=0,
                           allow_small_or_imprecise_dtypes=True).then_inc(s["iota"], 1)

            def query(it, j):
                n, qt, h = tile(it, j)
                ge(pool, s["s_ready"], n - 1)
                nc.gpsimd.tensor_tensor(qs[:, j % 2, :], qT[:, at(qt * P, P)],
                                        mask[:, at(h, 1)].to_broadcast([P, P]), ALU.mult).then_inc(s["qs_ready"], 1)

            def step(it, j):
                n = tile(it, j)[0]
                nxt = after(it, j, 3)
                if nxt:
                    query(*nxt)
                pool.wait_ge(s["side_done"], n + 1)
                pool.wait_ge(s["exp_done"], n + 1)
                ge(pool, s["next_done"], n - 1)
                nc.gpsimd.tensor_tensor(low[:, j % 2, :], ex[:, j % 2, :], side[:, j % 2, :],
                                        ALU.mult).then_inc(s["low_done"], 1)

            for j in range(3):
                query(0, j)
            run(pool, step)

        @block.tensor
        def _(pe):
            def scores(it, j):
                n = tile(it, j)[0]
                pe.wait_ge(s["qs_ready"], n + 1)
                ge(pe, s["sc_stored"], n)
                for c in range(NCH):
                    ins = pe.matmul(ps[:, c * BANK:(c + 1) * BANK], qs[:, j % 2, :], kT[:, c * BANK:(c + 1) * BANK],
                                    start=True, stop=True)
                ins.then_inc(s["s_ready"], 1)

            def mix(it, j):
                n, qt, h = tile(it, j)
                pe.wait_ge(s["kept"], n + 1)
                for b in range(NCH):
                    ge(pe, s["pt_stored"], n * NCH + b - 1)
                    for k in range(4):
                        kb = b * 4 + k
                        ins = pe.transpose(ps[:, (4 + b % 2) * BANK + k * P:(4 + b % 2) * BANK + (k + 1) * P],
                                           pr[:, j % 2, kb * P:(kb + 1) * P], S.ident[:])
                    ins.then_inc(s["turned"], 1)
                pe.wait_ge(s["pt_stored"], n * NCH + NCH)
                ge(pe, s["attn_done"], n - 1)
                for kb in range(NB):
                    ins = pe.matmul(ps[:, (6 + j % 2) * BANK:(6 + j % 2) * BANK + DH], pT[:, kb * P:(kb + 1) * P],
                                    V[:, kb, at(h * DH, DH)], start=(kb == 0), stop=(kb == NB - 1))
                ins.then_inc(s["mixed"], 1)

            scores(0, 0)
            scores(0, 1)

            def step(it, j):
                nxt, old = after(it, j, 2), before(it, j, 2)
                if nxt:
                    scores(*nxt)
                if old:
                    mix(*old)

            run(pe, step)
            mix(N // BODY - 1, BODY - 2)
            mix(N // BODY - 1, BODY - 1)

        @block.scalar
        def _(act):
            def copy_scores(it, j):
                n = tile(it, j)[0]
                act.wait_ge(s["s_ready"], n + 1)
                ge(act, s["side_done"], n - 3)
                act.copy(sc[:, j % 4, :], ps[:, 0:T]).then_inc(s["sc_stored"], 1)

            def exps(it, j):
                n = tile(it, j)[0]
                act.wait_ge(s["max_ready"], n + 1)
                ge(act, s["kept"], n - 1)
                act.activation(ex[:, j % 2, :], sc[:, j % 4, :], ACT.Exp, scale=SCALE,
                               bias=nmax[:, j % 4, :]).then_inc(s["exp_done"], 1)

            def signs(it, j):
                n = tile(it, j)[0]
                act.wait_ge(s["pivot_ready"], n + 1)
                ge(act, s["low_done"], n - 1)
                act.activation(side[:, j % 2, :], sc[:, j % 4, :], ACT.Sign, scale=-1.0,
                               bias=tops[:, j % 2, ROUNDS - 1, 7:8],
                               accum_out=above[:, j % 4, :]).then_inc(s["side_done"], 1)

            def count_kept(it, j):
                n = tile(it, j)[0]
                act.wait_ge(s["kept"], n + 1)
                ge(act, s["count_done"], n)
                act.sem_inc(s["gate"], 1)
                act.activation(junk[:], pr[:, j % 2, :], ACT.Sign, accum_out=count[:, at(n, 1)]).then_inc(s["count_done"], 1)

            def move_turned(it, j):
                n = tile(it, j)[0]
                ge(act, s["mixed"], n)
                for b in range(NCH):
                    act.wait_ge(s["turned"], n * NCH + b + 1)
                    act.copy(pT[:, b * BANK:(b + 1) * BANK],
                             ps[:, (4 + b % 2) * BANK:(5 + b % 2) * BANK]).then_inc(s["pt_stored"], 1)

            copy_scores(0, 0)
            copy_scores(0, 1)

            def step(it, j):
                nxt, old = after(it, j, 2), before(it, j, 2)
                if old:
                    count_kept(*old)
                exps(it, j)
                if nxt:
                    copy_scores(*nxt)
                if old:
                    move_turned(*old)
                signs(it, j)

            run(act, step)
            for j in (BODY - 2, BODY - 1):
                count_kept(N // BODY - 1, j)
                move_turned(N // BODY - 1, j)

        @block.vector
        def _(v):
            def seg_max(j, k):
                return v.max(cand[:, j % 2, k * 8:(k + 1) * 8], sc[:, j % 4, k:T:SEGS])

            def select(it, j):
                n = tile(it, j)[0]
                nxt = after(it, j, 1)
                if nxt:
                    v.wait_ge(s["sc_stored"], n + 2)
                    v.sem_inc(s["gate"], 1)
                c, todo = cand[:, j % 2, :], list(range(SEGS)) if nxt else []
                base = 2 * ROUNDS * j
                for r in range(ROUNDS):
                    top = tops[:, j % 2, r, :]
                    v.max(top, c).then_inc(s["chain"], 1)
                    if todo:
                        ins = seg_max(nxt[1], todo.pop(0))
                    v.wait_ge(s["chain"], base + 2 * r + 1)
                    if r == 0:
                        v.tensor_scalar(nmax[:, j % 4, :], tops[:, j % 2, 0, 0:1], -SCALE, None,
                                        ALU.mult).then_inc(s["max_ready"], 1)
                    if r < ROUNDS - 1:
                        v.match_replace(c, top, c, LOWEST).then_inc(s["chain"], 1)
                    else:
                        v.sem_inc(s["chain"], 1)
                        v.sem_inc(s["pivot_ready"], 1)
                    if todo:
                        ins = seg_max(nxt[1], todo.pop(0))
                    if r < ROUNDS - 1:
                        v.wait_ge(s["chain"], base + 2 * r + 2)
                while todo:
                    ins = seg_max(nxt[1], todo.pop(0))
                if nxt:
                    ins.then_inc(s["seg_done"], 1)

            def keep(it, j):
                n = tile(it, j)[0]
                v.wait_ge(s["side_done"], n + 1)
                v.tensor_scalar(rank[:, j % 2, :], above[:, j % 4, :], 0.5, TOPK - 1 - (T + 1) / 2.0, ALU.mult,
                                ALU.add).then_inc(s["rank_done"], 1)
                v.wait_ge(s["low_done"], n + 1)
                v.sem_inc(s["gate"], 1)
                v.max(nextT[:, j % 2, :], low[:, j % 2, :]).then_inc(s["next_done"], 1)
                v.wait_ge(s["next_done"], n + 1)
                v.scalar_tensor_tensor(pick[:, j % 2, :], iota8[:], rank[:, j % 2, :], nextT[:, j % 2, :],
                                       ALU.is_equal, ALU.mult, accum_out=kth[:, j % 2, :]).then_inc(s["kth_done"], 1)
                v.wait_ge(s["kth_done"], n + 1)
                ge(v, s["turned"], (n - 1) * NCH)
                ge(v, s["count_done"], n - 1)
                v.scalar_tensor_tensor(pr[:, j % 2, :], ex[:, j % 2, :], kth[:, j % 2, :], ex[:, j % 2, :],
                                       ALU.is_ge, ALU.mult, accum_out=den[:, j % 4, :]).then_inc(s["kept"], 1)

            def finish(it, j):
                n, qt, h = tile(it, j)
                v.reciprocal(rden[:, j % 2, :], den[:, j % 4, :]).then_inc(s["rden_done"], 1)
                v.wait_ge(s["rden_done"], n + 1)
                v.wait_ge(s["mixed"], n + 1)
                v.sem_inc(s["gate"], 1)
                v.tensor_scalar(attn[:, at(qt * D + h * DH, DH)], ps[:, (6 + j % 2) * BANK:(6 + j % 2) * BANK + DH],
                                rden[:, j % 2, :], None, ALU.mult).then_inc(s["attn_done"], 1)

            v.wait_ge(s["iota"], 1)
            v.wait_ge(s["sc_stored"], 1)
            for k in range(SEGS):
                ins = seg_max(0, k)
            ins.then_inc(s["seg_done"], 1)

            def step(it, j):
                if j == 0 :
                    v.sem_clear(s["chain"])
                n = tile(it, j)[0]
                v.wait_ge(s["seg_done"], n + 1)
                v.sem_inc(s["gate"], 1)
                select(it, j)
                old = before(it, j, 1)
                if old:
                    keep(*old)
                old = before(it, j, 3)
                if old:
                    finish(*old)

            run(v, step)
            last = N // BODY - 1
            keep(last, BODY - 1)
            for j in (BODY - 3, BODY - 2, BODY - 1):
                finish(last, j)


def redo(nc, ctx, S, qT, kT, V, count):
    with ExitStack() as own:
        NT, T = S.NT, S.T
        NCH, NB = T // BANK, T // P
        N = NT * HEADS
        HALVES = N // P
        SCALE = 1.0 / float(np.sqrt(DH))
        I32 = mybir.dt.int32
        sb = lambda name, shape, dt=F32: own.enter_context(nc.sbuf_tensor("re_" + name, shape, dt))
        bad = sb("bad", [P, N])
        flag = sb("flag", [P, HALVES])
        row = sb("row", [1, 2, N])
        per = sb("per", [1, NT])
        flag_i = sb("flag_i", [1, N], I32)
        order_i = sb("order_i", [1, N], I32)
        per_i = sb("per_i", [1, NT], I32)
        qs = sb("qs", [P, P])
        sc = sb("sc", [P, T])
        rest = sb("rest", [P, T])
        ex = sb("ex", [P, T])
        pr = sb("pr", [P, T])
        pT = sb("pT", [P, T])
        tops = sb("tops", [P, TOPK // 8, 8])
        nmax = sb("nmax", [P, 1])
        den = sb("den", [P, 1])
        rden = sb("rden", [P, 1])
        names = ("bad_done flag_sum flag_done rows_ready rows_done ints_done redone qs_ready s_ready sc_stored chain "
                 "max_ready exp_done kept turned pt_stored mixed rden_done gate").split()
        s = {n: ctx.enter_context(nc.semaphore("re_" + n)) for n in names}
        ps = S.ps
        block = own.enter_context(nc.Block())

        def each_flagged(eng, body):
            eng.wait_ge(s["ints_done"], 4)
            with eng.Fori(0, NT) as qt:
                with eng.If(eng.value_load(per_i[0:1, bass.ds(qt, 1)], min_val=0, max_val=HEADS) > 0):
                    with eng.Fori(0, HEADS) as h:
                        n = qt * HEADS + h
                        with eng.If(eng.value_load(flag_i[0:1, bass.ds(n, 1)], min_val=0, max_val=1) > 0):
                            k = eng.value_load(order_i[0:1, bass.ds(n, 1)], min_val=0, max_val=N - 1)
                            eng.wait_ge(s["redone"], k + 1)
                            eng.sem_inc(s["gate"], 1)
                            body(qt, h, k)

        @block.gpsimd
        def _(pool):
            def body(qt, h, k):
                nc.gpsimd.tensor_tensor(qs[:], qT[:, bass.ds(qt * P, P)],
                                        S.headmask[:, bass.ds(h, 1)].to_broadcast([P, P]),
                                        ALU.mult).then_inc(s["qs_ready"], 1)

            each_flagged(pool, body)

        @block.tensor
        def _(pe):
            pe.wait_ge(s["bad_done"], 1)
            for i in range(HALVES):
                ins = pe.matmul(ps[:, i:i + 1], bad[:, i * P:(i + 1) * P], S.ones[:, 0:1], start=True, stop=True)
            ins.then_inc(s["flag_sum"], 1)
            pe.wait_ge(s["flag_done"], 1)
            for i in range(HALVES):
                pe.matmul(ps[0:1, BANK + i * P:BANK + (i + 1) * P], flag[:, i:i + 1], S.ident[:], start=True, stop=True)
                for k in range(i + 1):
                    ins = pe.matmul(ps[0:1, 2 * BANK + i * P:2 * BANK + (i + 1) * P], flag[:, k:k + 1],
                                    S.upper[:] if k == i else S.ones[:], start=(k == 0), stop=(k == i))
            ins.then_inc(s["rows_ready"], 1)

            def body(qt, h, k):
                pe.wait_ge(s["qs_ready"], k + 1)
                for c in range(NCH):
                    ins = pe.matmul(ps[:, c * BANK:(c + 1) * BANK], qs[:], kT[:, c * BANK:(c + 1) * BANK],
                                    start=True, stop=True)
                ins.then_inc(s["s_ready"], 1)
                pe.wait_ge(s["kept"], k + 1)
                for b in range(NB):
                    ins = pe.transpose(ps[:, b * P:(b + 1) * P], pr[:, b * P:(b + 1) * P], S.ident[:])
                ins.then_inc(s["turned"], 1)
                pe.wait_ge(s["pt_stored"], k + 1)
                for b in range(NB):
                    ins = pe.matmul(ps[:, 6 * BANK:6 * BANK + DH], pT[:, b * P:(b + 1) * P],
                                    V[:, b, bass.ds(h * DH, DH)], start=(b == 0), stop=(b == NB - 1))
                ins.then_inc(s["mixed"], 1)

            each_flagged(pe, body)

        @block.scalar
        def _(act):
            def body(qt, h, k):
                act.wait_ge(s["s_ready"], k + 1)
                act.copy(sc[:], ps[:, 0:T]).then_inc(s["sc_stored"], 1)
                act.wait_ge(s["max_ready"], k + 1)
                act.activation(ex[:], sc[:], ACT.Exp, scale=SCALE, bias=nmax[:]).then_inc(s["exp_done"], 1)
                act.wait_ge(s["turned"], k + 1)
                act.copy(pT[:], ps[:, 0:T]).then_inc(s["pt_stored"], 1)

            each_flagged(act, body)

        @block.vector
        def _(v):
            v.tensor_scalar(bad[:], count[:], float(TOPK), None, ALU.not_equal).then_inc(s["bad_done"], 1)
            v.wait_ge(s["flag_sum"], 1)
            v.tensor_scalar(flag[:], ps[:, 0:HALVES], 1.0, None, ALU.min).then_inc(s["flag_done"], 1)
            v.wait_ge(s["rows_ready"], 1)
            v.tensor_copy(row[:, 0, :], ps[0:1, BANK:BANK + N])
            v.tensor_copy(row[:, 1, :], ps[0:1, 2 * BANK:2 * BANK + N]).then_inc(s["rows_done"], 1)
            v.wait_ge(s["rows_done"], 1)
            v.tensor_reduce(per[:], row[:, 0, :].rearrange("o (q h) -> o q h", h=HEADS), AX.X,
                            ALU.add).then_inc(s["ints_done"], 1)
            v.tensor_copy(flag_i[:], row[:, 0, :]).then_inc(s["ints_done"], 1)
            v.tensor_tensor(order_i[:], row[:, 1, :], row[:, 0, :], ALU.subtract).then_inc(s["ints_done"], 1)
            v.wait_ge(s["ints_done"], 3)
            v.sem_inc(s["redone"], 1)
            v.tensor_copy(per_i[:], per[:]).then_inc(s["ints_done"], 1)

            def body(qt, h, k):
                v.sem_clear(s["chain"])
                v.wait_ge(s["sc_stored"], k + 1)
                v.sem_inc(s["gate"], 1)
                for r in range(TOPK // 8):
                    v.max(tops[:, r, :], (sc if r == 0 else rest)[:]).then_inc(s["chain"], 1)
                    v.wait_ge(s["chain"], 2 * r + 1)
                    v.match_replace(rest[:], tops[:, r, :], (sc if r == 0 else rest)[:], LOWEST).then_inc(s["chain"], 1)
                    v.wait_ge(s["chain"], 2 * r + 2)
                v.tensor_scalar(nmax[:], tops[:, 0, 0:1], -SCALE, None, ALU.mult).then_inc(s["max_ready"], 1)
                v.wait_ge(s["exp_done"], k + 1)
                v.scalar_tensor_tensor(pr[:], rest[:], LOWEST, ex[:], ALU.is_le, ALU.mult,
                                       accum_out=den[:]).then_inc(s["kept"], 1)
                v.wait_ge(s["kept"], k + 1)
                v.reciprocal(rden[:], den[:]).then_inc(s["rden_done"], 1)
                v.wait_ge(s["rden_done"], k + 1)
                v.wait_ge(s["mixed"], k + 1)
                v.sem_inc(s["gate"], 1)
                v.tensor_scalar(S.hT[:, bass.ds(qt * D + h * DH, DH)], ps[:, 6 * BANK:6 * BANK + DH], rden[:], None,
                                ALU.mult).then_inc(s["redone"], 1)

            each_flagged(v, body)


def project_out(nc, ctx, S, A, wo):
    with ExitStack() as own:
        NT, T = S.NT, S.T
        s = {n: ctx.enter_context(nc.semaphore("po_" + n)) for n in "turned stored ready added".split()}
        aT = own.enter_context(nc.sbuf_tensor("po_aT", [P, T], F32))
        ps = S.ps
        block = own.enter_context(nc.Block())

        @block.tensor
        def _(pe):
            for t in range(NT):
                pe.transpose(ps[:, t * P:(t + 1) * P], S.hT[:, t * P:(t + 1) * P], S.ident[:]).then_inc(s["turned"], 1)
            for t in range(NT):
                if t % 4 == 0:
                    pe.wait_ge(s["stored"], t // 4 + 1)
                pe.matmul(ps[:, 4 * BANK + t * D:4 * BANK + (t + 1) * D], aT[:, t * P:(t + 1) * P], wo[:], start=True,
                          stop=True).then_inc(s["ready"], 1)

        @block.scalar
        def _(act):
            for b in range(4):
                act.wait_ge(s["turned"], 4 * (b + 1))
                act.copy(aT[:, b * BANK:(b + 1) * BANK], ps[:, b * BANK:(b + 1) * BANK]).then_inc(s["stored"], 1)

        @block.vector
        def _(v):
            for b in range(4):
                v.wait_ge(s["ready"], 4 * (b + 1))
                v.tensor_tensor(S.x[:, 4 * b:4 * b + 4, :], S.x[:, 4 * b:4 * b + 4, :],
                                ps[:, (4 + b) * BANK:(5 + b) * BANK].rearrange("p (t d) -> p t d", d=D),
                                ALU.add).then_inc(s["added"], 1)
            v.wait_ge(s["added"], 4)


class Shared:
    pass


def program(nc, ins, out, stages):
    S, A = Shared(), ins
    S.T = A["u"].shape[0]
    S.NT = S.T // P
    with ExitStack() as ctx:
        sb = lambda name, shape: ctx.enter_context(nc.sbuf_tensor(name, shape, F32))
        S.x = sb("x", [P, S.NT, D])
        S.hn = sb("hn", [P, S.NT, D])
        S.hT = sb("hT", [P, S.T])
        S.st = sb("st", [P, S.NT, 6])
        S.sm = sb("sm", [P, 8, S.NT])
        S.ps = ctx.enter_context(nc.psum_tensor("ps", [P, 8 * BANK], F32))
        S.x_loaded = ctx.enter_context(nc.semaphore("x_loaded"))
        S.m_loaded = ctx.enter_context(nc.semaphore("m_loaded"))
        constants(nc, ctx, S)
        mamba(nc, ctx, S, A)
        moe_sems, moe_norm = moe_semaphores(nc, ctx), Norm(nc, ctx, "moe_ln", S)
        if stages >= 2:
            moe(nc, S, A, "moe_a", moe_sems, moe_norm)
        if stages >= 3:
            attention(nc, ctx, S, A)
        if stages >= 4:
            clear(nc, list(moe_sems.values()) + moe_norm.all())
            moe(nc, S, A, "moe_b", moe_sems, moe_norm, out)
        else:
            write_out(nc, ctx, S, out)


def clear(nc, sems):
    with nc.Block() as block:

        @block.gpsimd
        def _(pool):
            for sem in sems:
                pool.sem_clear(sem)


def write_out(nc, ctx, S, out):
    stored = ctx.enter_context(nc.semaphore("stored"))
    with nc.Block() as block:

        @block.sync
        def _(sp):
            sp.dma_start(out.rearrange("(t p) d -> p t d", p=P), S.x[:]).then_inc(stored, 16)
            sp.wait_ge(stored, 16)





def kernel(**inputs):
    import numpy as _np
    import concourse.bacc as _bacc
    from concourse import mybir as _mybir
    from concourse.bass_utils import run_bass_kernel_spmd as _run

    i = {k: _np.asarray(v) for k, v in inputs.items()}
    u = i["L0_attn_a_u"]

    qkv = i["L0_attn_b_w_qkv_w"].reshape(HEADS, 3, DH, D).transpose(3, 1, 0, 2).reshape(D, 3, HEADS * DH)
    bias = i["L0_attn_b_w_qkv_b"].reshape(HEADS, 3, DH).transpose(0, 2, 1).reshape(HEADS * DH, 3)
    arrays = {
        "u": u.reshape(-1, D),
        "w_in": i["L0_attn_a_W_in"].T,
        "conv_w": i["L0_attn_a_conv_w"],
        "conv_b": i["L0_attn_a_conv_b"].reshape(-1, P).T,
        "dt_bias": i["L0_attn_a_dt_bias"],
        "a_log": i["L0_attn_a_A_log"],
        "dskip": i["L0_attn_a_D"],
        "norm_w": i["L0_attn_a_norm_w"].reshape(-1, P).T,
        "w_mo": i["L0_attn_a_W_out"].T,
        "wqk": qkv[:, :2],
        "bqk": bias[:, :2],
        "wv": qkv[:, 2],
        "bv": bias[:, 2],
        "w_o": i["L0_attn_b_w_out_w"].T,
        "b_o": i["L0_attn_b_w_out_b"],
        "gate_w": i["L0_ffn_gate_w"],
        "gate_b": i["L0_ffn_gate_b"],
        "w1": i["L0_ffn_w1"],
        "b1T": i["L0_ffn_b1"].reshape(-1, P).T,
        "w2": i["L0_ffn_w2"],
        "b2": i["L0_ffn_b2"],
    }
    arrays = {k: _np.ascontiguousarray(a) for k, a in arrays.items()}
    nc = _bacc.Bacc("TRN2", target_bir_lowering=False, num_devices=1)
    aps = {k: nc.dram_tensor(f"in_{k}", a.shape, _mybir.dt.from_np(a.dtype), kind="ExternalInput").ap()
           for k, a in arrays.items()}
    out = nc.dram_tensor("out_x", (u.shape[1], D), _mybir.dt.float32, kind="ExternalOutput").ap()
    program(nc, aps, out, STAGES)
    r = _run(nc, [{f"in_{k}": a for k, a in arrays.items()}], core_ids=[0])
    return r.results[0]["out_x"].reshape(u.shape)
STAGES = 4
```

```python
from contextlib import ExitStack

import numpy as np

import concourse.bass as bass
from concourse import mybir

ALU = mybir.AluOpType
ACT = mybir.ActivationFunctionType
AX = mybir.AxisListType
F32 = mybir.dt.float32
BF16 = mybir.dt.bfloat16

P = 128
D = 128
BANK = 512
EPS = 1e-5
BIG = 1e30


HEADS, DH = 16, 8


class Chain:

    def __init__(self, eng, sem):
        self.eng, self.sem, self.n = eng, sem, 0

    def __call__(self, ins):
        self.n += 1
        ins.then_inc(self.sem, 1)
        self.eng.wait_ge(self.sem, self.n)


def constants(nc, ctx, S):
    sb = lambda name, shape: ctx.enter_context(nc.sbuf_tensor(name, shape, F32))
    S.ident = sb("ident", [P, P])
    S.upper = sb("upper", [P, P])
    S.cap = sb("cap", [P, P])
    S.ones = sb("ones", [P, P])
    S.headmask = sb("headmask", [P, HEADS])
    filled = ctx.enter_context(nc.semaphore("const_filled"))
    built = ctx.enter_context(nc.semaphore("const_built"))
    with nc.Block() as block:

        @block.gpsimd
        def _(pool):
            nc.gpsimd.memset(S.ident[:], 0.0)
            nc.gpsimd.memset(S.upper[:], 1.0)
            nc.gpsimd.memset(S.cap[:], 0.0)
            nc.gpsimd.memset(S.ones[:], 1.0).then_inc(filled, 1)
            pool.wait_ge(filled, 1)
            nc.gpsimd.affine_select(out=S.ident[:], in_=S.ident[:], compare_op=ALU.not_equal, fill=1.0,
                                    base=0, pattern=[[-1, P]], channel_multiplier=1)
            nc.gpsimd.affine_select(out=S.upper[:], in_=S.upper[:], compare_op=ALU.is_ge, fill=0.0,
                                    base=0, pattern=[[1, P]], channel_multiplier=-1)
            nc.gpsimd.affine_select(out=S.cap[:], in_=S.cap[:], compare_op=ALU.is_ge, fill=-BIG,
                                    base=0, pattern=[[1, P]], channel_multiplier=-1).then_inc(built, 1)
            pool.wait_ge(built, 1)
            nc.gpsimd.memset(S.headmask[:], 1.0).then_inc(built, 1)
            pool.wait_ge(built, 2)
            nc.gpsimd.affine_select(out=S.headmask[:], in_=S.headmask[:], compare_op=ALU.is_ge, fill=0.0, base=0,
                                    pattern=[[-DH, HEADS]], channel_multiplier=1).then_inc(built, 1)
            pool.wait_ge(built, 3)
            nc.gpsimd.affine_select(out=S.headmask[:], in_=S.headmask[:], compare_op=ALU.is_ge, fill=0.0, base=DH - 1,
                                    pattern=[[DH, HEADS]], channel_multiplier=-1).then_inc(built, 1)
            pool.wait_ge(built, 4)


class Norm:

    def __init__(self, nc, ctx, tag, S):
        sem = lambda n: ctx.enter_context(nc.semaphore(f"{tag}_{n}"))
        self.S = S
        self.stats_done, self.chain, self.var_ready = sem("stats_done"), sem("stat_chain"), sem("var_ready")
        self.sqrt_done, self.normed = sem("sqrt_done"), sem("normed")
        self.turned, self.stored = sem("turned"), sem("hT_stored")

    def all(self):
        return [self.stats_done, self.chain, self.var_ready, self.sqrt_done, self.normed, self.turned, self.stored]

    def vector(self, v, NT):
        S = self.S
        with v.Fori(0, NT) as t:
            v.bn_stats(S.st[:, t, :], S.x[:, t, :]).then_inc(self.stats_done, 1)
        v.wait_ge(self.stats_done, NT)
        me, mo = S.st[:, :, 1], S.st[:, :, 4]
        qe, qo = S.st[:, :, 2], S.st[:, :, 5]
        a = lambda k: S.sm[:, k, 0:NT]
        step = Chain(v, self.chain)
        v.tensor_tensor(a(0), me, mo, ALU.add)
        v.tensor_tensor(a(1), me, mo, ALU.subtract)
        step(v.tensor_tensor(a(2), qe, qo, ALU.add))
        v.tensor_scalar(a(3), a(0), 0.5, None, ALU.mult)
        v.tensor_tensor(a(4), a(1), a(1), ALU.mult)
        step(v.tensor_scalar(a(5), a(2), 1.0 / D, EPS, ALU.mult, ALU.add))
        v.scalar_tensor_tensor(a(6), a(4), 0.25, a(5), ALU.mult, ALU.add).then_inc(self.var_ready, 1)
        v.wait_ge(self.sqrt_done, 1)
        step(v.reciprocal(a(0), a(7)))
        with v.Fori(0, NT) as t:
            v.tensor_scalar(S.hn[:, t, :], S.x[:, t, :], S.sm[:, 3, bass.ds(t, 1)], S.sm[:, 0, bass.ds(t, 1)],
                            ALU.subtract, ALU.mult).then_inc(self.normed, 1)
        for b in (1, 3):
            v.wait_ge(self.turned, 4 * (b + 1))
            v.tensor_copy(S.hT[:, b * BANK:(b + 1) * BANK], S.ps[:, b * BANK:(b + 1) * BANK]).then_inc(self.stored, 1)

    def scalar(self, act, NT):
        S = self.S
        act.wait_ge(self.var_ready, 1)
        act.activation(S.sm[:, 7, 0:NT], S.sm[:, 6, 0:NT], ACT.Sqrt).then_inc(self.sqrt_done, 1)
        for b in (0, 2):
            act.wait_ge(self.turned, 4 * (b + 1))
            act.copy(S.hT[:, b * BANK:(b + 1) * BANK], S.ps[:, b * BANK:(b + 1) * BANK]).then_inc(self.stored, 1)

    def tensor(self, pe, NT):
        S = self.S
        for t in range(NT):
            pe.wait_ge(self.normed, t + 1)
            pe.transpose(S.ps[:, bass.ds(t * P, P)], S.hn[:, t, :], S.ident[:]).then_inc(self.turned, 1)
        pe.wait_ge(self.stored, NT * P // BANK)


def mamba(nc, ctx, S, A):
    with ExitStack() as own:
        sb = lambda name, shape: own.enter_context(nc.sbuf_tensor(name, shape, F32))
        sem = lambda name: ctx.enter_context(nc.semaphore("m_" + name))
        NT, T, H, G = S.NT, S.T, 2, 4
        w_in = sb("w_in", [P, A["w_in"].shape[1]])
        w_mo = sb("w_mo", [P, H, D])
        convw = sb("convw", [P, G, 4])
        vecs = sb("vecs", [P, G + H])
        rows = sb("rows", [P, 3, H])
        xp = sb("xp", [P, G, 3 + T])
        xc = sb("xc", [P, G, T])
        z = sb("z", [P, NT, H * P])
        y = sb("y", [P, NT, H * P])
        dtr = sb("dtr", [P, 6, NT * H])
        negA = sb("negA", [P, H])
        diagD = sb("diagD", [P, H, P])
        state = sb("state", [P, 2, H, P])
        xt = sb("xt", [P, 2, 3 * P])
        uda = sb("uda", [P, 2, H, P])
        arg = sb("arg", [P, 2, H, P])
        el = sb("el", [P, 2, H, P])
        ec = sb("ec", [P, 2, H, P])
        cd = sb("cd", [P, 2, H, P])
        mt = sb("mt", [P, 2, H, P])
        bw = sb("bw", [P, 2, H, P])
        sq = sb("sq", [P, H * P])
        ygT = sb("ygT", [P, 2, H, P])
        norm = Norm(nc, ctx, "ln0", S)
        loaded = S.m_loaded
        names = ("xin_ready xin_stored z_ready z_stored dt_ready dt_stored dt_chain pad_zero conv_step act_chain silu_done "
                 "cs_ready cs_stored dec_done wdt_done uda_done csb_ready ec_done arg_done exp_done turned xt_stored g_ready "
                 "mix_done y_ready y_done ds_ready state_done yn_chain ssq_done rms_sqrt yn_done ygt_ready ygt_stored "
                 "o_ready res_done diag_done sumsq const_done").split()
        s = {n: sem(n) for n in names}
        ps = S.ps
        block = own.enter_context(nc.Block())

        @block.sync
        def _(sp):
            sp.dma_start(S.x[:], A["u"].rearrange("(t p) d -> p t d", p=P)).then_inc(S.x_loaded, 16)
            sp.dma_start(w_in[:], A["w_in"]).then_inc(loaded, 16)
            sp.dma_start(convw[:], A["conv_w"].rearrange("(g p) k -> p g k", p=P)).then_inc(loaded, 16)
            sp.dma_start(vecs[:, 0:G], A["conv_b"]).then_inc(loaded, 16)
            sp.dma_start(vecs[:, G:G + H], A["norm_w"]).then_inc(loaded, 16)
            sp.dma_start(w_mo[:], A["w_mo"].rearrange("(h p) o -> p h o", p=P)).then_inc(loaded, 16)
            for k, vec in enumerate((A["dt_bias"], A["a_log"], A["dskip"])):
                sp.dma_start(rows[:, k, :], vec.partition_broadcast(P)).then_inc(loaded, 16)

        @block.tensor
        def _(pe):
            norm.tensor(pe, NT)
            pe.wait_ge(loaded, 16 * 8)
            for n in range(G * 4):
                g, c = n // 4, n % 4
                if n >= 4:
                    pe.wait_ge(s["xin_stored"], n - 3)
                pe.matmul(ps[:, (4 + n % 4) * BANK:(5 + n % 4) * BANK], w_in[:, H * P + g * P:H * P + (g + 1) * P],
                          S.hT[:, c * BANK:(c + 1) * BANK], start=True, stop=True).then_inc(s["xin_ready"], 1)
            for t in range(NT):
                pe.matmul(ps[:, bass.ds(t * H, H)], S.hT[:, bass.ds(t * P, P)], w_in[:, 6 * P:6 * P + H],
                          start=True, stop=True).then_inc(s["dt_ready"], 1)
            for i in range(NT // 2):
                for u in range(2):
                    if i >= 1:
                        pe.wait_ge(s["z_stored"], i * 2 - 1 + u)
                    pe.matmul(ps[:, (2 + u) * BANK:(2 + u) * BANK + H * P], S.hT[:, bass.ds(i * 2 * P + u * P, P)],
                              w_in[:, 0:H * P], start=True, stop=True).then_inc(s["z_ready"], 1)
            pe.wait_ge(s["dt_stored"], 1)
            pe.matmul(ps[:, BANK:BANK + NT * H], S.upper[:], dtr[:, 1, :], start=True, stop=True)
            pe.matmul(ps[:, BANK + 64:BANK + 64 + NT * H], S.ones[:], dtr[:, 1, :], start=True,
                      stop=True).then_inc(s["cs_ready"], 1)
            pe.wait_ge(s["silu_done"], G + 1)
            pe.wait_ge(s["const_done"], 2)
            pe.wait_ge(s["cs_stored"], 1)

            def chunk(c, u):
                tk = bass.ds(c * P, P)
                for k in range(3):
                    ins = pe.transpose(ps[:, u * BANK + k * P:u * BANK + (k + 1) * P], xc[:, k, tk], S.ident[:])
                ins.then_inc(s["turned"], 1)
                pe.matmul(ps[:, (2 + u) * BANK:(2 + u) * BANK + P], xc[:, 2, tk], xc[:, 3, tk], start=True,
                          stop=True).then_inc(s["g_ready"], 1)
                pe.wait_ge(s["uda_done"], c + 1)
                pe.matmul(ps[:, (4 + u) * BANK:(4 + u) * BANK + H * P], S.ones[:],
                          uda[:, u, :, :].rearrange("p h l -> p (h l)"), start=True,
                          stop=True).then_inc(s["csb_ready"], 1)
                pe.wait_ge(s["xt_stored"], c + 1)
                pe.wait_ge(s["mix_done"], c + 1)
                for h in range(H):
                    Y = ps[:, 6 * BANK + h * P:6 * BANK + (h + 1) * P]
                    xh = xt[:, u, h * P:(h + 1) * P]
                    pe.matmul(Y, mt[:, u, h, :], xh, start=True, stop=False)
                    pe.matmul(Y, diagD[:, h, :], xh, start=False, stop=False)
                    ins = pe.matmul(Y, cd[:, u, h, :], state[:, u, h, :], start=False, stop=True)
                ins.then_inc(s["y_ready"], 1)
                for h in range(H):
                    ins = pe.matmul(ps[:, 7 * BANK + h * P:7 * BANK + (h + 1) * P], bw[:, u, h, :],
                                    xt[:, u, h * P:(h + 1) * P], start=True, stop=True)
                ins.then_inc(s["ds_ready"], 1)
                pe.wait_ge(s["y_done"], c + 1)
                pe.wait_ge(s["state_done"], c + 1)

            for i in range(NT // 2):
                for u in range(2):
                    chunk(i * 2 + u, u)

            for i in range(NT // 2):
                for u in range(2):
                    t = i * 2 + u
                    pe.wait_ge(s["yn_done"], t + 1)
                    for h in range(H):
                        ins = pe.transpose(ps[:, u * BANK + h * P:u * BANK + (h + 1) * P],
                                           y[:, t, h * P:(h + 1) * P], S.ident[:])
                    ins.then_inc(s["ygt_ready"], 1)
                    pe.wait_ge(s["ygt_stored"], t + 1)
                    for h in range(H):
                        ins = pe.matmul(ps[:, (2 + u) * BANK:(2 + u) * BANK + D], ygT[:, u, h, :], w_mo[:, h, :],
                                        start=(h == 0), stop=(h == H - 1))
                    ins.then_inc(s["o_ready"], 1)
                    pe.wait_ge(s["res_done"], t + 1)

        @block.scalar
        def _(act):
            norm.scalar(act, NT)
            for n in range(G * 4):
                g, c = n // 4, n % 4
                act.wait_ge(s["xin_ready"], n + 1)
                act.copy(xp[:, g, 3 + c * BANK:3 + (c + 1) * BANK],
                         ps[:, (4 + n % 4) * BANK:(5 + n % 4) * BANK]).then_inc(s["xin_stored"], 1)
            link = Chain(act, s["act_chain"])
            act.wait_ge(s["dt_chain"], 3)
            link(act.activation(dtr[:, 3, :], dtr[:, 2, :], ACT.Exp))
            act.activation(negA[:], rows[:, 1, :], ACT.Exp)
            act.activation(dtr[:, 4, :], dtr[:, 3, :], ACT.Ln, bias=1.0).then_inc(s["act_chain"], 1)
            with act.Fori(0, NT // 2) as i:
                for u in range(2):
                    act.wait_ge(s["z_ready"], i * 2 + u + 1)
                    act.activation(z[:, i * 2 + u, :], ps[:, (2 + u) * BANK:(2 + u) * BANK + H * P],
                                   ACT.Silu).then_inc(s["z_stored"], 1)
            for g in range(G):
                act.wait_ge(s["conv_step"], 4 * (g + 1))
                act.activation(xc[:, g, :], xp[:, g, 3:3 + T], ACT.Silu).then_inc(s["silu_done"], 1)
            act.wait_ge(s["cs_stored"], 1)
            act.activation(dtr[:, 4, :], dtr[:, 3, :], ACT.Exp)
            act.activation(dtr[:, 5, :], dtr[:, 5, :], ACT.Exp).then_inc(s["silu_done"], 1)

            def chunk(c, u):
                act.wait_ge(s["turned"], c + 1)
                act.copy(xt[:, u, :], ps[:, u * BANK:u * BANK + 3 * P]).then_inc(s["xt_stored"], 1)
                act.wait_ge(s["csb_ready"], c + 1)
                act.activation(ec[:, u, :, :].rearrange("p h l -> p (h l)"),
                               ps[:, (4 + u) * BANK:(4 + u) * BANK + H * P], ACT.Exp).then_inc(s["ec_done"], 1)
                act.wait_ge(s["arg_done"], c + 1)
                act.activation(el[:, u, :, :].rearrange("p h l -> p (h l)"),
                               arg[:, u, :, :].rearrange("p h l -> p (h l)"), ACT.Exp).then_inc(s["exp_done"], 1)

            with act.Fori(0, NT // 2) as i:
                for u in range(2):
                    chunk(i * 2 + u, u)
            act.wait_ge(s["ssq_done"], 1)
            act.activation(S.sm[:, 1, 0:NT], S.sm[:, 0, 0:NT], ACT.Sqrt).then_inc(s["rms_sqrt"], 1)
            with act.Fori(0, NT // 2) as i:
                for u in range(2):
                    act.wait_ge(s["ygt_ready"], i * 2 + u + 1)
                    for h in range(H):
                        ins = act.activation(ygT[:, u, h, :], ps[:, u * BANK + h * P:u * BANK + (h + 1) * P],
                                             ACT.Copy, scale=vecs[:, G + h:G + h + 1])
                    ins.then_inc(s["ygt_stored"], 1)

        @block.gpsimd
        def _(pool):
            nc.gpsimd.memset(xp[:, :, 0:3], 0.0).then_inc(s["pad_zero"], 1)
            nc.gpsimd.memset(state[:, 0, :, :], 0.0).then_inc(s["const_done"], 1)
            pool.wait_ge(loaded, 16 * 8)
            for h in range(H):
                ins = nc.gpsimd.tensor_scalar(diagD[:, h, :], S.ident[:], rows[:, 2, h:h + 1], None, ALU.mult)
            ins.then_inc(s["const_done"], 1)

        @block.vector
        def _(v):
            v.wait_ge(S.x_loaded, 16)
            norm.vector(v, NT)
            v.wait_ge(loaded, 16 * 8)
            v.wait_ge(s["pad_zero"], 1)
            step = Chain(v, s["dt_chain"])
            d = lambda k: dtr[:, k, :]
            dth = lambda k, h: dtr[:, k, :].rearrange("p (t h) -> p t h", h=H)[:, :, h]
            v.wait_ge(s["dt_ready"], NT)
            psd = ps[:, 0:NT * H].rearrange("p (t h) -> p t h", h=H)
            for h in range(H):
                ins = v.tensor_scalar(dth(0, h), psd[:, :, h], rows[:, 0, h:h + 1], None, ALU.add)
            step(ins)
            step(v.tensor_scalar(d(5), d(0), -1.0, None, ALU.mult))
            step(v.tensor_tensor(d(2), d(0), d(5), ALU.min))
            v.wait_ge(s["act_chain"], 2)
            step(v.tensor_scalar(d(1), d(0), 0.0, None, ALU.max))
            step(v.tensor_tensor(d(0), d(1), d(4), ALU.add))
            for h in range(H):
                ins = v.tensor_scalar(dth(1, h), dth(0, h), negA[:, h:h + 1], -1.0, ALU.mult, ALU.mult)
            ins.then_inc(s["dt_stored"], 1)
            for g in range(G):
                v.wait_ge(s["xin_stored"], 4 * (g + 1))
                link = g * 4
                v.tensor_scalar(xc[:, g, :], xp[:, g, 0:T], convw[:, g, 0:1], vecs[:, g:g + 1], ALU.mult,
                                ALU.add).then_inc(s["conv_step"], 1)
                v.wait_ge(s["conv_step"], link + 1)
                for k in (1, 2):
                    v.scalar_tensor_tensor(xc[:, g, :], xp[:, g, k:k + T], convw[:, g, k:k + 1], xc[:, g, :],
                                           ALU.mult, ALU.add).then_inc(s["conv_step"], 1)
                    v.wait_ge(s["conv_step"], link + 1 + k)
                v.scalar_tensor_tensor(xp[:, g, 3:3 + T], xp[:, g, 3:3 + T], convw[:, g, 3:4], xc[:, g, :],
                                       ALU.mult, ALU.add).then_inc(s["conv_step"], 1)
            v.wait_ge(s["cs_ready"], 1)
            v.tensor_copy(d(2), ps[:, BANK:BANK + NT * H])
            step(v.tensor_copy(d(5), ps[:, BANK + 64:BANK + 64 + NT * H]))
            v.tensor_tensor(d(3), d(5), d(2), ALU.subtract).then_inc(s["cs_stored"], 1)
            v.wait_ge(s["silu_done"], G + 1)
            step(v.tensor_tensor(d(4), d(4), d(0), ALU.mult))

            def chunk(c, u):
                col = lambda k, h: dtr[:, k, bass.ds(c * H + h, 1)]
                for h in range(H):
                    ins = v.tensor_scalar(uda[:, u, h, :], S.upper[:], col(1, h), None, ALU.mult)
                ins.then_inc(s["uda_done"], 1)
                v.wait_ge(s["ec_done"], c + 1)
                for h in range(H):
                    ins = v.scalar_tensor_tensor(arg[:, u, h, :], ps[:, (4 + u) * BANK + h * P:(4 + u) * BANK + (h + 1) * P],
                                                 col(2, h), S.cap[:], ALU.subtract, ALU.min)
                ins.then_inc(s["arg_done"], 1)
                v.wait_ge(s["xt_stored"], c + 1)
                for h in range(H):
                    v.tensor_scalar(bw[:, u, h, :], xt[:, u, 2 * P:3 * P], col(4, h), None, ALU.mult)
                v.wait_ge(s["exp_done"], c + 1)
                v.wait_ge(s["g_ready"], c + 1)
                for h in range(H):
                    v.tensor_tensor(cd[:, u, h, :], xc[:, 3, bass.ds(c * P, P)], ec[:, u, h, :], ALU.mult)
                    ins = v.scalar_tensor_tensor(mt[:, u, h, :], el[:, u, h, :], col(0, h),
                                                 ps[:, (2 + u) * BANK:(2 + u) * BANK + P], ALU.mult, ALU.mult)
                ins.then_inc(s["mix_done"], 1)
                v.wait_ge(s["y_ready"], c + 1)
                v.tensor_tensor(y[:, c, :], ps[:, 6 * BANK:6 * BANK + H * P], z[:, c, :],
                                ALU.mult).then_inc(s["y_done"], 1)
                v.wait_ge(s["ds_ready"], c + 1)
                for h in range(H):
                    ins = v.scalar_tensor_tensor(state[:, 1 - u, h, :], state[:, u, h, :], col(5, h),
                                                 ps[:, 7 * BANK + h * P:7 * BANK + (h + 1) * P], ALU.mult, ALU.add)
                ins.then_inc(s["state_done"], 1)
                v.wait_ge(s["state_done"], c + 1)

            v.wait_ge(s["const_done"], 2)
            with v.Fori(0, NT // 2) as i:
                for u in range(2):
                    chunk(i * 2 + u, u)
            v.wait_ge(s["y_done"], NT)
            with v.Fori(0, NT) as t:
                v.tensor_tensor(z[:, t, :], y[:, t, :], y[:, t, :], ALU.mult).then_inc(s["sumsq"], 1)
            v.wait_ge(s["sumsq"], NT)
            link = Chain(v, s["yn_chain"])
            link(v.tensor_reduce(S.sm[:, 2, 0:NT], z[:], AX.X, ALU.add))
            v.tensor_scalar(S.sm[:, 0, 0:NT], S.sm[:, 2, 0:NT], 1.0 / (H * P), EPS, ALU.mult,
                            ALU.add).then_inc(s["ssq_done"], 1)
            v.wait_ge(s["rms_sqrt"], 1)
            link(v.reciprocal(S.sm[:, 3, 0:NT], S.sm[:, 1, 0:NT]))
            with v.Fori(0, NT) as t:
                v.tensor_scalar(y[:, t, :], y[:, t, :], S.sm[:, 3, bass.ds(t, 1)], None,
                                ALU.mult).then_inc(s["yn_done"], 1)
            with v.Fori(0, NT // 2) as i:
                for u in range(2):
                    t = i * 2 + u
                    v.wait_ge(s["o_ready"], t + 1)
                    v.tensor_tensor(S.x[:, t, :], S.x[:, t, :], ps[:, (2 + u) * BANK:(2 + u) * BANK + D],
                                    ALU.add).then_inc(s["res_done"], 1)
            v.wait_ge(s["res_done"], NT)


def moe_semaphores(nc, ctx):
    sem = lambda n: ctx.enter_context(nc.semaphore("moe_" + n))
    names = ("loaded gate_ready gate_chain top_done top_diff exp_done comb_done combt_ready combt_stored "
             "bias_ready acc_init iota_done h_ready hid_ready y_ready y_added stored w_loaded "
             "w1_loaded_0 w1_loaded_1 w2_loaded_0 w2_loaded_1 gate").split()
    return {n: sem(n) for n in names}


def moe(nc, S, A, tag, s, norm, out=None):
    with ExitStack() as own:
        sb = lambda name, shape, dt=F32: own.enter_context(nc.sbuf_tensor(f"{tag}_{name}", shape, dt))
        NT, T, E, FB = S.NT, S.T, 8, 4
        NC = T // BANK
        w1 = sb("w1", [P, 2, FB * P])
        w2 = sb("w2", [P, 2, FB, D])
        b1 = sb("b1", [P, E * FB])
        b2 = sb("b2", [E, D])
        gw = sb("gw", [P, E])
        gb = sb("gb", [P, E])
        lg = sb("lg", [P, NT, E])
        m8 = sb("m8", [P, NT, E])
        i8 = sb("i8", [P, NT, E], mybir.dt.uint32)
        i8f = sb("i8f", [P, NT, E])
        iot = sb("iot", [P, NT, E])
        c1 = sb("c1", [P, NT, E])
        c2 = sb("c2", [P, NT, E])
        comb = sb("comb", [P, NT, E])
        combT = sb("combT", [E, T])
        hid = sb("hid", [P, 2, FB, BANK])
        ps = S.ps
        acc = S.x
        block = own.enter_context(nc.Block())

        @block.sync
        def _(sp):
            sp.dma_start(gw[:], A["gate_w"]).then_inc(s["loaded"], 16)
            sp.dma_start(gb[:], A["gate_b"].partition_broadcast(P)).then_inc(s["loaded"], 16)
            sp.dma_start(b2[:], A["b2"]).then_inc(s["loaded"], 16)
            sp.dma_start(b1[:], A["b1T"]).then_inc(s["w_loaded"], 16)


            def load_expert(e, u):
                sp.dma_start(w1[:, u, :], A["w1"][e, :, :]).then_inc(s[f"w1_loaded_{u}"], 16)
                sp.dma_start(w2[:, u, :, :], A["w2"][e, :, :].rearrange("(k f) d -> f k d", f=P)).then_inc(
                    s[f"w2_loaded_{u}"], 16)

            load_expert(0, 0)
            load_expert(1, 1)
            with sp.Fori(1, E // 2) as i:
                for u in range(2):
                    sp.wait_ge(s["y_ready"], (i * 2 + u - 1) * NC)
                    load_expert(i * 2 + u, u)
            if out is not None:
                sp.wait_ge(s["y_added"], 4 * NC * E + 1)
                sp.dma_start(out.rearrange("(t p) d -> p t d", p=P), S.x[:]).then_inc(s["stored"], 16)
                sp.wait_ge(s["stored"], 16)

        @block.gpsimd
        def _(pool):
            nc.gpsimd.iota(iot[:], pattern=[[0, NT], [1, E]], base=0, channel_multiplier=0,
                           allow_small_or_imprecise_dtypes=True).then_inc(s["iota_done"], 1)

        @block.tensor
        def _(pe):
            norm.tensor(pe, NT)
            pe.wait_ge(s["loaded"], 48)
            for t in range(NT):
                pe.matmul(ps[:, bass.ds(t * E, E)], S.hT[:, bass.ds(t * P, P)], gw[:], start=True,
                          stop=True).then_inc(s["gate_ready"], 1)


            def hidden(u, c, n):
                if n is not None:
                    pe.wait_ge(s["hid_ready"], n)
                for f in range(FB):
                    ins = pe.matmul(ps[:, f * BANK:(f + 1) * BANK], w1[:, u, f * P:(f + 1) * P],
                                    S.hT[:, c * BANK:(c + 1) * BANK], start=True, stop=True)
                ins.then_inc(s["h_ready"], 1)

            def down(u, c, n):
                pe.wait_ge(s["hid_ready"], n + 1)
                for k in range(4):
                    Y = ps[:, (6 + c % 2) * BANK + k * P:(6 + c % 2) * BANK + (k + 1) * P]
                    for f in range(FB):
                        ins = pe.matmul(Y, hid[:, c % 2, f, k * P:(k + 1) * P], w2[:, u, f, :],
                                        start=(f == 0), stop=(f == FB - 1))
                ins.then_inc(s["y_ready"], 1)

            pe.wait_ge(s["comb_done"], 1)
            for t in range(NT):
                pe.transpose(ps[0:E, bass.ds(t * P, P)], comb[:, t, :], S.ident[:]).then_inc(s["combt_ready"], 1)
            pe.wait_ge(s["combt_stored"], NC)
            for t in range(NT):
                pe.matmul(ps[:, bass.ds(t * P, P)], combT[:, bass.ds(t * P, P)], b2[:], start=True,
                          stop=True).then_inc(s["bias_ready"], 1)
            pe.wait_ge(s["acc_init"], NC)

            pe.wait_ge(s["w1_loaded_0"], 16)
            hidden(0, 0, None)

            def expert(i, u, last=False):
                e = i * 2 + u
                pe.wait_ge(s[f"w2_loaded_{u}"], i * 16 + 16)
                for c in range(NC):
                    n = e * NC + c
                    if c < NC - 1:
                        hidden(u, c + 1, n + 1)
                    elif not last:
                        pe.wait_ge(s[f"w1_loaded_{1 - u}"], (i + u) * 16 + 16)
                        hidden(1 - u, 0, n + 1)
                    pe.wait_ge(s["y_added"], (n * 4 - 3) if c >= 1 else e * 16 + 1)
                    down(u, c, n)

            with pe.Fori(0, E // 2 - 1) as i:
                expert(i, 0)
                expert(i, 1)
            expert(E // 2 - 1, 0)
            expert(E // 2 - 1, 1, last=True)

        @block.scalar
        def _(act):
            norm.scalar(act, NT)
            act.wait_ge(s["top_diff"], 1)
            act.activation(S.sm[:, 1, 0:NT], S.sm[:, 0, 0:NT], ACT.Exp).then_inc(s["exp_done"], 1)
            for c in range(NC):
                act.wait_ge(s["combt_ready"], 4 * (c + 1))
                act.copy(combT[:, c * BANK:(c + 1) * BANK], ps[0:E, c * BANK:(c + 1) * BANK]).then_inc(
                    s["combt_stored"], 1)
            act.wait_ge(s["w_loaded"], 16)

            def gelus(e, c, first=False):
                n = e * NC + c
                act.wait_ge(s["h_ready"], n + 1)
                if not (first and c < 2):
                    act.wait_ge(s["y_ready"], n - 1)
                act.sem_inc(s["gate"], 1)
                for f in range(FB):
                    ins = act.activation(hid[:, c % 2, f, :], ps[:, f * BANK:(f + 1) * BANK], ACT.Gelu,
                                         bias=b1[:, bass.ds(e * FB + f, 1)])
                ins.then_inc(s["hid_ready"], 1)

            for c in range(NC):
                gelus(0, c, first=True)
            with act.Fori(1, E) as e:
                for c in range(NC):
                    gelus(e, c)

        @block.vector
        def _(v):
            norm.vector(v, NT)
            step = Chain(v, s["gate_chain"])
            bc = lambda ap: ap.unsqueeze(2).to_broadcast([P, NT, E])
            v.wait_ge(s["loaded"], 48)
            v.wait_ge(s["gate_ready"], NT)
            step(v.tensor_tensor(lg[:], ps[:, 0:NT * E].rearrange("p (t e) -> p t e", e=E),
                                 gb[:].unsqueeze(1).to_broadcast([P, NT, E]), ALU.add))
            for t in range(NT):
                ins = v.max(m8[:, t, :], lg[:, t, :])
            ins.then_inc(s["top_done"], 1)
            v.wait_ge(s["top_done"], 1)
            v.tensor_tensor(S.sm[:, 0, 0:NT], m8[:, :, 1], m8[:, :, 0], ALU.subtract).then_inc(s["top_diff"], 1)
            for t in range(NT):
                ins = v.max_index(i8[:, t, :], m8[:, t, :], lg[:, t, :])
            step(ins)
            step(v.tensor_copy(i8f[:], i8[:]))
            v.wait_ge(s["iota_done"], 1)
            v.tensor_tensor(c1[:], iot[:], bc(i8f[:, :, 0]), ALU.is_equal)
            v.tensor_tensor(c2[:], iot[:], bc(i8f[:, :, 1]), ALU.is_equal)
            v.wait_ge(s["exp_done"], 1)
            step(v.tensor_scalar(S.sm[:, 2, 0:NT], S.sm[:, 1, 0:NT], 1.0, None, ALU.add))
            step(v.reciprocal(S.sm[:, 3, 0:NT], S.sm[:, 2, 0:NT]))
            step(v.tensor_tensor(S.sm[:, 4, 0:NT], S.sm[:, 3, 0:NT], S.sm[:, 1, 0:NT], ALU.mult))
            v.tensor_tensor(c1[:], c1[:], bc(S.sm[:, 3, 0:NT]), ALU.mult)
            step(v.tensor_tensor(c2[:], c2[:], bc(S.sm[:, 4, 0:NT]), ALU.mult))
            v.tensor_tensor(comb[:], c1[:], c2[:], ALU.add).then_inc(s["comb_done"], 1)
            for c in range(NC):
                v.wait_ge(s["bias_ready"], 4 * (c + 1))
                v.tensor_tensor(acc[:, 4 * c:4 * c + 4, :], acc[:, 4 * c:4 * c + 4, :],
                                ps[:, c * BANK:(c + 1) * BANK].rearrange("p (t d) -> p t d", d=D),
                                ALU.add).then_inc(s["acc_init"], 1)
            v.wait_ge(s["acc_init"], NC)
            v.sem_inc(s["y_added"], 1)
            v.wait_ge(s["comb_done"], 1)
            v.wait_ge(s["acc_init"], NC)
            with v.Fori(0, E) as e:
                for c in range(NC):
                    n = e * NC + c
                    v.wait_ge(s["y_ready"], n + 1)
                    v.wait_ge(s["y_added"], e * 16 + 1)
                    for k in range(4):
                        t = 4 * c + k
                        Y = ps[:, (6 + c % 2) * BANK + k * P:(6 + c % 2) * BANK + (k + 1) * P]
                        v.scalar_tensor_tensor(acc[:, t, :], Y, comb[:, t, bass.ds(e, 1)], acc[:, t, :],
                                               ALU.mult, ALU.add).then_inc(s["y_added"], 1)
            v.wait_ge(s["y_added"], 4 * NC * E + 1)


TOPK = 64
PARTS = 3
SEGS = 16
ROUNDS = 7
LOWEST = -3.0e38


def attention(nc, ctx, S, A):
    with ExitStack() as own:
        NT, T = S.NT, S.T
        NCH = T // BANK
        sb = lambda name, shape, dt=F32: own.enter_context(nc.sbuf_tensor("at_" + name, shape, dt))
        sem = lambda name: ctx.enter_context(nc.semaphore("at_" + name))
        qT = sb("qT", [P, T])
        kT = sb("kT", [P, T])
        V = sb("V", [P, NT, HEADS, DH + 1])
        wo = sb("wo", [P, D])
        count = sb("count", [P, NT * HEADS])
        parts = nc.dram_tensor("qk_parts", (2, HEADS, PARTS, DH, T), BF16, kind="Internal").ap()
        project_qkv(nc, ctx, S, A, qT, kT, V, wo, parts)
        select_and_mix(nc, ctx, S, parts, V, count)
        redo(nc, ctx, S, qT, kT, V, count)
        project_out(nc, ctx, S, A, wo)


def project_qkv(nc, ctx, S, A, qT, kT, V, wo, parts):
    with ExitStack() as own:
        NT, T = S.NT, S.T
        NCH = T // BANK
        sb = lambda name, shape, dt=F32: own.enter_context(nc.sbuf_tensor("qk_" + name, shape, dt))
        wqk = sb("wqk", [P, 2, P])
        bqk = sb("bqk", [P, 2])
        wv = sb("wv", [P, D])
        bv = sb("bv", [P, D])
        bo = sb("bo", [P, D])
        part = sb("part", [P, 2, PARTS, T], BF16)
        left = sb("left", [P, 2, T])
        norm = Norm(nc, ctx, "atln", S)
        s = {n: ctx.enter_context(nc.semaphore("qk_" + n)) for n in
             "loaded ready_a ready_v stored_a stored_v v_ready v_stored res high_done left_done_0 left_done_1 mid_done low_done_0 low_done_1 kept_in_dram".split()}
        ps = S.ps
        block = own.enter_context(nc.Block())

        @block.sync
        def _(sp):
            sp.dma_start(wqk[:], A["wqk"]).then_inc(s["loaded"], 16)
            sp.dma_start(bqk[:], A["bqk"]).then_inc(s["loaded"], 16)
            sp.dma_start(wv[:], A["wv"]).then_inc(s["loaded"], 16)
            sp.dma_start(bv[:], A["bv"].partition_broadcast(P)).then_inc(s["loaded"], 16)
            sp.dma_start(wo[:], A["w_o"]).then_inc(s["loaded"], 16)
            sp.dma_start(bo[:], A["b_o"].partition_broadcast(P)).then_inc(s["loaded"], 16)
            for k, done in enumerate(("high_done", "mid_done", "low_done")):
                for side in range(2):
                    if k < 2:
                        sp.wait_ge(s[done], side + 1)
                    else:
                        sp.wait_ge(s[f"{done}_{side}"], 1)
                    sp.dma_start(parts[side, :, k, :, :], part[:, side, k, :]).then_inc(s["kept_in_dram"], 16)
            sp.wait_ge(s["kept_in_dram"], 16 * 2 * PARTS)

        items = [(side, c) for side in range(2) for c in range(NCH)]

        @block.tensor
        def _(pe):
            norm.tensor(pe, NT)
            pe.wait_ge(s["loaded"], 96)
            for n, (side, c) in enumerate(items):
                who = "a" if c % 2 == 0 else "v"
                if n >= NCH:
                    pe.wait_ge(s["stored_" + who], n // NCH * 2 - 1 + c // 2)
                pe.matmul(ps[:, c * BANK:(c + 1) * BANK], wqk[:, side, :], S.hT[:, c * BANK:(c + 1) * BANK],
                          start=True, stop=True).then_inc(s["ready_" + who], 1)
            for t in range(NT):
                pe.matmul(ps[:, 4 * BANK + t * D:4 * BANK + (t + 1) * D], S.hT[:, t * P:(t + 1) * P], wv[:],
                          start=True, stop=True).then_inc(s["v_ready"], 1)

        @block.scalar
        def _(act):
            norm.scalar(act, NT)
            act.wait_ge(s["loaded"], 96)
            for n, (side, c) in enumerate(items):
                if c % 2 == 0:
                    act.wait_ge(s["ready_a"], n // NCH * 2 + c // 2 + 1)
                    act.activation((qT, kT)[side][:, c * BANK:(c + 1) * BANK], ps[:, c * BANK:(c + 1) * BANK],
                                   ACT.Identity,
                                   bias=bqk[:, side:side + 1]).then_inc(s["stored_a"], 1)
            for side in range(2):
                act.wait_ge(s["stored_a"], NCH // 2 * (side + 1))
                act.wait_ge(s["stored_v"], NCH // 2 * (side + 1))
                act.copy(part[:, side, 0, :], (qT, kT)[side][:]).then_inc(s["high_done"], 1)
            for side in range(2):
                act.wait_ge(s[f"left_done_{side}"], 1)
                act.copy(part[:, side, 1, :], left[:, side, :]).then_inc(s["mid_done"], 1)

        @block.gpsimd
        def _(pool):
            nc.gpsimd.memset(V[:, :, :, DH:DH + 1], 1.0)
            pool.wait_ge(s["high_done"], 2)
            nc.gpsimd.tensor_tensor(left[:, 1, :], kT[:], part[:, 1, 0, :], ALU.subtract).then_inc(s["left_done_1"], 1)
            pool.wait_ge(s["mid_done"], 2)
            nc.gpsimd.tensor_tensor(part[:, 1, 2, :], left[:, 1, :], part[:, 1, 1, :],
                                    ALU.subtract).then_inc(s["low_done_1"], 1)

        @block.vector
        def _(v):
            norm.vector(v, NT)
            v.wait_ge(s["loaded"], 96)
            v.tensor_tensor(S.x[:], S.x[:], S.hn[:], ALU.add).then_inc(s["res"], 1)
            v.wait_ge(s["res"], 1)
            v.tensor_tensor(S.x[:], S.x[:], bo[:].unsqueeze(1).to_broadcast([P, NT, D]), ALU.add).then_inc(s["res"], 1)
            for n, (side, c) in enumerate(items):
                if c % 2 == 1:
                    v.wait_ge(s["ready_v"], n // NCH * 2 + c // 2 + 1)
                    v.tensor_scalar((qT, kT)[side][:, c * BANK:(c + 1) * BANK], ps[:, c * BANK:(c + 1) * BANK],
                                    bqk[:, side:side + 1], None,
                                    ALU.add).then_inc(s["stored_v"], 1)
            v.wait_ge(s["high_done"], 1)
            v.tensor_tensor(left[:, 0, :], qT[:], part[:, 0, 0, :], ALU.subtract).then_inc(s["left_done_0"], 1)
            for c in range(NCH):
                v.wait_ge(s["v_ready"], 4 * (c + 1))
                v.tensor_tensor(V[:, 4 * c:4 * c + 4, :, 0:DH],
                                ps[:, (4 + c) * BANK:(5 + c) * BANK].rearrange("p (t h d) -> p t h d", h=HEADS, d=DH),
                                bv[:].rearrange("p (h d) -> p h d", d=DH).unsqueeze(1).to_broadcast(
                                    [P, 4, HEADS, DH]), ALU.add).then_inc(s["v_stored"], 1)
            v.wait_ge(s["mid_done"], 1)
            v.tensor_tensor(part[:, 0, 2, :], left[:, 0, :], part[:, 0, 1, :], ALU.subtract).then_inc(
                s["low_done_0"], 1)


def ge(eng, sem, value):
    if not (isinstance(value, int) and value <= 0):
        eng.wait_ge(sem, value)


def select_and_mix(nc, ctx, S, parts, V, count):
    with ExitStack() as own:
        NT, T = S.NT, S.T
        NCH, NB = T // BANK, T // P
        SCALE = 1.0 / float(np.sqrt(DH))
        BODY = NT // 2
        ROWS = PARTS * PARTS * DH
        N = NT * HEADS
        SEG = T // SEGS
        sb = lambda name, shape, dt=F32: own.enter_context(nc.sbuf_tensor("sm_" + name, shape, dt))
        qh = sb("qh", [ROWS, 2, T], BF16)
        kh = sb("kh", [ROWS, 2, T], BF16)
        sc = sb("sc", [P, 4, T])
        ex = sb("ex", [P, 4, T])
        side = sb("side", [P, 2, T], mybir.dt.bfloat16)
        drop = sb("drop", [P, 2, T], BF16)
        low = sb("low", [P, 2, T])
        pr = sb("pr", [P, 2, T])
        pT = sb("pT", [P, 2, T])
        cand = sb("cand", [P, 2, SEGS * 8])
        tops = sb("tops", [P, 2, ROUNDS, 8])
        nmax = sb("nmax", [P, 4, 1])
        rank = sb("rank", [P, 2, 1])
        nextT = sb("nextT", [P, 2, 8])
        pick = sb("pick", [P, 2, 8])
        kth = sb("kth", [P, 2, 1])
        rden = sb("rden", [P, 2, 1])
        above = sb("above", [P, 4, 1])
        iota8 = sb("iota8", [P, 8])
        attn = S.hT
        names = ("head_loaded head_ready s_ready sc_stored seg_done max_ready exp_done pivot_ready side_done low_done chain "
                 "rank_done next_done kth_done dropped kept turned pt_stored pt_stored_v mixed rden_done attn_done gate iota").split()
        s = {n: ctx.enter_context(nc.semaphore("sm_" + n)) for n in names}
        ps = S.ps
        block = own.enter_context(nc.Block())

        def tile(it, j):
            return it * BODY + j, (it % 2) * BODY + j, it // 2

        def at(start, size):
            return slice(start, start + size) if isinstance(start, int) else bass.ds(start, size)

        def run(eng, step, first=0, last=0):
            for j in range(BODY):
                step(0, j)
            with eng.Fori(1, N // BODY - 1) as it:
                for j in range(BODY):
                    step(it, j)
            for j in range(BODY):
                step(N // BODY - 1, j)

        def before(it, j, k):
            if j >= k:
                return it, j - k
            if isinstance(it, int) and it == 0:
                return None
            return it - 1, j - k + BODY

        def after(it, j, k):
            if j + k < BODY:
                return it, j + k
            if isinstance(it, int) and it == N // BODY - 1:
                return None
            return it + 1, j + k - BODY

        @block.sync
        def _(sp):
            def load(h, slot):
                for a in range(PARTS):
                    r = slice(a * PARTS * DH, (a + 1) * PARTS * DH)
                    qa = parts[0, at(h, 1), a, :, :].to_broadcast([PARTS, DH, T])
                    kb = parts[1, at(h, 1), :, :, :].rearrange("o b d t -> (o b d) t")
                    sp.dma_start(qh[r, at(slot, 1), :], qa).then_inc(s["head_loaded"], 16)
                    sp.dma_start(kh[r, at(slot, 1), :], kb).then_inc(s["head_loaded"], 16)

            load(0, 0)
            sp.wait_ge(s["head_loaded"], 16 * 2 * PARTS)
            sp.sem_inc(s["head_ready"], 1)
            load(1, 1)
            sp.wait_ge(s["head_loaded"], 2 * 16 * 2 * PARTS)
            sp.sem_inc(s["head_ready"], 1)
            with sp.Fori(1, HEADS // 2) as i:
                for u in range(2):
                    h = i * 2 + u
                    sp.wait_ge(s["s_ready"], (i * 2 - 1 + u) * NT)
                    load(h, u)
                    sp.wait_ge(s["head_loaded"], (h + 1) * 16 * 2 * PARTS)
                    sp.sem_inc(s["head_ready"], 1)

        @block.gpsimd
        def _(pool):
            nc.gpsimd.iota(iota8[:], pattern=[[1, 8]], base=0, channel_multiplier=0,
                           allow_small_or_imprecise_dtypes=True).then_inc(s["iota"], 1)

            def below(it, j):
                n = tile(it, j)[0]
                pool.wait_ge(s["side_done"], n + 1)
                pool.wait_ge(s["exp_done"], n + 1)
                ge(pool, s["next_done"], n - 1)
                nc.gpsimd.tensor_tensor(low[:, j % 2, :], ex[:, j % 4, :], side[:, j % 2, :],
                                        ALU.mult).then_inc(s["low_done"], 1)

            def keep(it, j):
                n = tile(it, j)[0]
                pool.wait_ge(s["dropped"], n + 1)
                ge(pool, s["turned"], (n - 1) * NCH)
                nc.gpsimd.tensor_tensor(pr[:, j % 2, :], ex[:, j % 4, :], drop[:, j % 2, :],
                                        ALU.mult).then_inc(s["kept"], 1)

            def step(it, j):
                below(it, j)
                old = before(it, j, 1)
                if old:
                    keep(*old)

            run(pool, step)
            keep(N // BODY - 1, BODY - 1)

        @block.tensor
        def _(pe):
            qf = qh[:].rearrange("r u t -> r (u t)")
            kf = kh[:].rearrange("r u t -> r (u t)")
            vf = V[:].rearrange("p t h d -> p t (h d)")

            def scores(it, j):
                n, qt, h = tile(it, j)
                if j == 0:
                    pe.wait_ge(s["head_ready"], h + 1)
                ge(pe, s["sc_stored"], n)
                for c in range(NCH):
                    ins = pe.matmul(ps[:, c * BANK:(c + 1) * BANK], qf[:, at((h % 2) * T + qt * P, P)],
                                    kf[:, at((h % 2) * T + c * BANK, BANK)], start=True, stop=True)
                ins.then_inc(s["s_ready"], 1)

            def turn(it, j, groups):
                n = tile(it, j)[0]
                pe.wait_ge(s["kept"], n + 1)
                for b in groups:
                    if b == 0:
                        ge(pe, s["pt_stored"], n * (NCH - 1))
                    elif b == 1:
                        ge(pe, s["pt_stored_v"], n)
                    else:
                        pe.wait_ge(s["pt_stored"], n * (NCH - 1) + b - 1)
                    for k in range(4):
                        kb = b * 4 + k
                        ins = pe.transpose(ps[:, (4 + b % 2) * BANK + k * P:(4 + b % 2) * BANK + (k + 1) * P],
                                           pr[:, j % 2, kb * P:(kb + 1) * P], S.ident[:])
                    ins.then_inc(s["turned"], 1)

            def mix(it, j):
                n, qt, h = tile(it, j)
                pe.wait_ge(s["pt_stored"], n * (NCH - 1) + NCH - 1)
                pe.wait_ge(s["pt_stored_v"], n + 1)
                ge(pe, s["attn_done"], n - 1)
                for kb in range(NB):
                    ins = pe.matmul(ps[:, (6 + j % 2) * BANK:(6 + j % 2) * BANK + DH + 1],
                                    pT[:, j % 2, kb * P:(kb + 1) * P], vf[:, kb, at(h * (DH + 1), DH + 1)],
                                    start=(kb == 0), stop=(kb == NB - 1))
                ins.then_inc(s["mixed"], 1)

            EARLY, LATE = range(NCH // 2), range(NCH // 2, NCH)
            scores(0, 0)
            scores(0, 1)

            def step(it, j):
                nxt, new, old = after(it, j, 2), before(it, j, 3), before(it, j, 4)
                if old:
                    turn(*old, LATE)
                if nxt:
                    scores(*nxt)
                if new:
                    turn(*new, EARLY)
                if old:
                    mix(*old)

            run(pe, step)
            last = N // BODY - 1
            for j in range(BODY - 4, BODY):
                turn(last, j, LATE)
                if j + 1 < BODY:
                    turn(last, j + 1, EARLY)
                mix(last, j)

        @block.scalar
        def _(act):
            def copy_scores(it, j):
                n = tile(it, j)[0]
                act.wait_ge(s["s_ready"], n + 1)
                ge(act, s["side_done"], n - 3)
                act.copy(sc[:, j % 4, :], ps[:, 0:T]).then_inc(s["sc_stored"], 1)

            def exps(it, j):
                n = tile(it, j)[0]
                act.wait_ge(s["max_ready"], n + 1)
                ge(act, s["kept"], n - 3)
                act.activation(ex[:, j % 4, :], sc[:, j % 4, :], ACT.Exp, scale=SCALE,
                               bias=nmax[:, j % 4, :]).then_inc(s["exp_done"], 1)

            def signs(it, j):
                n = tile(it, j)[0]
                act.wait_ge(s["pivot_ready"], n + 1)
                ge(act, s["low_done"], n - 1)
                act.activation(side[:, j % 2, :], sc[:, j % 4, :], ACT.Sign, scale=-1.0,
                               bias=tops[:, j % 2, ROUNDS - 1, 7:8],
                               accum_out=above[:, j % 4, :]).then_inc(s["side_done"], 1)

            def signs_kept(it, j):
                n = tile(it, j)[0]
                act.wait_ge(s["kth_done"], n + 1)
                ge(act, s["kept"], n - 1)
                ge(act, s["dropped"], n)
                act.sem_inc(s["gate"], 1)
                act.activation(drop[:, j % 2, :], ex[:, j % 4, :], ACT.Sign, scale=-(1.0 + 2.0 ** -23),
                               bias=kth[:, j % 2, :], accum_out=count[:, at(n, 1)]).then_inc(s["dropped"], 1)

            def move_turned(it, j, groups):
                n = tile(it, j)[0]
                ge(act, s["mixed"], n - 1)
                for b in groups:
                    act.wait_ge(s["turned"], n * NCH + b + 1)
                    act.activation(pT[:, j % 2, b * BANK:(b + 1) * BANK],
                                   ps[:, (4 + b % 2) * BANK:(5 + b % 2) * BANK], ACT.Relu,
                                   scale=-1.0).then_inc(s["pt_stored"], 1)

            copy_scores(0, 0)
            copy_scores(0, 1)

            def step(it, j):
                nxt, old = after(it, j, 2), before(it, j, 3)
                exps(it, j)
                if old:
                    move_turned(*old, range(1))
                if nxt:
                    copy_scores(*nxt)
                if old:
                    move_turned(*old, range(1, NCH - 1))
                signs(it, j)
                old = before(it, j, 1)
                if old:
                    signs_kept(*old)

            run(act, step)
            last = N // BODY - 1
            signs_kept(last, BODY - 1)
            for j in (BODY - 3, BODY - 2, BODY - 1):
                move_turned(last, j, range(NCH - 1))

        @block.vector
        def _(v):
            def seg_max(j, k):
                return v.max(cand[:, j % 2, k * 8:(k + 1) * 8], sc[:, j % 4, k:T:SEGS])

            def select(it, j):
                n = tile(it, j)[0]
                nxt = after(it, j, 1)
                if nxt:
                    v.wait_ge(s["sc_stored"], n + 2)
                    v.sem_inc(s["gate"], 1)
                c, todo = cand[:, j % 2, :], list(range(SEGS)) if nxt else []
                base = 2 * ROUNDS * j
                for r in range(ROUNDS):
                    top = tops[:, j % 2, r, :]
                    v.max(top, c).then_inc(s["chain"], 1)
                    if todo:
                        ins = seg_max(nxt[1], todo.pop(0))
                    v.wait_ge(s["chain"], base + 2 * r + 1)
                    if r == 0:
                        v.tensor_scalar(nmax[:, j % 4, :], tops[:, j % 2, 0, 0:1], -SCALE, None,
                                        ALU.mult).then_inc(s["max_ready"], 1)
                    if r < ROUNDS - 1:
                        v.match_replace(c, top, c, LOWEST).then_inc(s["chain"], 1)
                    else:
                        v.sem_inc(s["chain"], 1)
                        v.sem_inc(s["pivot_ready"], 1)
                    if todo:
                        ins = seg_max(nxt[1], todo.pop(0))
                    if r < ROUNDS - 1:
                        v.wait_ge(s["chain"], base + 2 * r + 2)
                while todo:
                    ins = seg_max(nxt[1], todo.pop(0))
                if nxt:
                    ins.then_inc(s["seg_done"], 1)

            def find(it, j, old):
                n = tile(it, j)[0]
                if old:
                    invert(*old)
                v.wait_ge(s["side_done"], n + 1)
                v.tensor_scalar(rank[:, j % 2, :], above[:, j % 4, :], 0.5, TOPK - 1 - (T + 1) / 2.0, ALU.mult,
                                ALU.add).then_inc(s["rank_done"], 1)
                v.wait_ge(s["low_done"], n + 1)
                v.sem_inc(s["gate"], 1)
                v.max(nextT[:, j % 2, :], low[:, j % 2, :]).then_inc(s["next_done"], 1)
                if old:
                    output(*old)
                v.wait_ge(s["next_done"], n + 1)
                v.scalar_tensor_tensor(pick[:, j % 2, :], iota8[:], rank[:, j % 2, :], nextT[:, j % 2, :],
                                       ALU.is_equal, ALU.mult, accum_out=kth[:, j % 2, :]).then_inc(s["kth_done"], 1)

            def invert(it, j):
                n = tile(it, j)[0]
                v.wait_ge(s["mixed"], n + 1)
                v.reciprocal(rden[:, j % 2, :], ps[:, (6 + j % 2) * BANK + DH:(6 + j % 2) * BANK + DH + 1]).then_inc(
                    s["rden_done"], 1)

            def output(it, j):
                n, qt, h = tile(it, j)
                v.wait_ge(s["rden_done"], n + 1)
                v.sem_inc(s["gate"], 1)
                v.tensor_scalar(attn[:, at(qt * D + h * DH, DH)], ps[:, (6 + j % 2) * BANK:(6 + j % 2) * BANK + DH],
                                rden[:, j % 2, :], None, ALU.mult).then_inc(s["attn_done"], 1)

            def move_last(it, j):
                n = tile(it, j)[0]
                v.wait_ge(s["turned"], n * NCH + NCH)
                ge(v, s["mixed"], n - 1)
                v.tensor_scalar(pT[:, j % 2, (NCH - 1) * BANK:], ps[:, 5 * BANK:6 * BANK], -1.0, 0.0, ALU.mult,
                                ALU.max).then_inc(s["pt_stored_v"], 1)

            v.wait_ge(s["iota"], 1)
            v.wait_ge(s["sc_stored"], 1)
            for k in range(SEGS):
                ins = seg_max(0, k)
            ins.then_inc(s["seg_done"], 1)

            def step(it, j):
                if j == 0 :
                    v.sem_clear(s["chain"])
                n = tile(it, j)[0]
                v.wait_ge(s["seg_done"], n + 1)
                v.sem_inc(s["gate"], 1)
                select(it, j)
                old = before(it, j, 1)
                if old:
                    find(*old, before(it, j, 5))
                old = before(it, j, 3)
                if old:
                    move_last(*old)

            run(v, step)
            last = N // BODY - 1
            find(last, BODY - 1, (last, BODY - 5))
            invert(last, BODY - 4)
            output(last, BODY - 4)
            for j in (BODY - 3, BODY - 2, BODY - 1):
                move_last(last, j)
                invert(last, j)
                output(last, j)


def redo(nc, ctx, S, qT, kT, V, count):
    with ExitStack() as own:
        NT, T = S.NT, S.T
        NCH, NB = T // BANK, T // P
        N = NT * HEADS
        HALVES = N // P
        SCALE = 1.0 / float(np.sqrt(DH))
        I32 = mybir.dt.int32
        sb = lambda name, shape, dt=F32: own.enter_context(nc.sbuf_tensor("re_" + name, shape, dt))
        bad = sb("bad", [P, N])
        flag = sb("flag", [P, HALVES])
        place = sb("place", [P, HALVES])
        tile_no = sb("tile_no", [P, HALVES])
        one_to_n = sb("one_to_n", [P, N])
        onehot = sb("onehot", [P, HALVES, N])
        list_i = sb("list_i", [1, N], I32)
        total_i = sb("total_i", [1, 1], I32)
        qs = sb("qs", [P, P])
        sc = sb("sc", [P, T])
        rest = sb("rest", [P, T])
        ex = sb("ex", [P, T])
        pr = sb("pr", [P, T])
        pT = sb("pT", [P, T])
        tops = sb("tops", [P, TOPK // 8, 8])
        nmax = sb("nmax", [P, 1])
        den = sb("den", [P, 1])
        rden = sb("rden", [P, 1])
        names = ("iotas bad_done flag_sum flag_done placed place_done onehot_done listed ints_done redone qs_ready s_ready sc_stored chain "
                 "max_ready exp_done kept turned pt_stored mixed rden_done gate").split()
        s = {n: ctx.enter_context(nc.semaphore("re_" + n)) for n in names}
        ps = S.ps
        block = own.enter_context(nc.Block())

        def each_flagged(eng, body):
            eng.wait_ge(s["ints_done"], 2)
            total = eng.value_load(total_i[0:1, 0:1], min_val=0, max_val=N)
            with eng.Fori(0, N // 32) as a:
                with eng.If(total > a * 32):
                    with eng.Fori(0, 8) as b:
                        with eng.If(total > a * 32 + b * 4):
                            with eng.Fori(0, 4) as c:
                                k = a * 32 + b * 4 + c
                                with eng.If(total > k):
                                    n = eng.value_load(list_i[0:1, bass.ds(k, 1)], min_val=0, max_val=N - 1)
                                    eng.wait_ge(s["redone"], k + 1)
                                    eng.sem_inc(s["gate"], 1)
                                    body(n % NT, n // NT, k)

        @block.gpsimd
        def _(pool):
            nc.gpsimd.iota(one_to_n[:], pattern=[[1, N]], base=1, channel_multiplier=0,
                           allow_small_or_imprecise_dtypes=True).then_inc(s["iotas"], 1)
            nc.gpsimd.iota(tile_no[:], pattern=[[P, HALVES]], base=0, channel_multiplier=1,
                           allow_small_or_imprecise_dtypes=True).then_inc(s["iotas"], 1)

            def body(qt, h, k):
                nc.gpsimd.tensor_tensor(qs[:], qT[:, bass.ds(qt * P, P)],
                                        S.headmask[:, bass.ds(h, 1)].to_broadcast([P, P]),
                                        ALU.mult).then_inc(s["qs_ready"], 1)

            each_flagged(pool, body)

        @block.tensor
        def _(pe):
            vf = V[:].rearrange("p t h d -> p t (h d)")
            pe.wait_ge(s["bad_done"], 1)
            for i in range(HALVES):
                ins = pe.matmul(ps[:, i:i + 1], bad[:, i * P:(i + 1) * P], S.ones[:, 0:1], start=True, stop=True)
            ins.then_inc(s["flag_sum"], 1)
            pe.wait_ge(s["flag_done"], 1)
            for i in range(HALVES):
                for k in range(i + 1):
                    pe.matmul(ps[:, BANK + i:BANK + i + 1], (S.upper if k == i else S.ones)[:], flag[:, k:k + 1],
                              start=(k == 0), stop=(k == i))
            for i in range(HALVES):
                ins = pe.matmul(ps[:, BANK + HALVES:BANK + HALVES + 1], S.ones[:], flag[:, i:i + 1], start=(i == 0),
                                stop=(i == HALVES - 1))
            ins.then_inc(s["placed"], 1)
            pe.wait_ge(s["onehot_done"], HALVES)
            pe.wait_ge(s["iotas"], 2)
            for i in range(HALVES):
                ins = pe.matmul(ps[0:1, 2 * BANK:2 * BANK + N], tile_no[:, i:i + 1], onehot[:, i, :], start=(i == 0),
                                stop=(i == HALVES - 1))
            ins.then_inc(s["listed"], 1)

            def body(qt, h, k):
                pe.wait_ge(s["qs_ready"], k + 1)
                for c in range(NCH):
                    ins = pe.matmul(ps[:, c * BANK:(c + 1) * BANK], qs[:], kT[:, c * BANK:(c + 1) * BANK],
                                    start=True, stop=True)
                ins.then_inc(s["s_ready"], 1)
                pe.wait_ge(s["kept"], k + 1)
                for b in range(NB):
                    ins = pe.transpose(ps[:, b * P:(b + 1) * P], pr[:, b * P:(b + 1) * P], S.ident[:])
                    if b % 4 == 3:
                        ins.then_inc(s["turned"], 1)
                for b in range(NB):
                    if b % 4 == 0:
                        pe.wait_ge(s["pt_stored"], k * NCH + b // 4 + 1)
                    ins = pe.matmul(ps[:, 6 * BANK:6 * BANK + DH], pT[:, b * P:(b + 1) * P],
                                    vf[:, b, bass.ds(h * (DH + 1), DH)], start=(b == 0), stop=(b == NB - 1))
                ins.then_inc(s["mixed"], 1)

            each_flagged(pe, body)

        @block.scalar
        def _(act):
            def body(qt, h, k):
                act.wait_ge(s["s_ready"], k + 1)
                act.copy(sc[:], ps[:, 0:T]).then_inc(s["sc_stored"], 1)
                act.wait_ge(s["max_ready"], k + 1)
                act.activation(ex[:], sc[:], ACT.Exp, scale=SCALE, bias=nmax[:]).then_inc(s["exp_done"], 1)
                for b in range(NCH):
                    act.wait_ge(s["turned"], k * NCH + b + 1)
                    act.copy(pT[:, b * BANK:(b + 1) * BANK], ps[:, b * BANK:(b + 1) * BANK]).then_inc(s["pt_stored"], 1)

            each_flagged(act, body)

        @block.vector
        def _(v):
            v.tensor_scalar(bad[:], count[:], float(T - 2 * TOPK), None, ALU.not_equal).then_inc(s["bad_done"], 1)
            v.wait_ge(s["flag_sum"], 1)
            v.tensor_scalar(flag[:], ps[:, 0:HALVES], 1.0, None, ALU.min).then_inc(s["flag_done"], 1)
            v.wait_ge(s["placed"], 1)
            v.tensor_copy(place[:], ps[:, BANK:BANK + HALVES]).then_inc(s["place_done"], 1)
            v.tensor_copy(total_i[:], ps[0:1, BANK + HALVES:BANK + HALVES + 1]).then_inc(s["ints_done"], 1)
            v.wait_ge(s["iotas"], 1)
            v.wait_ge(s["place_done"], 1)
            for i in range(HALVES):
                v.tensor_scalar(onehot[:, i, :], one_to_n[:], place[:, i:i + 1], flag[:, i:i + 1], ALU.is_equal,
                                ALU.mult).then_inc(s["onehot_done"], 1)
            v.sem_inc(s["redone"], 1)
            v.wait_ge(s["listed"], 1)
            v.tensor_copy(list_i[:], ps[0:1, 2 * BANK:2 * BANK + N]).then_inc(s["ints_done"], 1)

            def body(qt, h, k):
                v.sem_clear(s["chain"])
                v.wait_ge(s["sc_stored"], k + 1)
                v.sem_inc(s["gate"], 1)
                for r in range(TOPK // 8):
                    v.max(tops[:, r, :], (sc if r == 0 else rest)[:]).then_inc(s["chain"], 1)
                    v.wait_ge(s["chain"], 2 * r + 1)
                    if r == 0:
                        v.tensor_scalar(nmax[:], tops[:, 0, 0:1], -SCALE, None, ALU.mult).then_inc(s["max_ready"], 1)
                    v.match_replace(rest[:], tops[:, r, :], (sc if r == 0 else rest)[:], LOWEST).then_inc(s["chain"], 1)
                    v.wait_ge(s["chain"], 2 * r + 2)
                v.wait_ge(s["exp_done"], k + 1)
                v.scalar_tensor_tensor(pr[:], rest[:], LOWEST, ex[:], ALU.is_le, ALU.mult,
                                       accum_out=den[:]).then_inc(s["kept"], 1)
                v.wait_ge(s["kept"], k + 1)
                v.reciprocal(rden[:], den[:]).then_inc(s["rden_done"], 1)
                v.wait_ge(s["rden_done"], k + 1)
                v.wait_ge(s["mixed"], k + 1)
                v.sem_inc(s["gate"], 1)
                v.tensor_scalar(S.hT[:, bass.ds(qt * D + h * DH, DH)], ps[:, 6 * BANK:6 * BANK + DH], rden[:], None,
                                ALU.mult).then_inc(s["redone"], 1)

            each_flagged(v, body)


def project_out(nc, ctx, S, A, wo):
    with ExitStack() as own:
        NT, T = S.NT, S.T
        s = {n: ctx.enter_context(nc.semaphore("po_" + n)) for n in "turned stored ready added".split()}
        aT = own.enter_context(nc.sbuf_tensor("po_aT", [P, T], F32))
        ps = S.ps
        block = own.enter_context(nc.Block())

        @block.tensor
        def _(pe):
            for t in range(NT):
                pe.transpose(ps[:, t * P:(t + 1) * P], S.hT[:, t * P:(t + 1) * P], S.ident[:]).then_inc(s["turned"], 1)
            for t in range(NT):
                if t % 4 == 0:
                    pe.wait_ge(s["stored"], t // 4 + 1)
                pe.matmul(ps[:, 4 * BANK + t * D:4 * BANK + (t + 1) * D], aT[:, t * P:(t + 1) * P], wo[:], start=True,
                          stop=True).then_inc(s["ready"], 1)

        @block.scalar
        def _(act):
            for b in range(4):
                act.wait_ge(s["turned"], 4 * (b + 1))
                act.copy(aT[:, b * BANK:(b + 1) * BANK], ps[:, b * BANK:(b + 1) * BANK]).then_inc(s["stored"], 1)

        @block.vector
        def _(v):
            for b in range(4):
                v.wait_ge(s["ready"], 4 * (b + 1))
                v.tensor_tensor(S.x[:, 4 * b:4 * b + 4, :], S.x[:, 4 * b:4 * b + 4, :],
                                ps[:, (4 + b) * BANK:(5 + b) * BANK].rearrange("p (t d) -> p t d", d=D),
                                ALU.add).then_inc(s["added"], 1)
            v.wait_ge(s["added"], 4)


class Shared:
    pass


def program(nc, ins, out, stages):
    S, A = Shared(), ins
    S.T = A["u"].shape[0]
    S.NT = S.T // P
    with ExitStack() as ctx:
        sb = lambda name, shape: ctx.enter_context(nc.sbuf_tensor(name, shape, F32))
        S.x = sb("x", [P, S.NT, D])
        S.hn = sb("hn", [P, S.NT, D])
        S.hT = sb("hT", [P, S.T])
        S.st = sb("st", [P, S.NT, 6])
        S.sm = sb("sm", [P, 8, S.NT])
        S.ps = ctx.enter_context(nc.psum_tensor("ps", [P, 8 * BANK], F32))
        S.x_loaded = ctx.enter_context(nc.semaphore("x_loaded"))
        S.m_loaded = ctx.enter_context(nc.semaphore("m_loaded"))
        constants(nc, ctx, S)
        mamba(nc, ctx, S, A)
        moe_sems, moe_norm = moe_semaphores(nc, ctx), Norm(nc, ctx, "moe_ln", S)
        if stages >= 2:
            moe(nc, S, A, "moe_a", moe_sems, moe_norm)
        if stages >= 3:
            attention(nc, ctx, S, A)
        if stages >= 4:
            clear(nc, list(moe_sems.values()) + moe_norm.all())
            moe(nc, S, A, "moe_b", moe_sems, moe_norm, out)
        else:
            write_out(nc, ctx, S, out)


def clear(nc, sems):
    with nc.Block() as block:

        @block.gpsimd
        def _(pool):
            for sem in sems:
                pool.sem_clear(sem)


def write_out(nc, ctx, S, out):
    stored = ctx.enter_context(nc.semaphore("stored"))
    with nc.Block() as block:

        @block.sync
        def _(sp):
            sp.dma_start(out.rearrange("(t p) d -> p t d", p=P), S.x[:]).then_inc(stored, 16)
            sp.wait_ge(stored, 16)





def kernel(**inputs):
    import numpy as _np
    import concourse.bacc as _bacc
    from concourse import mybir as _mybir
    from concourse.bass_utils import run_bass_kernel_spmd as _run

    i = {k: _np.asarray(v) for k, v in inputs.items()}
    u = i["L0_attn_a_u"]

    qkv = i["L0_attn_b_w_qkv_w"].reshape(HEADS, 3, DH, D).transpose(3, 1, 0, 2).reshape(D, 3, HEADS * DH)
    bias = i["L0_attn_b_w_qkv_b"].reshape(HEADS, 3, DH).transpose(0, 2, 1).reshape(HEADS * DH, 3)
    arrays = {
        "u": u.reshape(-1, D),
        "w_in": i["L0_attn_a_W_in"].T,
        "conv_w": i["L0_attn_a_conv_w"],
        "conv_b": i["L0_attn_a_conv_b"].reshape(-1, P).T,
        "dt_bias": i["L0_attn_a_dt_bias"],
        "a_log": i["L0_attn_a_A_log"],
        "dskip": i["L0_attn_a_D"],
        "norm_w": i["L0_attn_a_norm_w"].reshape(-1, P).T,
        "w_mo": i["L0_attn_a_W_out"].T,
        "wqk": qkv[:, :2],
        "bqk": bias[:, :2],
        "wv": qkv[:, 2],
        "bv": bias[:, 2],
        "w_o": i["L0_attn_b_w_out_w"].T,
        "b_o": i["L0_attn_b_w_out_b"],
        "gate_w": i["L0_ffn_gate_w"],
        "gate_b": i["L0_ffn_gate_b"],
        "w1": i["L0_ffn_w1"],
        "b1T": i["L0_ffn_b1"].reshape(-1, P).T,
        "w2": i["L0_ffn_w2"],
        "b2": i["L0_ffn_b2"],
    }
    arrays = {k: _np.ascontiguousarray(a) for k, a in arrays.items()}
    nc = _bacc.Bacc("TRN2", target_bir_lowering=False, num_devices=1)
    aps = {k: nc.dram_tensor(f"in_{k}", a.shape, _mybir.dt.from_np(a.dtype), kind="ExternalInput").ap()
           for k, a in arrays.items()}
    out = nc.dram_tensor("out_x", (u.shape[1], D), _mybir.dt.float32, kind="ExternalOutput").ap()
    program(nc, aps, out, STAGES)
    r = _run(nc, [{f"in_{k}": a for k, a in arrays.items()}], core_ids=[0])
    return r.results[0]["out_x"].reshape(u.shape)
STAGES = 4
```

```python
from contextlib import ExitStack

import numpy as np

import concourse.bass as bass
from concourse import mybir

ALU = mybir.AluOpType
ACT = mybir.ActivationFunctionType
AX = mybir.AxisListType
F32 = mybir.dt.float32
BF16 = mybir.dt.bfloat16

P = 128
D = 128
BANK = 512
EPS = 1e-5
BIG = 1e30


HEADS, DH = 16, 8
TOPK = 64
PARTS = 3
SEGS = 16
ROUNDS = 7
LOWEST = -3.0e38


class Chain:

    def __init__(self, eng, sem):
        self.eng, self.sem, self.n = eng, sem, 0

    def __call__(self, ins):
        self.n += 1
        ins.then_inc(self.sem, 1)
        self.eng.wait_ge(self.sem, self.n)


def constants(nc, ctx, S):
    sb = lambda name, shape: ctx.enter_context(nc.sbuf_tensor(name, shape, F32))
    S.ident = sb("ident", [P, P])
    S.upper = sb("upper", [P, P])
    S.cap = sb("cap", [P, P])
    S.ones = sb("ones", [P, P])
    S.headmask = sb("headmask", [P, HEADS])
    filled = ctx.enter_context(nc.semaphore("const_filled"))
    built = ctx.enter_context(nc.semaphore("const_built"))
    with nc.Block() as block:

        @block.gpsimd
        def _(pool):
            nc.gpsimd.memset(S.ident[:], 0.0)
            nc.gpsimd.memset(S.upper[:], 1.0)
            nc.gpsimd.memset(S.cap[:], 0.0)
            nc.gpsimd.memset(S.ones[:], 1.0).then_inc(filled, 1)
            pool.wait_ge(filled, 1)
            nc.gpsimd.affine_select(out=S.ident[:], in_=S.ident[:], compare_op=ALU.not_equal, fill=1.0,
                                    base=0, pattern=[[-1, P]], channel_multiplier=1)
            nc.gpsimd.affine_select(out=S.upper[:], in_=S.upper[:], compare_op=ALU.is_ge, fill=0.0,
                                    base=0, pattern=[[1, P]], channel_multiplier=-1)
            nc.gpsimd.affine_select(out=S.cap[:], in_=S.cap[:], compare_op=ALU.is_ge, fill=-BIG,
                                    base=0, pattern=[[1, P]], channel_multiplier=-1).then_inc(built, 1)
            pool.wait_ge(built, 1)
            nc.gpsimd.memset(S.headmask[:], 1.0).then_inc(built, 1)
            pool.wait_ge(built, 2)
            nc.gpsimd.affine_select(out=S.headmask[:], in_=S.headmask[:], compare_op=ALU.is_ge, fill=0.0, base=0,
                                    pattern=[[-DH, HEADS]], channel_multiplier=1).then_inc(built, 1)
            pool.wait_ge(built, 3)
            nc.gpsimd.affine_select(out=S.headmask[:], in_=S.headmask[:], compare_op=ALU.is_ge, fill=0.0, base=DH - 1,
                                    pattern=[[DH, HEADS]], channel_multiplier=-1).then_inc(built, 1)
            pool.wait_ge(built, 4)


class Norm:

    def __init__(self, nc, ctx, tag, S):
        sem = lambda n: ctx.enter_context(nc.semaphore(f"{tag}_{n}"))
        self.S = S
        self.stats_done, self.chain, self.var_ready = sem("stats_done"), sem("stat_chain"), sem("var_ready")
        self.sqrt_done, self.normed = sem("sqrt_done"), sem("normed")
        self.turned, self.stored = sem("turned"), sem("hT_stored")

    def all(self):
        return [self.stats_done, self.chain, self.var_ready, self.sqrt_done, self.normed, self.turned, self.stored]

    def vector(self, v, NT):
        S = self.S
        for t in range(NT):
            v.bn_stats(S.st[:, t, :], S.x[:, t, :]).then_inc(self.stats_done, 1)
        v.wait_ge(self.stats_done, NT)
        me, mo = S.st[:, :, 1], S.st[:, :, 4]
        qe, qo = S.st[:, :, 2], S.st[:, :, 5]
        a = lambda k: S.sm[:, k, 0:NT]
        step = Chain(v, self.chain)
        v.tensor_tensor(a(0), me, mo, ALU.add)
        v.tensor_tensor(a(1), me, mo, ALU.subtract)
        step(v.tensor_tensor(a(2), qe, qo, ALU.add))
        v.tensor_scalar(a(3), a(0), 0.5, None, ALU.mult)
        v.tensor_tensor(a(4), a(1), a(1), ALU.mult)
        step(v.tensor_scalar(a(5), a(2), 1.0 / D, EPS, ALU.mult, ALU.add))
        v.scalar_tensor_tensor(a(6), a(4), 0.25, a(5), ALU.mult, ALU.add).then_inc(self.var_ready, 1)
        v.wait_ge(self.sqrt_done, 1)
        step(v.reciprocal(a(0), a(7)))
        for t in range(NT):
            v.tensor_scalar(S.hn[:, t, :], S.x[:, t, :], S.sm[:, 3, t:t + 1], S.sm[:, 0, t:t + 1],
                            ALU.subtract, ALU.mult).then_inc(self.normed, 1)
        for b in (1, 3):
            v.wait_ge(self.turned, 4 * (b + 1))
            v.tensor_copy(S.hT[:, b * BANK:(b + 1) * BANK], S.ps[:, b * BANK:(b + 1) * BANK]).then_inc(self.stored, 1)

    def scalar(self, act, NT):
        S = self.S
        act.wait_ge(self.var_ready, 1)
        act.activation(S.sm[:, 7, 0:NT], S.sm[:, 6, 0:NT], ACT.Sqrt).then_inc(self.sqrt_done, 1)
        for b in (0, 2):
            act.wait_ge(self.turned, 4 * (b + 1))
            act.copy(S.hT[:, b * BANK:(b + 1) * BANK], S.ps[:, b * BANK:(b + 1) * BANK]).then_inc(self.stored, 1)

    def tensor(self, pe, NT):
        S = self.S
        for t in range(NT):
            pe.wait_ge(self.normed, t + 1)
            pe.transpose(S.ps[:, bass.ds(t * P, P)], S.hn[:, t, :], S.ident[:]).then_inc(self.turned, 1)
        pe.wait_ge(self.stored, NT * P // BANK)


def mamba(nc, ctx, S, A):
    with ExitStack() as own:
        sb = lambda name, shape: own.enter_context(nc.sbuf_tensor(name, shape, F32))
        sem = lambda name: ctx.enter_context(nc.semaphore("m_" + name))
        NT, T, H, G = S.NT, S.T, 2, 4
        w_in = sb("w_in", [P, A["w_in"].shape[1]])
        w_mo = sb("w_mo", [P, H, D])
        convw = sb("convw", [P, G, 4])
        vecs = sb("vecs", [P, G + H])
        rows = sb("rows", [P, 3, H])
        xp = sb("xp", [P, G, 3 + T])
        xc = sb("xc", [P, G, T])
        z = sb("z", [P, NT, H * P])
        y = sb("y", [P, NT, H * P])
        dtr = sb("dtr", [P, 6, NT * H])
        negA = sb("negA", [P, H])
        diagD = sb("diagD", [P, H, P])
        state = sb("state", [P, 2, H, P])
        xt = sb("xt", [P, 2, 3 * P])
        uda = sb("uda", [P, 2, H, P])
        arg = sb("arg", [P, 2, H, P])
        el = sb("el", [P, 2, H, P])
        ec = sb("ec", [P, 2, H, P])
        cd = sb("cd", [P, 2, H, P])
        mt = sb("mt", [P, 2, H, P])
        bw = sb("bw", [P, 2, H, P])
        ygT = sb("ygT", [P, 2, H, P])
        norm = Norm(nc, ctx, "ln0", S)
        loaded = S.m_loaded
        names = ("xin_ready xin_stored z_ready z_stored dt_ready dt_stored dt_chain pad_zero conv_step act_chain "
                 "silu_done "
                 "cs_ready cs_stored uda_done csb_ready ec_done arg_done exp_done turned xt_stored g_ready "
                 "mix_done y_ready y_done ds_ready state_done yn_chain ssq_done rms_sqrt yn_done ygt_ready ygt_stored "
                 "o_ready res_done sumsq const_done").split()
        s = {n: sem(n) for n in names}
        ps = S.ps
        block = own.enter_context(nc.Block())

        @block.sync
        def _(sp):
            sp.dma_start(S.x[:], A["u"].rearrange("(t p) d -> p t d", p=P)).then_inc(S.x_loaded, 16)
            sp.dma_start(w_in[:], A["w_in"]).then_inc(loaded, 16)
            sp.dma_start(convw[:], A["conv_w"].rearrange("(g p) k -> p g k", p=P)).then_inc(loaded, 16)
            sp.dma_start(vecs[:, 0:G], A["conv_b"]).then_inc(loaded, 16)
            sp.dma_start(vecs[:, G:G + H], A["norm_w"]).then_inc(loaded, 16)
            sp.dma_start(w_mo[:], A["w_mo"].rearrange("(h p) o -> p h o", p=P)).then_inc(loaded, 16)
            for k, vec in enumerate((A["dt_bias"], A["a_log"], A["dskip"])):
                sp.dma_start(rows[:, k, :], vec.partition_broadcast(P)).then_inc(loaded, 16)

        @block.tensor
        def _(pe):
            norm.tensor(pe, NT)
            pe.wait_ge(loaded, 16 * 8)
            for n in range(G * 4):
                g, c = n // 4, n % 4
                if n >= 4:
                    pe.wait_ge(s["xin_stored"], n - 3)
                pe.matmul(ps[:, (4 + n % 4) * BANK:(5 + n % 4) * BANK], w_in[:, H * P + g * P:H * P + (g + 1) * P],
                          S.hT[:, c * BANK:(c + 1) * BANK], start=True, stop=True).then_inc(s["xin_ready"], 1)
            for t in range(NT):
                pe.matmul(ps[:, bass.ds(t * H, H)], S.hT[:, bass.ds(t * P, P)], w_in[:, 6 * P:6 * P + H],
                          start=True, stop=True).then_inc(s["dt_ready"], 1)
            for i in range(NT // 2):
                for u in range(2):
                    if i >= 1:
                        pe.wait_ge(s["z_stored"], i * 2 - 1 + u)
                    pe.matmul(ps[:, (2 + u) * BANK:(2 + u) * BANK + H * P], S.hT[:, bass.ds(i * 2 * P + u * P, P)],
                              w_in[:, 0:H * P], start=True, stop=True).then_inc(s["z_ready"], 1)
            pe.wait_ge(s["dt_stored"], 1)
            pe.matmul(ps[:, BANK:BANK + NT * H], S.upper[:], dtr[:, 1, :], start=True, stop=True)
            pe.matmul(ps[:, BANK + 64:BANK + 64 + NT * H], S.ones[:], dtr[:, 1, :], start=True,
                      stop=True).then_inc(s["cs_ready"], 1)
            pe.wait_ge(s["silu_done"], G + 1)
            pe.wait_ge(s["const_done"], 2)
            pe.wait_ge(s["cs_stored"], 1)

            def prepare(c, u):
                tk = bass.ds(c * P, P)
                for k in range(3):
                    ins = pe.transpose(ps[:, u * BANK + k * P:u * BANK + (k + 1) * P], xc[:, k, tk], S.ident[:])
                ins.then_inc(s["turned"], 1)
                pe.matmul(ps[:, (2 + u) * BANK:(2 + u) * BANK + P], xc[:, 2, tk], xc[:, 3, tk], start=True,
                          stop=True).then_inc(s["g_ready"], 1)
                pe.wait_ge(s["uda_done"], c + 1)
                pe.matmul(ps[:, (4 + u) * BANK:(4 + u) * BANK + H * P], S.ones[:],
                          uda[:, u, :, :].rearrange("p h l -> p (h l)"), start=True,
                          stop=True).then_inc(s["csb_ready"], 1)

            def mix(c, u):
                pe.wait_ge(s["xt_stored"], c + 1)
                pe.wait_ge(s["mix_done"], c + 1)
                if c:
                    pe.wait_ge(s["y_done"], c)
                    pe.wait_ge(s["state_done"], c)
                for h in range(H):
                    Y = ps[:, 6 * BANK + h * P:6 * BANK + (h + 1) * P]
                    xh = xt[:, u, h * P:(h + 1) * P]
                    pe.matmul(Y, mt[:, u, h, :], xh, start=True, stop=False)
                    pe.matmul(Y, diagD[:, h, :], xh, start=False, stop=False)
                    ins = pe.matmul(Y, cd[:, u, h, :], state[:, u, h, :], start=False, stop=True)
                ins.then_inc(s["y_ready"], 1)
                for h in range(H):
                    ins = pe.matmul(ps[:, 7 * BANK + h * P:7 * BANK + (h + 1) * P], bw[:, u, h, :],
                                    xt[:, u, h * P:(h + 1) * P], start=True, stop=True)
                ins.then_inc(s["ds_ready"], 1)

            prepare(0, 0)
            for c in range(NT):
                if c + 1 < NT:
                    prepare(c + 1, (c + 1) % 2)
                mix(c, c % 2)

            def turn(t, u):
                pe.wait_ge(s["yn_done"], t + 1)
                if t >= 2:
                    pe.wait_ge(s["ygt_stored"], t - 1)
                for h in range(H):
                    ins = pe.transpose(ps[:, u * BANK + h * P:u * BANK + (h + 1) * P], y[:, t, h * P:(h + 1) * P],
                                       S.ident[:])
                ins.then_inc(s["ygt_ready"], 1)

            def project(t, u):
                pe.wait_ge(s["ygt_stored"], t + 1)
                if t >= 2:
                    pe.wait_ge(s["res_done"], t - 1)
                for h in range(H):
                    ins = pe.matmul(ps[:, (2 + u) * BANK:(2 + u) * BANK + D], ygT[:, u, h, :], w_mo[:, h, :],
                                    start=(h == 0), stop=(h == H - 1))
                ins.then_inc(s["o_ready"], 1)

            turn(0, 0)
            for t in range(NT):
                if t + 1 < NT:
                    turn(t + 1, (t + 1) % 2)
                project(t, t % 2)

        @block.scalar
        def _(act):
            norm.scalar(act, NT)
            for n in range(G * 4):
                g, c = n // 4, n % 4
                act.wait_ge(s["xin_ready"], n + 1)
                act.copy(xp[:, g, 3 + c * BANK:3 + (c + 1) * BANK],
                         ps[:, (4 + n % 4) * BANK:(5 + n % 4) * BANK]).then_inc(s["xin_stored"], 1)
            link = Chain(act, s["act_chain"])
            act.wait_ge(s["dt_chain"], 3)
            link(act.activation(dtr[:, 3, :], dtr[:, 2, :], ACT.Exp))
            act.activation(negA[:], rows[:, 1, :], ACT.Exp)
            act.activation(dtr[:, 4, :], dtr[:, 3, :], ACT.Ln, bias=1.0).then_inc(s["act_chain"], 1)
            with act.Fori(0, NT // 2) as i:
                for u in range(2):
                    act.wait_ge(s["z_ready"], i * 2 + u + 1)
                    act.activation(z[:, i * 2 + u, :], ps[:, (2 + u) * BANK:(2 + u) * BANK + H * P],
                                   ACT.Silu).then_inc(s["z_stored"], 1)
            for g in range(G):
                act.wait_ge(s["conv_step"], 4 * (g + 1))
                act.activation(xc[:, g, :], xp[:, g, 3:3 + T], ACT.Silu).then_inc(s["silu_done"], 1)
            act.wait_ge(s["cs_stored"], 1)
            act.activation(dtr[:, 4, :], dtr[:, 3, :], ACT.Exp)
            act.activation(dtr[:, 5, :], dtr[:, 5, :], ACT.Exp).then_inc(s["silu_done"], 1)

            def chunk(c, u):
                act.wait_ge(s["turned"], c + 1)
                act.copy(xt[:, u, :], ps[:, u * BANK:u * BANK + 3 * P]).then_inc(s["xt_stored"], 1)
                act.wait_ge(s["csb_ready"], c + 1)
                act.activation(ec[:, u, :, :].rearrange("p h l -> p (h l)"),
                               ps[:, (4 + u) * BANK:(4 + u) * BANK + H * P], ACT.Exp).then_inc(s["ec_done"], 1)
                act.wait_ge(s["arg_done"], c + 1)
                act.activation(el[:, u, :, :].rearrange("p h l -> p (h l)"),
                               arg[:, u, :, :].rearrange("p h l -> p (h l)"), ACT.Exp).then_inc(s["exp_done"], 1)

            with act.Fori(0, NT // 2) as i:
                for u in range(2):
                    chunk(i * 2 + u, u)
            act.wait_ge(s["ssq_done"], 1)
            act.activation(S.sm[:, 1, 0:NT], S.sm[:, 0, 0:NT], ACT.Sqrt).then_inc(s["rms_sqrt"], 1)
            for t in range(NT):
                u = t % 2
                act.wait_ge(s["ygt_ready"], t + 1)
                if t >= 2:
                    act.wait_ge(s["o_ready"], t - 1)
                for h in range(H):
                    ins = act.activation(ygT[:, u, h, :], ps[:, u * BANK + h * P:u * BANK + (h + 1) * P],
                                         ACT.Copy, scale=vecs[:, G + h:G + h + 1])
                ins.then_inc(s["ygt_stored"], 1)

        @block.gpsimd
        def _(pool):
            nc.gpsimd.memset(xp[:, :, 0:3], 0.0).then_inc(s["pad_zero"], 1)
            nc.gpsimd.memset(state[:, 0, :, :], 0.0).then_inc(s["const_done"], 1)
            pool.wait_ge(loaded, 16 * 8)
            for h in range(H):
                ins = nc.gpsimd.tensor_scalar(diagD[:, h, :], S.ident[:], rows[:, 2, h:h + 1], None, ALU.mult)
            ins.then_inc(s["const_done"], 1)

        @block.vector
        def _(v):
            v.wait_ge(S.x_loaded, 16)
            norm.vector(v, NT)
            v.wait_ge(loaded, 16 * 8)
            v.wait_ge(s["pad_zero"], 1)
            step = Chain(v, s["dt_chain"])
            d = lambda k: dtr[:, k, :]
            dth = lambda k, h: dtr[:, k, :].rearrange("p (t h) -> p t h", h=H)[:, :, h]
            v.wait_ge(s["dt_ready"], NT)
            psd = ps[:, 0:NT * H].rearrange("p (t h) -> p t h", h=H)
            for h in range(H):
                ins = v.tensor_scalar(dth(0, h), psd[:, :, h], rows[:, 0, h:h + 1], None, ALU.add)
            step(ins)
            step(v.tensor_scalar(d(5), d(0), -1.0, None, ALU.mult))
            step(v.tensor_tensor(d(2), d(0), d(5), ALU.min))
            v.wait_ge(s["act_chain"], 2)
            step(v.tensor_scalar(d(1), d(0), 0.0, None, ALU.max))
            step(v.tensor_tensor(d(0), d(1), d(4), ALU.add))
            for h in range(H):
                ins = v.tensor_scalar(dth(1, h), dth(0, h), negA[:, h:h + 1], -1.0, ALU.mult, ALU.mult)
            ins.then_inc(s["dt_stored"], 1)
            for g in range(G):
                v.wait_ge(s["xin_stored"], 4 * (g + 1))
                link = g * 4
                v.tensor_scalar(xc[:, g, :], xp[:, g, 0:T], convw[:, g, 0:1], vecs[:, g:g + 1], ALU.mult,
                                ALU.add).then_inc(s["conv_step"], 1)
                v.wait_ge(s["conv_step"], link + 1)
                for k in (1, 2):
                    v.scalar_tensor_tensor(xc[:, g, :], xp[:, g, k:k + T], convw[:, g, k:k + 1], xc[:, g, :],
                                           ALU.mult, ALU.add).then_inc(s["conv_step"], 1)
                    v.wait_ge(s["conv_step"], link + 1 + k)
                v.scalar_tensor_tensor(xp[:, g, 3:3 + T], xp[:, g, 3:3 + T], convw[:, g, 3:4], xc[:, g, :],
                                       ALU.mult, ALU.add).then_inc(s["conv_step"], 1)
            v.wait_ge(s["cs_ready"], 1)
            v.tensor_copy(d(2), ps[:, BANK:BANK + NT * H])
            step(v.tensor_copy(d(5), ps[:, BANK + 64:BANK + 64 + NT * H]))
            v.tensor_tensor(d(3), d(5), d(2), ALU.subtract).then_inc(s["cs_stored"], 1)
            v.wait_ge(s["silu_done"], G + 1)
            step(v.tensor_tensor(d(4), d(4), d(0), ALU.mult))

            col = lambda k, c, h: dtr[:, k, bass.ds(c * H + h, 1)]

            def spread(c, u):
                for h in range(H):
                    ins = v.tensor_scalar(uda[:, u, h, :], S.upper[:], col(1, c, h), None, ALU.mult)
                ins.then_inc(s["uda_done"], 1)

            def decays(c, u):
                v.wait_ge(s["ec_done"], c + 1)
                for h in range(H):
                    csb = ps[:, (4 + u) * BANK + h * P:(4 + u) * BANK + (h + 1) * P]
                    ins = v.scalar_tensor_tensor(arg[:, u, h, :], csb, col(2, c, h), S.cap[:], ALU.subtract, ALU.min)
                ins.then_inc(s["arg_done"], 1)
                v.wait_ge(s["xt_stored"], c + 1)
                for h in range(H):
                    v.tensor_scalar(bw[:, u, h, :], xt[:, u, 2 * P:3 * P], col(4, c, h), None, ALU.mult)

            def weigh(c, u):
                v.wait_ge(s["exp_done"], c + 1)
                v.wait_ge(s["g_ready"], c + 1)
                for h in range(H):
                    v.tensor_tensor(cd[:, u, h, :], xc[:, 3, bass.ds(c * P, P)], ec[:, u, h, :], ALU.mult)
                    ins = v.scalar_tensor_tensor(mt[:, u, h, :], el[:, u, h, :], col(0, c, h),
                                                 ps[:, (2 + u) * BANK:(2 + u) * BANK + P], ALU.mult, ALU.mult)
                ins.then_inc(s["mix_done"], 1)

            def collect(c, u):
                v.wait_ge(s["y_ready"], c + 1)
                v.tensor_tensor(y[:, c, :], ps[:, 6 * BANK:6 * BANK + H * P], z[:, c, :],
                                ALU.mult).then_inc(s["y_done"], 1)
                v.wait_ge(s["ds_ready"], c + 1)
                for h in range(H):
                    ins = v.scalar_tensor_tensor(state[:, 1 - u, h, :], state[:, u, h, :], col(5, c, h),
                                                 ps[:, 7 * BANK + h * P:7 * BANK + (h + 1) * P], ALU.mult, ALU.add)
                ins.then_inc(s["state_done"], 1)
                v.wait_ge(s["state_done"], c + 1)

            def chunk(c, u):
                spread(c + 1, 1 - u)
                weigh(c, u)
                decays(c + 1, 1 - u)
                collect(c, u)

            v.wait_ge(s["const_done"], 2)
            spread(0, 0)
            decays(0, 0)
            with v.Fori(0, NT // 2 - 1) as i:
                for u in range(2):
                    chunk(i * 2 + u, u)
            chunk(NT - 2, 0)
            weigh(NT - 1, 1)
            collect(NT - 1, 1)
            v.wait_ge(s["y_done"], NT)
            v.tensor_tensor(z[:], y[:], y[:], ALU.mult).then_inc(s["sumsq"], 1)
            v.wait_ge(s["sumsq"], 1)
            link = Chain(v, s["yn_chain"])
            link(v.tensor_reduce(S.sm[:, 2, 0:NT], z[:], AX.X, ALU.add))
            v.tensor_scalar(S.sm[:, 0, 0:NT], S.sm[:, 2, 0:NT], 1.0 / (H * P), EPS, ALU.mult,
                            ALU.add).then_inc(s["ssq_done"], 1)
            v.wait_ge(s["rms_sqrt"], 1)
            link(v.reciprocal(S.sm[:, 3, 0:NT], S.sm[:, 1, 0:NT]))
            for t in range(NT):
                v.tensor_scalar(y[:, t, :], y[:, t, :], S.sm[:, 3, t:t + 1], None, ALU.mult).then_inc(s["yn_done"], 1)
            for t in range(NT):
                u = t % 2
                v.wait_ge(s["o_ready"], t + 1)
                v.tensor_tensor(S.x[:, t, :], S.x[:, t, :], ps[:, (2 + u) * BANK:(2 + u) * BANK + D],
                                ALU.add).then_inc(s["res_done"], 1)
            v.wait_ge(s["res_done"], NT)


def moe_semaphores(nc, ctx):
    sem = lambda n: ctx.enter_context(nc.semaphore("moe_" + n))
    names = ("loaded gate_ready gate_chain top_done top_diff exp_done comb_done combt_ready combt_stored "
             "bias_ready acc_init iota_done h_ready hid_ready y_ready y_added stored w_loaded "
             "w1_loaded_0 w1_loaded_1 w2_loaded_0 w2_loaded_1 gate").split()
    return {n: sem(n) for n in names}


def moe(nc, S, A, tag, s, norm, out=None):
    with ExitStack() as own:
        sb = lambda name, shape, dt=F32: own.enter_context(nc.sbuf_tensor(f"{tag}_{name}", shape, dt))
        NT, T, E, FB = S.NT, S.T, 8, 4
        NC = T // BANK
        w1 = sb("w1", [P, 2, FB * P])
        w2 = sb("w2", [P, 2, FB, D])
        b1 = sb("b1", [P, E * FB])
        b2 = sb("b2", [E, D])
        gw = sb("gw", [P, E])
        gb = sb("gb", [P, E])
        lg = sb("lg", [P, NT, E])
        m8 = sb("m8", [P, NT, E])
        i8 = sb("i8", [P, NT, E], mybir.dt.uint32)
        i8f = sb("i8f", [P, NT, E])
        iot = sb("iot", [P, NT, E])
        c1 = sb("c1", [P, NT, E])
        c2 = sb("c2", [P, NT, E])
        comb = sb("comb", [P, NT, E])
        combT = sb("combT", [E, T])
        hid = sb("hid", [P, 2, FB, BANK])
        ps = S.ps
        acc = S.x
        block = own.enter_context(nc.Block())

        @block.sync
        def _(sp):
            sp.dma_start(gw[:], A["gate_w"]).then_inc(s["loaded"], 16)
            sp.dma_start(gb[:], A["gate_b"].partition_broadcast(P)).then_inc(s["loaded"], 16)
            sp.dma_start(b2[:], A["b2"]).then_inc(s["loaded"], 16)
            sp.dma_start(b1[:], A["b1T"]).then_inc(s["w_loaded"], 16)

            def load_expert(e, u):
                sp.dma_start(w1[:, u, :], A["w1"][e, :, :]).then_inc(s[f"w1_loaded_{u}"], 16)
                sp.dma_start(w2[:, u, :, :], A["w2"][e, :, :].rearrange("(k f) d -> f k d", f=P)).then_inc(
                    s[f"w2_loaded_{u}"], 16)

            load_expert(0, 0)
            load_expert(1, 1)
            with sp.Fori(1, E // 2) as i:
                for u in range(2):
                    sp.wait_ge(s["y_ready"], (i * 2 + u - 1) * NC)
                    load_expert(i * 2 + u, u)
            if out is not None:
                sp.wait_ge(s["y_added"], 4 * NC * E + 1)
                sp.dma_start(out.rearrange("(t p) d -> p t d", p=P), S.x[:]).then_inc(s["stored"], 16)
                sp.wait_ge(s["stored"], 16)

        @block.gpsimd
        def _(pool):
            nc.gpsimd.iota(iot[:], pattern=[[0, NT], [1, E]], base=0, channel_multiplier=0,
                           allow_small_or_imprecise_dtypes=True).then_inc(s["iota_done"], 1)

        @block.tensor
        def _(pe):
            norm.tensor(pe, NT)
            pe.wait_ge(s["loaded"], 48)
            for t in range(NT):
                pe.matmul(ps[:, bass.ds(t * E, E)], S.hT[:, bass.ds(t * P, P)], gw[:], start=True,
                          stop=True).then_inc(s["gate_ready"], 1)

            def hidden(u, c, n):
                if n is not None:
                    pe.wait_ge(s["hid_ready"], n)
                for f in range(FB):
                    ins = pe.matmul(ps[:, f * BANK:(f + 1) * BANK], w1[:, u, f * P:(f + 1) * P],
                                    S.hT[:, c * BANK:(c + 1) * BANK], start=True, stop=True)
                ins.then_inc(s["h_ready"], 1)

            def down(u, c, n):
                pe.wait_ge(s["hid_ready"], n + 1)
                for k in range(4):
                    Y = ps[:, (6 + c % 2) * BANK + k * P:(6 + c % 2) * BANK + (k + 1) * P]
                    for f in range(FB):
                        ins = pe.matmul(Y, hid[:, c % 2, f, k * P:(k + 1) * P], w2[:, u, f, :],
                                        start=(f == 0), stop=(f == FB - 1))
                ins.then_inc(s["y_ready"], 1)

            pe.wait_ge(s["comb_done"], 1)
            for t in range(NT):
                pe.transpose(ps[0:E, bass.ds(t * P, P)], comb[:, t, :], S.ident[:]).then_inc(s["combt_ready"], 1)
            pe.wait_ge(s["combt_stored"], NC)
            for t in range(NT):
                pe.matmul(ps[:, bass.ds(t * P, P)], combT[:, bass.ds(t * P, P)], b2[:], start=True,
                          stop=True).then_inc(s["bias_ready"], 1)
            pe.wait_ge(s["acc_init"], NC)

            pe.wait_ge(s["w1_loaded_0"], 16)
            hidden(0, 0, None)

            def expert(i, u, last=False):
                e = i * 2 + u
                pe.wait_ge(s[f"w2_loaded_{u}"], i * 16 + 16)
                for c in range(NC):
                    n = e * NC + c
                    if c < NC - 1:
                        hidden(u, c + 1, n + 1)
                    elif not last:
                        pe.wait_ge(s[f"w1_loaded_{1 - u}"], (i + u) * 16 + 16)
                        hidden(1 - u, 0, n + 1)
                    pe.wait_ge(s["y_added"], (n * 4 - 3) if c >= 1 else e * 16 + 1)
                    down(u, c, n)

            with pe.Fori(0, E // 2 - 1) as i:
                expert(i, 0)
                expert(i, 1)
            expert(E // 2 - 1, 0)
            expert(E // 2 - 1, 1, last=True)

        @block.scalar
        def _(act):
            norm.scalar(act, NT)
            act.wait_ge(s["top_diff"], 1)
            act.activation(S.sm[:, 1, 0:NT], S.sm[:, 0, 0:NT], ACT.Exp).then_inc(s["exp_done"], 1)
            for c in range(NC):
                act.wait_ge(s["combt_ready"], 4 * (c + 1))
                act.copy(combT[:, c * BANK:(c + 1) * BANK], ps[0:E, c * BANK:(c + 1) * BANK]).then_inc(
                    s["combt_stored"], 1)
            act.wait_ge(s["w_loaded"], 16)

            def gelus(e, c, first=False):
                n = e * NC + c
                act.wait_ge(s["h_ready"], n + 1)
                if not (first and c < 2):
                    act.wait_ge(s["y_ready"], n - 1)
                act.sem_inc(s["gate"], 1)
                for f in range(FB):
                    ins = act.activation(hid[:, c % 2, f, :], ps[:, f * BANK:(f + 1) * BANK], ACT.Gelu,
                                         bias=b1[:, bass.ds(e * FB + f, 1)])
                ins.then_inc(s["hid_ready"], 1)

            for c in range(NC):
                gelus(0, c, first=True)
            with act.Fori(1, E) as e:
                for c in range(NC):
                    gelus(e, c)

        @block.vector
        def _(v):
            norm.vector(v, NT)
            step = Chain(v, s["gate_chain"])
            bc = lambda ap: ap.unsqueeze(2).to_broadcast([P, NT, E])
            v.wait_ge(s["loaded"], 48)
            v.wait_ge(s["gate_ready"], NT)
            step(v.tensor_tensor(lg[:], ps[:, 0:NT * E].rearrange("p (t e) -> p t e", e=E),
                                 gb[:].unsqueeze(1).to_broadcast([P, NT, E]), ALU.add))
            for t in range(NT):
                ins = v.max(m8[:, t, :], lg[:, t, :])
            ins.then_inc(s["top_done"], 1)
            v.wait_ge(s["top_done"], 1)
            v.tensor_tensor(S.sm[:, 0, 0:NT], m8[:, :, 1], m8[:, :, 0], ALU.subtract).then_inc(s["top_diff"], 1)
            for t in range(NT):
                ins = v.max_index(i8[:, t, :], m8[:, t, :], lg[:, t, :])
            step(ins)
            step(v.tensor_copy(i8f[:], i8[:]))
            v.wait_ge(s["iota_done"], 1)
            v.tensor_tensor(c1[:], iot[:], bc(i8f[:, :, 0]), ALU.is_equal)
            v.tensor_tensor(c2[:], iot[:], bc(i8f[:, :, 1]), ALU.is_equal)
            v.wait_ge(s["exp_done"], 1)
            step(v.tensor_scalar(S.sm[:, 2, 0:NT], S.sm[:, 1, 0:NT], 1.0, None, ALU.add))
            step(v.reciprocal(S.sm[:, 3, 0:NT], S.sm[:, 2, 0:NT]))
            step(v.tensor_tensor(S.sm[:, 4, 0:NT], S.sm[:, 3, 0:NT], S.sm[:, 1, 0:NT], ALU.mult))
            v.tensor_tensor(c1[:], c1[:], bc(S.sm[:, 3, 0:NT]), ALU.mult)
            step(v.tensor_tensor(c2[:], c2[:], bc(S.sm[:, 4, 0:NT]), ALU.mult))
            v.tensor_tensor(comb[:], c1[:], c2[:], ALU.add).then_inc(s["comb_done"], 1)
            for c in range(NC):
                v.wait_ge(s["bias_ready"], 4 * (c + 1))
                v.tensor_tensor(acc[:, 4 * c:4 * c + 4, :], acc[:, 4 * c:4 * c + 4, :],
                                ps[:, c * BANK:(c + 1) * BANK].rearrange("p (t d) -> p t d", d=D),
                                ALU.add).then_inc(s["acc_init"], 1)
            v.wait_ge(s["acc_init"], NC)
            v.sem_inc(s["y_added"], 1)
            v.wait_ge(s["comb_done"], 1)
            v.wait_ge(s["acc_init"], NC)
            with v.Fori(0, E) as e:
                for c in range(NC):
                    n = e * NC + c
                    v.wait_ge(s["y_ready"], n + 1)
                    v.wait_ge(s["y_added"], e * 16 + 1)
                    for k in range(4):
                        t = 4 * c + k
                        Y = ps[:, (6 + c % 2) * BANK + k * P:(6 + c % 2) * BANK + (k + 1) * P]
                        v.scalar_tensor_tensor(acc[:, t, :], Y, comb[:, t, bass.ds(e, 1)], acc[:, t, :],
                                               ALU.mult, ALU.add).then_inc(s["y_added"], 1)
            v.wait_ge(s["y_added"], 4 * NC * E + 1)


def attention(nc, ctx, S, A):
    with ExitStack() as own:
        NT, T = S.NT, S.T
        NCH = T // BANK
        sb = lambda name, shape, dt=F32: own.enter_context(nc.sbuf_tensor("at_" + name, shape, dt))
        sem = lambda name: ctx.enter_context(nc.semaphore("at_" + name))
        qT = sb("qT", [P, T])
        kT = sb("kT", [P, T])
        V = sb("V", [P, NT, HEADS, DH + 1])
        wo = sb("wo", [P, D])
        count = sb("count", [P, NT * HEADS])
        parts = nc.dram_tensor("qk_parts", (2, HEADS, PARTS, DH, T), BF16, kind="Internal").ap()
        project_qkv(nc, ctx, S, A, qT, kT, V, wo, parts)
        select_and_mix(nc, ctx, S, parts, V, count)
        redo(nc, ctx, S, qT, kT, V, count)
        project_out(nc, ctx, S, A, wo)


def project_qkv(nc, ctx, S, A, qT, kT, V, wo, parts):
    with ExitStack() as own:
        NT, T = S.NT, S.T
        NCH = T // BANK
        sb = lambda name, shape, dt=F32: own.enter_context(nc.sbuf_tensor("qk_" + name, shape, dt))
        wqk = sb("wqk", [P, 2, P])
        bqk = sb("bqk", [P, 2])
        wv = sb("wv", [P, D])
        bv = sb("bv", [P, D])
        bo = sb("bo", [P, D])
        part = sb("part", [P, 2, PARTS, T], BF16)
        left = sb("left", [P, 2, T])
        norm = Norm(nc, ctx, "atln", S)
        s = {n: ctx.enter_context(nc.semaphore("qk_" + n)) for n in
             ("loaded ready_a ready_v stored_a stored_v v_ready v_stored res high_done left_done_0 left_done_1 "
              "mid_done low_done_0 low_done_1 kept_in_dram").split()}
        ps = S.ps
        block = own.enter_context(nc.Block())

        @block.sync
        def _(sp):
            sp.dma_start(wqk[:], A["wqk"]).then_inc(s["loaded"], 16)
            sp.dma_start(bqk[:], A["bqk"]).then_inc(s["loaded"], 16)
            sp.dma_start(wv[:], A["wv"]).then_inc(s["loaded"], 16)
            sp.dma_start(bv[:], A["bv"].partition_broadcast(P)).then_inc(s["loaded"], 16)
            sp.dma_start(wo[:], A["w_o"]).then_inc(s["loaded"], 16)
            sp.dma_start(bo[:], A["b_o"].partition_broadcast(P)).then_inc(s["loaded"], 16)
            for k, done in enumerate(("high_done", "mid_done", "low_done")):
                for side in range(2):
                    if k < 2:
                        sp.wait_ge(s[done], side + 1)
                    else:
                        sp.wait_ge(s[f"{done}_{side}"], 1)
                    sp.dma_start(parts[side, :, k, :, :], part[:, side, k, :]).then_inc(s["kept_in_dram"], 16)
            sp.wait_ge(s["kept_in_dram"], 16 * 2 * PARTS)

        items = [(side, c) for side in range(2) for c in range(NCH)]

        @block.tensor
        def _(pe):
            norm.tensor(pe, NT)
            pe.wait_ge(s["loaded"], 96)
            for n, (side, c) in enumerate(items):
                who = "a" if c % 2 == 0 else "v"
                if n >= NCH:
                    pe.wait_ge(s["stored_" + who], n // NCH * 2 - 1 + c // 2)
                pe.matmul(ps[:, c * BANK:(c + 1) * BANK], wqk[:, side, :], S.hT[:, c * BANK:(c + 1) * BANK],
                          start=True, stop=True).then_inc(s["ready_" + who], 1)
            for t in range(NT):
                pe.matmul(ps[:, 4 * BANK + t * D:4 * BANK + (t + 1) * D], S.hT[:, t * P:(t + 1) * P], wv[:],
                          start=True, stop=True).then_inc(s["v_ready"], 1)

        @block.scalar
        def _(act):
            norm.scalar(act, NT)
            act.wait_ge(s["loaded"], 96)
            for n, (side, c) in enumerate(items):
                if c % 2 == 0:
                    act.wait_ge(s["ready_a"], n // NCH * 2 + c // 2 + 1)
                    act.activation((qT, kT)[side][:, c * BANK:(c + 1) * BANK], ps[:, c * BANK:(c + 1) * BANK],
                                   ACT.Identity,
                                   bias=bqk[:, side:side + 1]).then_inc(s["stored_a"], 1)
            for side in range(2):
                act.wait_ge(s["stored_a"], NCH // 2 * (side + 1))
                act.wait_ge(s["stored_v"], NCH // 2 * (side + 1))
                act.copy(part[:, side, 0, :], (qT, kT)[side][:]).then_inc(s["high_done"], 1)
            for side in range(2):
                act.wait_ge(s[f"left_done_{side}"], 1)
                act.copy(part[:, side, 1, :], left[:, side, :]).then_inc(s["mid_done"], 1)

        @block.gpsimd
        def _(pool):
            nc.gpsimd.memset(V[:, :, :, DH:DH + 1], 1.0)
            pool.wait_ge(s["high_done"], 2)
            nc.gpsimd.tensor_tensor(left[:, 1, :], kT[:], part[:, 1, 0, :], ALU.subtract).then_inc(s["left_done_1"], 1)
            pool.wait_ge(s["mid_done"], 2)
            nc.gpsimd.tensor_tensor(part[:, 1, 2, :], left[:, 1, :], part[:, 1, 1, :],
                                    ALU.subtract).then_inc(s["low_done_1"], 1)

        @block.vector
        def _(v):
            norm.vector(v, NT)
            v.wait_ge(s["loaded"], 96)
            v.tensor_tensor(S.x[:], S.x[:], S.hn[:], ALU.add).then_inc(s["res"], 1)
            v.wait_ge(s["res"], 1)
            v.tensor_tensor(S.x[:], S.x[:], bo[:].unsqueeze(1).to_broadcast([P, NT, D]), ALU.add).then_inc(s["res"], 1)
            for n, (side, c) in enumerate(items):
                if c % 2 == 1:
                    v.wait_ge(s["ready_v"], n // NCH * 2 + c // 2 + 1)
                    v.tensor_scalar((qT, kT)[side][:, c * BANK:(c + 1) * BANK], ps[:, c * BANK:(c + 1) * BANK],
                                    bqk[:, side:side + 1], None,
                                    ALU.add).then_inc(s["stored_v"], 1)
            v.wait_ge(s["high_done"], 1)
            v.tensor_tensor(left[:, 0, :], qT[:], part[:, 0, 0, :], ALU.subtract).then_inc(s["left_done_0"], 1)
            for c in range(NCH):
                v.wait_ge(s["v_ready"], 4 * (c + 1))
                v.tensor_tensor(V[:, 4 * c:4 * c + 4, :, 0:DH],
                                ps[:, (4 + c) * BANK:(5 + c) * BANK].rearrange("p (t h d) -> p t h d", h=HEADS, d=DH),
                                bv[:].rearrange("p (h d) -> p h d", d=DH).unsqueeze(1).to_broadcast(
                                    [P, 4, HEADS, DH]), ALU.add).then_inc(s["v_stored"], 1)
            v.wait_ge(s["mid_done"], 1)
            v.tensor_tensor(part[:, 0, 2, :], left[:, 0, :], part[:, 0, 1, :], ALU.subtract).then_inc(
                s["low_done_0"], 1)


def ge(eng, sem, value):
    if not (isinstance(value, int) and value <= 0):
        eng.wait_ge(sem, value)


def select_and_mix(nc, ctx, S, parts, V, count):
    with ExitStack() as own:
        NT, T = S.NT, S.T
        NCH, NB = T // BANK, T // P
        SCALE = 1.0 / float(np.sqrt(DH))
        HALF = NT // 4
        BODY = NT // 2
        ROWS = PARTS * PARTS * DH
        N = NT * HEADS
        SEG = T // SEGS
        sb = lambda name, shape, dt=F32: own.enter_context(nc.sbuf_tensor("sm_" + name, shape, dt))
        qh = sb("qh", [ROWS, 2, T], BF16)
        kh = sb("kh", [ROWS, 2, T], BF16)
        sc = sb("sc", [P, 4, T])
        ex = sb("ex", [P, 4, T])
        side = sb("side", [P, 2, T], BF16)
        drop = sb("drop", [P, 2, T], BF16)
        low = sb("low", [P, 2, T])
        pr = sb("pr", [P, 2, T])
        pT = sb("pT", [P, 2, T])
        cand = sb("cand", [P, 2, SEGS * 8])
        tops = sb("tops", [P, 2, ROUNDS, 8])
        nmax = sb("nmax", [P, 4, 1])
        rank = sb("rank", [P, 2, 1])
        nextT = sb("nextT", [P, 2, 8])
        pick = sb("pick", [P, 2, 8])
        kth = sb("kth", [P, 2, 1])
        vh = sb("vh", [P, 2, NB, DH + 1])
        outT = sb("outT", [DH + 1, P])
        rden = sb("rden", [P, 2, 1])
        above = sb("above", [P, 4, 1])
        iota8 = sb("iota8", [P, 8])
        attn = S.hT
        names = ("head_loaded head_ready s_ready sc_stored seg_done max_ready exp_done pivot_ready side_done low_done "
                 "chain rank_done next_done kth_done dropped kept turned pt_stored pt_stored_v v_ready mixed "
                 "out_stored out_turned rden_done attn_done gate iota").split()
        s = {n: ctx.enter_context(nc.semaphore("sm_" + n)) for n in names}
        ps = S.ps
        block = own.enter_context(nc.Block())

        def tile(it, j):
            return it * BODY + j, (it % 2) * BODY + j, it // 2

        def at(start, size):
            return slice(start, start + size) if isinstance(start, int) else bass.ds(start, size)

        def near(it, j, k):
            body, place = (j + k) // BODY, (j + k) % BODY
            if isinstance(it, int) and not 0 <= it + body < N // BODY:
                return None
            return (it + body if body else it), place

        def run(eng, step, drain):
            for j in range(BODY):
                step(0, j)
            with eng.Fori(1, N // BODY - 1) as it:
                for j in range(BODY):
                    step(it, j)
            for j in range(BODY + drain):
                step(N // BODY - 1 + j // BODY, j % BODY)

        def do(stage, it, j, k, *more):
            at_tile = near(it, j, k)
            if at_tile:
                stage(*at_tile, *more)

        @block.sync
        def _(sp):
            def load(h, slot):
                for a in range(PARTS):
                    r = slice(a * PARTS * DH, (a + 1) * PARTS * DH)
                    qa = parts[0, at(h, 1), a, :, :].to_broadcast([PARTS, DH, T])
                    kb = parts[1, at(h, 1), :, :, :].rearrange("o b d t -> (o b d) t")
                    sp.dma_start(qh[r, at(slot, 1), :], qa).then_inc(s["head_loaded"], 16)
                    sp.dma_start(kh[r, at(slot, 1), :], kb).then_inc(s["head_loaded"], 16)

            load(0, 0)
            sp.wait_ge(s["head_loaded"], 16 * 2 * PARTS)
            sp.sem_inc(s["head_ready"], 1)
            load(1, 1)
            sp.wait_ge(s["head_loaded"], 2 * 16 * 2 * PARTS)
            sp.sem_inc(s["head_ready"], 1)
            with sp.Fori(1, HEADS // 2) as i:
                for u in range(2):
                    h = i * 2 + u
                    sp.wait_ge(s["s_ready"], (i * 2 - 1 + u) * NT)
                    load(h, u)
                    sp.wait_ge(s["head_loaded"], (h + 1) * 16 * 2 * PARTS)
                    sp.sem_inc(s["head_ready"], 1)

        @block.gpsimd
        def _(pool):
            nc.gpsimd.iota(iota8[:], pattern=[[1, 8]], base=0, channel_multiplier=0,
                           allow_small_or_imprecise_dtypes=True).then_inc(s["iota"], 1)

            def below(it, j):
                n = tile(it, j)[0]
                pool.wait_ge(s["side_done"], n + 1)
                pool.wait_ge(s["exp_done"], n + 1)
                ge(pool, s["next_done"], n - 1)
                nc.gpsimd.tensor_tensor(low[:, j % 2, :], ex[:, j % 4, :], side[:, j % 2, :],
                                        ALU.mult).then_inc(s["low_done"], 1)

            def keep(it, j):
                n = tile(it, j)[0]
                pool.wait_ge(s["dropped"], n + 1)
                ge(pool, s["turned"], (n - 1) * NCH)
                nc.gpsimd.tensor_tensor(pr[:, j % 2, :], ex[:, j % 4, :], drop[:, j % 2, :],
                                        ALU.mult).then_inc(s["kept"], 1)

            def copy_v(it, half):
                n, _, h = tile(it, half * HALF)
                ge(pool, s["mixed"], n - HALF if isinstance(n, int) and n < BODY else n - BODY + HALF)
                pool.sem_inc(s["gate"], 1)
                vf = V[:].rearrange("p t h d -> p t (h d)")
                nc.gpsimd.tensor_copy(vh[:, half, :, :], vf[:, :, at(h * (DH + 1), DH + 1)]).then_inc(s["v_ready"], 1)

            def step(it, j):
                if j % HALF == 1 and near(it, j, 0):
                    copy_v(it, j // HALF)
                do(below, it, j, 0)
                do(keep, it, j, -1)

            run(pool, step, 1)

        @block.tensor
        def _(pe):
            qf = qh[:].rearrange("r u t -> r (u t)")
            kf = kh[:].rearrange("r u t -> r (u t)")
            vf = V[:].rearrange("p t h d -> p t (h d)")

            def scores(it, j):
                n, qt, h = tile(it, j)
                if j == 0:
                    pe.wait_ge(s["head_ready"], h + 1)
                ge(pe, s["sc_stored"], n)
                for c in range(NCH):
                    ins = pe.matmul(ps[:, c * BANK:(c + 1) * BANK], qf[:, at((h % 2) * T + qt * P, P)],
                                    kf[:, at((h % 2) * T + c * BANK, BANK)], start=True, stop=True)
                ins.then_inc(s["s_ready"], 1)

            def turn(it, j, groups):
                n = tile(it, j)[0]
                if 0 in groups:
                    pe.wait_ge(s["kept"], n + 1)
                for b in groups:
                    if b == 0:
                        ge(pe, s["pt_stored"], n * (NCH - 1))
                    elif b == 1:
                        ge(pe, s["pt_stored_v"], n)
                    else:
                        pe.wait_ge(s["pt_stored"], n * (NCH - 1) + b - 1)
                    for k in range(4):
                        kb = b * 4 + k
                        ins = pe.transpose(ps[:, (4 + b % 2) * BANK + k * P:(4 + b % 2) * BANK + (k + 1) * P],
                                           pr[:, j % 2, kb * P:(kb + 1) * P], S.ident[:])
                    ins.then_inc(s["turned"], 1)

            def mix(it, j):
                n = tile(it, j)[0]
                if j % HALF == 0:
                    pe.wait_ge(s["v_ready"], it * (BODY // HALF) + j // HALF + 1)
                pe.wait_ge(s["pt_stored"], n * (NCH - 1) + NCH - 1)
                pe.wait_ge(s["pt_stored_v"], n + 1)
                ge(pe, s["out_stored"], n)
                for kb in range(NB):
                    ins = pe.matmul(ps[0:DH + 1, 6 * BANK:6 * BANK + P], vh[:, j // HALF, kb, :],
                                    pT[:, j % 2, kb * P:(kb + 1) * P], start=(kb == 0), stop=(kb == NB - 1))
                ins.then_inc(s["mixed"], 1)

            def turn_back(it, j):
                n = tile(it, j)[0]
                pe.wait_ge(s["out_stored"], n + 1)
                ge(pe, s["attn_done"], n)
                pe.sem_inc(s["gate"], 1)
                pe.transpose(ps[:, 7 * BANK:7 * BANK + DH + 1], outT[:], S.ident[0:DH + 1, 0:DH + 1]).then_inc(
                    s["out_turned"], 1)

            scores(0, 0)
            scores(0, 1)

            def step(it, j):
                do(turn, it, j, -3, (0,))
                do(scores, it, j, 2)
                do(turn, it, j, -3, (1,))
                do(turn_back, it, j, -5)
                do(turn, it, j, -3, (2,))
                do(mix, it, j, -4)
                do(turn, it, j, -3, (3,))

            run(pe, step, 5)

        @block.scalar
        def _(act):
            def copy_scores(it, j):
                n = tile(it, j)[0]
                act.wait_ge(s["s_ready"], n + 1)
                ge(act, s["side_done"], n - 3)
                act.copy(sc[:, j % 4, :], ps[:, 0:T]).then_inc(s["sc_stored"], 1)

            def exps(it, j):
                n = tile(it, j)[0]
                act.wait_ge(s["max_ready"], n + 1)
                ge(act, s["kept"], n - 3)
                act.activation(ex[:, j % 4, :], sc[:, j % 4, :], ACT.Exp, scale=SCALE,
                               bias=nmax[:, j % 4, :]).then_inc(s["exp_done"], 1)

            def signs(it, j):
                n = tile(it, j)[0]
                act.wait_ge(s["pivot_ready"], n + 1)
                ge(act, s["low_done"], n - 1)
                act.activation(side[:, j % 2, :], sc[:, j % 4, :], ACT.Sign, scale=-1.0,
                               bias=tops[:, j % 2, ROUNDS - 1, 7:8],
                               accum_out=above[:, j % 4, :]).then_inc(s["side_done"], 1)

            def signs_kept(it, j):
                n = tile(it, j)[0]
                act.wait_ge(s["kth_done"], n + 1)
                ge(act, s["kept"], n - 1)
                ge(act, s["dropped"], n)
                act.sem_inc(s["gate"], 1)
                act.activation(drop[:, j % 2, :], ex[:, j % 4, :], ACT.Sign, scale=-(1.0 + 2.0 ** -23),
                               bias=kth[:, j % 2, :], accum_out=count[:, at(n, 1)]).then_inc(s["dropped"], 1)

            def move_turned(it, j, groups):
                n = tile(it, j)[0]
                ge(act, s["mixed"], n - 1)
                for b in groups:
                    act.wait_ge(s["turned"], n * NCH + b + 1)
                    act.activation(pT[:, j % 2, b * BANK:(b + 1) * BANK],
                                   ps[:, (4 + b % 2) * BANK:(5 + b % 2) * BANK], ACT.Relu,
                                   scale=-1.0).then_inc(s["pt_stored"], 1)

            def store_out(it, j):
                n = tile(it, j)[0]
                act.wait_ge(s["mixed"], n + 1)
                ge(act, s["out_turned"], n)
                act.copy(outT[:], ps[0:DH + 1, 6 * BANK:6 * BANK + P]).then_inc(s["out_stored"], 1)

            copy_scores(0, 0)
            copy_scores(0, 1)

            def step(it, j):
                do(exps, it, j, 0)
                do(move_turned, it, j, -3, (1,))
                do(copy_scores, it, j, 2)
                do(signs, it, j, 0)
                do(move_turned, it, j, -3, (2,))
                do(signs_kept, it, j, -1)
                do(store_out, it, j, -4)
                do(move_turned, it, j, -2, (0,))

            run(act, step, 4)

        @block.vector
        def _(v):
            def seg_max(j, k):
                return v.max(cand[:, j % 2, k * 8:(k + 1) * 8], sc[:, j % 4, k:T:SEGS])

            def select(it, j):
                n = tile(it, j)[0]
                nxt = near(it, j, 1)
                if nxt:
                    v.wait_ge(s["sc_stored"], n + 2)
                    v.sem_inc(s["gate"], 1)
                c, todo = cand[:, j % 2, :], list(range(SEGS)) if nxt else []
                base = 2 * ROUNDS * j
                for r in range(ROUNDS):
                    top = tops[:, j % 2, r, :]
                    v.max(top, c).then_inc(s["chain"], 1)
                    if todo:
                        ins = seg_max(nxt[1], todo.pop(0))
                    v.wait_ge(s["chain"], base + 2 * r + 1)
                    if r == 0:
                        v.tensor_scalar(nmax[:, j % 4, :], tops[:, j % 2, 0, 0:1], -SCALE, None,
                                        ALU.mult).then_inc(s["max_ready"], 1)
                    if r < ROUNDS - 1:
                        v.match_replace(c, top, c, LOWEST).then_inc(s["chain"], 1)
                    else:
                        v.sem_inc(s["chain"], 1)
                        v.sem_inc(s["pivot_ready"], 1)
                    if todo:
                        ins = seg_max(nxt[1], todo.pop(0))
                    if r < ROUNDS - 1:
                        v.wait_ge(s["chain"], base + 2 * r + 2)
                while todo:
                    ins = seg_max(nxt[1], todo.pop(0))
                if nxt:
                    ins.then_inc(s["seg_done"], 1)

            def find(it, j):
                n = tile(it, j)[0]
                v.wait_ge(s["side_done"], n + 1)
                v.tensor_scalar(rank[:, j % 2, :], above[:, j % 4, :], 0.5, TOPK - 1 - (T + 1) / 2.0, ALU.mult,
                                ALU.add).then_inc(s["rank_done"], 1)
                v.wait_ge(s["low_done"], n + 1)
                v.sem_inc(s["gate"], 1)
                v.max(nextT[:, j % 2, :], low[:, j % 2, :]).then_inc(s["next_done"], 1)

            def pick_kth(it, j):
                n = tile(it, j)[0]
                v.wait_ge(s["next_done"], n + 1)
                v.scalar_tensor_tensor(pick[:, j % 2, :], iota8[:], rank[:, j % 2, :], nextT[:, j % 2, :],
                                       ALU.is_equal, ALU.mult, accum_out=kth[:, j % 2, :]).then_inc(s["kth_done"], 1)

            def invert(it, j):
                n = tile(it, j)[0]
                v.wait_ge(s["out_turned"], n + 1)
                v.reciprocal(rden[:, j % 2, :], ps[:, 7 * BANK + DH:7 * BANK + DH + 1]).then_inc(
                    s["rden_done"], 1)

            def output(it, j):
                n, qt, h = tile(it, j)
                v.wait_ge(s["rden_done"], n + 1)
                v.sem_inc(s["gate"], 1)
                v.tensor_scalar(attn[:, at(qt * D + h * DH, DH)], ps[:, 7 * BANK:7 * BANK + DH],
                                rden[:, j % 2, :], None, ALU.mult).then_inc(s["attn_done"], 1)

            def move_last(it, j):
                n = tile(it, j)[0]
                v.wait_ge(s["turned"], n * NCH + NCH)
                ge(v, s["mixed"], n - 1)
                v.tensor_scalar(pT[:, j % 2, (NCH - 1) * BANK:], ps[:, 5 * BANK:6 * BANK], -1.0, 0.0, ALU.mult,
                                ALU.max).then_inc(s["pt_stored_v"], 1)

            v.wait_ge(s["iota"], 1)
            v.wait_ge(s["sc_stored"], 1)
            for k in range(SEGS):
                ins = seg_max(0, k)
            ins.then_inc(s["seg_done"], 1)

            def step(it, j):
                n = tile(it, j)[0]
                if near(it, j, 0):
                    if j == 0:
                        v.sem_clear(s["chain"])
                    v.wait_ge(s["seg_done"], n + 1)
                    v.sem_inc(s["gate"], 1)
                    select(it, j)
                do(invert, it, j, -5)
                do(find, it, j, -1)
                do(output, it, j, -5)
                do(pick_kth, it, j, -1)
                do(move_last, it, j, -3)

            run(v, step, 5)


def redo(nc, ctx, S, qT, kT, V, count):
    with ExitStack() as own:
        NT, T = S.NT, S.T
        NCH, NB = T // BANK, T // P
        N = NT * HEADS
        HALVES = N // P
        SCALE = 1.0 / float(np.sqrt(DH))
        I32 = mybir.dt.int32
        sb = lambda name, shape, dt=F32: own.enter_context(nc.sbuf_tensor("re_" + name, shape, dt))
        bad = sb("bad", [P, N])
        flag = sb("flag", [P, HALVES])
        place = sb("place", [P, HALVES])
        tile_no = sb("tile_no", [P, HALVES])
        one_to_n = sb("one_to_n", [P, N])
        onehot = sb("onehot", [P, HALVES, N])
        list_i = sb("list_i", [1, 1 + N], I32)
        total_i = sb("total_i", [1, 1], I32)
        qs = sb("qs", [P, P])
        sc = sb("sc", [P, T])
        rest = sb("rest", [P, T])
        ex = sb("ex", [P, T])
        pr = sb("pr", [P, T])
        pT = sb("pT", [P, T])
        tops = sb("tops", [P, TOPK // 8, 8])
        nmax = sb("nmax", [P, 1])
        den = sb("den", [P, 1])
        rden = sb("rden", [P, 1])
        names = ("iotas bad_done flag_sum flag_done placed place_done onehot_done listed ints_done redone qs_ready "
                 "s_ready sc_stored rest_done chain "
                 "max_ready exp_done kept turned pt_stored mixed rden_done gate").split()
        s = {n: ctx.enter_context(nc.semaphore("re_" + n)) for n in names}
        ps = S.ps
        block = own.enter_context(nc.Block())

        def listed(eng, count):
            n = eng.value_load(list_i[0:1, bass.ds(count, 1)], min_val=0, max_val=N - 1)
            return n % NT, n // NT

        def each_flagged(eng, body, finish=None):
            eng.wait_ge(s["ints_done"], 2)
            total = eng.value_load(total_i[0:1, 0:1], min_val=0, max_val=N)
            with eng.Fori(0, N // 32) as a:
                with eng.If(total > a * 32):
                    with eng.Fori(0, 8) as b:
                        with eng.If(total > a * 32 + b * 4):
                            with eng.Fori(0, 4) as c:
                                k = a * 32 + b * 4 + c
                                with eng.If(total > k):
                                    body(k)
            if finish:
                with eng.If(total > 0):
                    finish(total)

        @block.gpsimd
        def _(pool):
            nc.gpsimd.iota(one_to_n[:], pattern=[[1, N]], base=1, channel_multiplier=0,
                           allow_small_or_imprecise_dtypes=True).then_inc(s["iotas"], 1)
            nc.gpsimd.iota(tile_no[:], pattern=[[P, HALVES]], base=0, channel_multiplier=1,
                           allow_small_or_imprecise_dtypes=True).then_inc(s["iotas"], 1)

            def body(k):
                qt, h = listed(pool, k + 1)
                pool.wait_ge(s["s_ready"], k + 1)
                pool.sem_inc(s["gate"], 1)
                nc.gpsimd.tensor_tensor(qs[:], qT[:, bass.ds(qt * P, P)],
                                        S.headmask[:, bass.ds(h, 1)].to_broadcast([P, P]),
                                        ALU.mult).then_inc(s["qs_ready"], 1)

            each_flagged(pool, body)

        @block.tensor
        def _(pe):
            vf = V[:].rearrange("p t h d -> p t (h d)")
            pe.wait_ge(s["bad_done"], 1)
            for i in range(HALVES):
                ins = pe.matmul(ps[:, i:i + 1], bad[:, i * P:(i + 1) * P], S.ones[:, 0:1], start=True, stop=True)
            ins.then_inc(s["flag_sum"], 1)
            pe.wait_ge(s["flag_done"], 1)
            for i in range(HALVES):
                for k in range(i + 1):
                    pe.matmul(ps[:, BANK + i:BANK + i + 1], (S.upper if k == i else S.ones)[:], flag[:, k:k + 1],
                              start=(k == 0), stop=(k == i))
            for i in range(HALVES):
                ins = pe.matmul(ps[:, BANK + HALVES:BANK + HALVES + 1], S.ones[:], flag[:, i:i + 1], start=(i == 0),
                                stop=(i == HALVES - 1))
            ins.then_inc(s["placed"], 1)
            pe.wait_ge(s["onehot_done"], HALVES)
            pe.wait_ge(s["iotas"], 2)
            for i in range(HALVES):
                ins = pe.matmul(ps[0:1, 2 * BANK:2 * BANK + N], tile_no[:, i:i + 1], onehot[:, i, :], start=(i == 0),
                                stop=(i == HALVES - 1))
            ins.then_inc(s["listed"], 1)

            def body(k):
                pe.wait_ge(s["qs_ready"], k + 1)
                pe.wait_ge(s["sc_stored"], k + 1)
                for c in range(NCH):
                    ins = pe.matmul(ps[:, c * BANK:(c + 1) * BANK], qs[:], kT[:, c * BANK:(c + 1) * BANK],
                                    start=True, stop=True)
                ins.then_inc(s["s_ready"], 1)
                with pe.If(k > 0):
                    finish(k)

            def finish(count):
                qt, h = listed(pe, count)
                pe.wait_ge(s["kept"], count + 1)
                pe.wait_ge(s["redone"], count)
                for b in range(NB):
                    ins = pe.transpose(ps[:, T + b * P:T + (b + 1) * P], pr[:, b * P:(b + 1) * P], S.ident[:])
                    if b % 4 == 3:
                        ins.then_inc(s["turned"], 1)
                for b in range(NB):
                    if b % 4 == 0:
                        pe.wait_ge(s["pt_stored"], count * NCH + b // 4 + 1)
                    ins = pe.matmul(ps[:, T:T + DH], pT[:, b * P:(b + 1) * P],
                                    vf[:, b, bass.ds(h * (DH + 1), DH)], start=(b == 0), stop=(b == NB - 1))
                ins.then_inc(s["mixed"], 1)

            each_flagged(pe, body, finish)

        @block.scalar
        def _(act):
            def body(k):
                act.wait_ge(s["s_ready"], k + 2)
                act.wait_ge(s["exp_done"], k + 1)
                act.wait_ge(s["rest_done"], k + 1)
                act.copy(sc[:], ps[:, 0:T]).then_inc(s["sc_stored"], 1)
                act.wait_ge(s["max_ready"], k + 1)
                act.wait_ge(s["sc_stored"], k + 2)
                act.activation(ex[:], sc[:], ACT.Exp, scale=SCALE, bias=nmax[:]).then_inc(s["exp_done"], 1)
                with act.If(k > 0):
                    finish(k)

            def finish(count):
                act.wait_ge(s["mixed"], count)
                for b in range(NCH):
                    act.wait_ge(s["turned"], count * NCH + b + 1)
                    act.copy(pT[:, b * BANK:(b + 1) * BANK], ps[:, T + b * BANK:T + (b + 1) * BANK]).then_inc(
                        s["pt_stored"], 1)

            each_flagged(act, body, finish)

        @block.vector
        def _(v):
            v.tensor_scalar(bad[:], count[:], float(T - 2 * TOPK), None, ALU.not_equal).then_inc(s["bad_done"], 1)
            v.wait_ge(s["flag_sum"], 1)
            v.tensor_scalar(flag[:], ps[:, 0:HALVES], 1.0, None, ALU.min).then_inc(s["flag_done"], 1)
            v.wait_ge(s["placed"], 1)
            v.tensor_copy(place[:], ps[:, BANK:BANK + HALVES]).then_inc(s["place_done"], 1)
            v.tensor_copy(total_i[:], ps[0:1, BANK + HALVES:BANK + HALVES + 1]).then_inc(s["ints_done"], 1)
            v.wait_ge(s["iotas"], 1)
            v.wait_ge(s["place_done"], 1)
            for i in range(HALVES):
                v.tensor_scalar(onehot[:, i, :], one_to_n[:], place[:, i:i + 1], flag[:, i:i + 1], ALU.is_equal,
                                ALU.mult).then_inc(s["onehot_done"], 1)
            for name in ("s_ready", "sc_stored", "exp_done", "rest_done", "kept", "mixed", "redone"):
                v.sem_inc(s[name], 1)
            v.sem_inc(s["turned"], NCH)
            v.sem_inc(s["pt_stored"], NCH)
            v.wait_ge(s["listed"], 1)
            v.tensor_copy(list_i[:, 1:], ps[0:1, 2 * BANK:2 * BANK + N]).then_inc(s["ints_done"], 1)

            def body(k):
                v.sem_clear(s["chain"])
                v.wait_ge(s["sc_stored"], k + 2)
                v.wait_ge(s["kept"], k + 1)
                v.sem_inc(s["gate"], 1)
                for r in range(TOPK // 8):
                    v.max(tops[:, r, :], (sc if r == 0 else rest)[:]).then_inc(s["chain"], 1)
                    v.wait_ge(s["chain"], 2 * r + 1)
                    if r == 0:
                        v.tensor_scalar(nmax[:], tops[:, 0, 0:1], -SCALE, None, ALU.mult).then_inc(s["max_ready"], 1)
                    v.match_replace(rest[:], tops[:, r, :], (sc if r == 0 else rest)[:], LOWEST).then_inc(s["chain"], 1)
                    v.wait_ge(s["chain"], 2 * r + 2)
                    if r == 0:
                        v.sem_inc(s["rest_done"], 1)
                with v.If(k > 0):
                    finish(k)
                v.wait_ge(s["exp_done"], k + 2)
                v.wait_ge(s["turned"], (k + 1) * NCH)
                v.scalar_tensor_tensor(pr[:], rest[:], LOWEST, ex[:], ALU.is_le, ALU.mult,
                                       accum_out=den[:]).then_inc(s["kept"], 1)

            def finish(count):
                qt, h = listed(v, count)
                v.wait_ge(s["kept"], count + 1)
                v.wait_ge(s["redone"], count)
                v.reciprocal(rden[:], den[:]).then_inc(s["rden_done"], 1)
                v.wait_ge(s["rden_done"], count)
                v.wait_ge(s["mixed"], count + 1)
                v.sem_inc(s["gate"], 1)
                v.tensor_scalar(S.hT[:, bass.ds(qt * D + h * DH, DH)], ps[:, T:T + DH], rden[:], None,
                                ALU.mult).then_inc(s["redone"], 1)

            each_flagged(v, body, finish)


def project_out(nc, ctx, S, A, wo):
    with ExitStack() as own:
        NT, T = S.NT, S.T
        s = {n: ctx.enter_context(nc.semaphore("po_" + n)) for n in "turned stored ready added".split()}
        aT = own.enter_context(nc.sbuf_tensor("po_aT", [P, T], F32))
        ps = S.ps
        block = own.enter_context(nc.Block())

        @block.tensor
        def _(pe):
            for t in range(NT):
                pe.transpose(ps[:, t * P:(t + 1) * P], S.hT[:, t * P:(t + 1) * P], S.ident[:]).then_inc(s["turned"], 1)
            for t in range(NT):
                if t % 4 == 0:
                    pe.wait_ge(s["stored"], t // 4 + 1)
                pe.matmul(ps[:, 4 * BANK + t * D:4 * BANK + (t + 1) * D], aT[:, t * P:(t + 1) * P], wo[:], start=True,
                          stop=True).then_inc(s["ready"], 1)

        @block.scalar
        def _(act):
            for b in range(4):
                act.wait_ge(s["turned"], 4 * (b + 1))
                act.copy(aT[:, b * BANK:(b + 1) * BANK], ps[:, b * BANK:(b + 1) * BANK]).then_inc(s["stored"], 1)

        @block.vector
        def _(v):
            for b in range(4):
                v.wait_ge(s["ready"], 4 * (b + 1))
                v.tensor_tensor(S.x[:, 4 * b:4 * b + 4, :], S.x[:, 4 * b:4 * b + 4, :],
                                ps[:, (4 + b) * BANK:(5 + b) * BANK].rearrange("p (t d) -> p t d", d=D),
                                ALU.add).then_inc(s["added"], 1)
            v.wait_ge(s["added"], 4)


class Shared:
    pass


def program(nc, ins, out):
    S, A = Shared(), ins
    S.T = A["u"].shape[0]
    S.NT = S.T // P
    with ExitStack() as ctx:
        sb = lambda name, shape: ctx.enter_context(nc.sbuf_tensor(name, shape, F32))
        S.x = sb("x", [P, S.NT, D])
        S.hn = sb("hn", [P, S.NT, D])
        S.hT = sb("hT", [P, S.T])
        S.st = sb("st", [P, S.NT, 6])
        S.sm = sb("sm", [P, 8, S.NT])
        S.ps = ctx.enter_context(nc.psum_tensor("ps", [P, 8 * BANK], F32))
        S.x_loaded = ctx.enter_context(nc.semaphore("x_loaded"))
        S.m_loaded = ctx.enter_context(nc.semaphore("m_loaded"))
        constants(nc, ctx, S)
        mamba(nc, ctx, S, A)
        moe_sems, moe_norm = moe_semaphores(nc, ctx), Norm(nc, ctx, "moe_ln", S)
        moe(nc, S, A, "moe_a", moe_sems, moe_norm)
        attention(nc, ctx, S, A)
        clear(nc, list(moe_sems.values()) + moe_norm.all())
        moe(nc, S, A, "moe_b", moe_sems, moe_norm, out)


def clear(nc, sems):
    with nc.Block() as block:

        @block.gpsimd
        def _(pool):
            for sem in sems:
                pool.sem_clear(sem)


def kernel(**inputs):
    import numpy as _np
    import concourse.bacc as _bacc
    from concourse import mybir as _mybir
    from concourse.bass_utils import run_bass_kernel_spmd as _run

    i = {k: _np.asarray(v) for k, v in inputs.items()}
    u = i["L0_attn_a_u"]

    qkv = i["L0_attn_b_w_qkv_w"].reshape(HEADS, 3, DH, D).transpose(3, 1, 0, 2).reshape(D, 3, HEADS * DH)
    bias = i["L0_attn_b_w_qkv_b"].reshape(HEADS, 3, DH).transpose(0, 2, 1).reshape(HEADS * DH, 3)
    arrays = {
        "u": u.reshape(-1, D),
        "w_in": i["L0_attn_a_W_in"].T,
        "conv_w": i["L0_attn_a_conv_w"],
        "conv_b": i["L0_attn_a_conv_b"].reshape(-1, P).T,
        "dt_bias": i["L0_attn_a_dt_bias"],
        "a_log": i["L0_attn_a_A_log"],
        "dskip": i["L0_attn_a_D"],
        "norm_w": i["L0_attn_a_norm_w"].reshape(-1, P).T,
        "w_mo": i["L0_attn_a_W_out"].T,
        "wqk": qkv[:, :2],
        "bqk": bias[:, :2],
        "wv": qkv[:, 2],
        "bv": bias[:, 2],
        "w_o": i["L0_attn_b_w_out_w"].T,
        "b_o": i["L0_attn_b_w_out_b"],
        "gate_w": i["L0_ffn_gate_w"],
        "gate_b": i["L0_ffn_gate_b"],
        "w1": i["L0_ffn_w1"],
        "b1T": i["L0_ffn_b1"].reshape(-1, P).T,
        "w2": i["L0_ffn_w2"],
        "b2": i["L0_ffn_b2"],
    }
    arrays = {k: _np.ascontiguousarray(a) for k, a in arrays.items()}
    nc = _bacc.Bacc("TRN2", target_bir_lowering=False, num_devices=1)
    aps = {k: nc.dram_tensor(f"in_{k}", a.shape, _mybir.dt.from_np(a.dtype), kind="ExternalInput").ap()
           for k, a in arrays.items()}
    out = nc.dram_tensor("out_x", (u.shape[1], D), _mybir.dt.float32, kind="ExternalOutput").ap()
    program(nc, aps, out)
    r = _run(nc, [{f"in_{k}": a for k, a in arrays.items()}], core_ids=[0])
    return r.results[0]["out_x"].reshape(u.shape)
```
